# Optimizing a Trainium2 kernel written in Bass

```python
import numpy as np
import jax
import jax.numpy as jnp

def _softmax(x, axis=-1):
    return jax.nn.softmax(x, axis=axis)

def _gelu(x):
    return jax.nn.gelu(x, approximate=True)

def _silu(x):
    return jax.nn.silu(x)

def _sigmoid(x):
    return jax.nn.sigmoid(x)

def _layernorm(x, axis=-1, eps=1e-05):
    m = jnp.mean(x, axis=axis, keepdims=True)
    v = jnp.var(x, axis=axis, keepdims=True)
    return (x - m) / jnp.sqrt(v + eps)

def _scatter_add(tgt, idx, src, axis=0):
    return tgt.at[idx].add(src)

def _segment_sum(src, seg, n):
    return jax.ops.segment_sum(src, seg, n)
kernel_name = 'mk_perceiver_d1_seqx_r2_73cd9f'

def setup_inputs(seed: int=0):
    np.random.seed(seed)
    _w = jnp.asarray

    def _rec_inputs():
        import jax
        import jax.numpy as jnp
        _rk = jax.random.key(seed)
        x = 0.0002417 + 0.9998 * jax.random.normal(jax.random.fold_in(_rk, 1), (64, 32, 512), jnp.float32)
        _lenS = 32 - jax.random.randint(jax.random.fold_in(_rk, 7), (64,), 0, max(1, 32 // 4) + 1, jnp.int32)
        _lenS2 = 257 - jax.random.randint(jax.random.fold_in(_rk, 8), (64,), 0, max(1, 257 // 4) + 1, jnp.int32)
        _ctx_1024P = jax.random.normal(jax.random.fold_in(_rk, 11), (64, 16, 512), jnp.float32)
        _ctx_1024c = jax.random.dirichlet(jax.random.fold_in(_rk, 511), 0.3 * jnp.ones((16,), jnp.float32), (64, 257))
        _ctx_1024t = jnp.einsum('bsk,bkd->bsd', _ctx_1024c, _ctx_1024P)
        _ctx_1024t = _ctx_1024t * jax.lax.rsqrt(jnp.mean(jnp.square(_ctx_1024t)) + 1e-12) * 0.953939
        ctx_1024 = 7.22013e-05 + 1.00017 * (_ctx_1024t + 0.3 * jax.random.normal(jax.random.fold_in(_rk, 611), (64, 257, 512), jnp.float32))
        _validS = jnp.arange(32)[None, :] < _lenS[:, None]
        _validS2 = jnp.arange(257)[None, :] < _lenS2[:, None]
        _causal = jnp.tril(jnp.ones((32, 32), dtype=bool))
        mask_BxS2_if0 = jnp.where(jnp.ones((64, 257), dtype=bool), 0, 1).astype(jnp.int32)
        return (x, ctx_1024, mask_BxS2_if0)
    x, ctx_1024, mask_BxS2_if0 = _rec_inputs()

    def _L0_xattn_setup():
        import jax, jax.numpy as jnp
        import numpy as np
        import math
        B, M, D, H, NK = (4, 1024, 512, 16, 5)
        HD = D // H

        def _gather_pad0(x, idx):
            Bx, Hx, W, hd = x.shape
            valid = (idx >= 0) & (idx < W)
            idxc = jnp.clip(idx, 0, W - 1).reshape(Bx, Hx, -1)
            g = jnp.take_along_axis(x, idxc[..., None], axis=2)
            g = g.reshape(idx.shape + (hd,))
            return g * valid[..., None].astype(x.dtype)
        key = jax.random.key(seed)
        ks = jax.random.split(key, 9)
        w = lambda k, shape: jax.random.normal(k, shape, jnp.float32) * 0.02
        return {'k': jax.random.normal(ks[0], (B, M, D), jnp.float32), 'v': jax.random.normal(ks[1], (B, M, D), jnp.float32), 'q': jax.random.normal(ks[2], (B, M, D), jnp.float32), 'mask': jnp.zeros((B, M), jnp.int32), 'Wk': w(ks[3], (D, D)), 'bk': jnp.zeros((D,), jnp.float32), 'Wv': w(ks[4], (D, D)), 'bv': jnp.zeros((D,), jnp.float32), 'Wq': w(ks[5], (D, D)), 'bq': jnp.zeros((D,), jnp.float32), 'Woff': w(ks[6], (H * NK, D)), 'boff': jnp.zeros((H * NK,), jnp.float32), 'Wo': w(ks[7], (D, D)), 'bo': jnp.zeros((D,), jnp.float32)}
    _L0_xattn_all = _L0_xattn_setup()
    _L0_xattn_in = {k: v for k, v in _L0_xattn_all.items() if k in ('Wk', 'bk', 'Wv', 'bv', 'Wq', 'bq', 'Woff', 'boff', 'Wo', 'bo')}
    del _L0_xattn_all

    def _L0_attn_setup():
        import jax, jax.numpy as jnp
        import numpy as np
        B, L, DIM, H, D_INNER, CHUNK, KSIZE = (4, 1024, 512, 16, 4, 16, 4)
        HD = DIM // H
        BASE_LR = 0.001

        def short_conv(x, w):
            l = x.shape[1]
            xp = jnp.pad(x, ((0, 0), (KSIZE - 1, 0), (0, 0)))
            y = sum((w[:, j] * xp[:, j:j + l, :] for j in range(KSIZE)))
            return y + x

        def _semilinear(hidden_states, Wq, Wk, Wv, Wlr, Wo, conv_q, conv_k, conv_v, W_in_init, W_out_init):
            b, l, _ = hidden_states.shape
            n = l // CHUNK
            q = short_conv(hidden_states @ Wq, conv_q).reshape(b, l, H, HD)
            k = short_conv(hidden_states @ Wk, conv_k).reshape(b, l, H, HD)
            v = short_conv(hidden_states @ Wv, conv_v).reshape(b, l, H, HD)
            lr = jax.nn.softplus(hidden_states @ Wlr + BASE_LR).reshape(b, l, H, 2)
            to_chunks = lambda t: jnp.moveaxis(t.reshape(b, n, CHUNK, H, t.shape[-1]), 1, 0)
            qc, kc, vc, lrc = (to_chunks(t) for t in (q, k, v, lr))
            mask = jnp.tril(jnp.ones((CHUNK, CHUNK), bool))
            scale = 1.0 / np.sqrt(HD).astype(np.float32)

            def step(carry, chunk):
                W_in, W_out = carry
                qch, kch, vch, lrch = chunk
                k_h = jax.nn.softmax(jnp.einsum('blhd,bDhd->blhD', kch, W_in), axis=-1) * lrch[..., 1:]
                q_h = jax.nn.softmax(jnp.einsum('blhd,bDhd->blhD', qch, W_in), axis=-1)
                qk = jnp.where(mask, jnp.einsum('bqhD,bkhD->bhqk', q_h, k_h), 0.0)
                o = jnp.einsum('bqhD,bDhd->bqhd', q_h, W_out) + jnp.einsum('bhqk,bkhd->bqhd', qk, vch)
                W_out = W_out + jnp.einsum('bnhD,bnhd->bDhd', k_h, vch)
                for _ in range(2):
                    Wc = jnp.concatenate([W_in, W_out], axis=2)
                    Kc = jnp.concatenate([kch, vch], axis=2)
                    Vc = jnp.concatenate([vch, kch], axis=2)
                    attn = jax.nn.softmax(jnp.einsum('bqhd,bkhd->bhqk', Wc, Kc) * scale, axis=-1)
                    G = jnp.einsum('bhqk,bkhd->bqhd', attn, Vc)
                    G_out, G_in = jnp.split(-G, 2, axis=2)
                    W_in = W_in - lrch[:, :1, :, :1] * G_in
                    W_out = W_out - lrch[:, :1, :, 1:] * G_out
                return ((W_in, W_out), o)
            W_in0 = jnp.broadcast_to(W_in_init, (b, D_INNER, H, HD)) + 0.0
            W_out0 = jnp.broadcast_to(W_out_init, (b, D_INNER, H, HD)) + 0.0
            _, o = jax.lax.scan(step, (W_in0, W_out0), (qc, kc, vc, lrc))
            o = jnp.moveaxis(o, 0, 1).reshape(b, l, H * HD)
            return o @ Wo
        key = jax.random.key(seed)
        ks = jax.random.split(key, 11)
        s = DIM ** (-0.5)
        cs = KSIZE ** (-0.5)
        return {'hidden_states': jax.random.normal(ks[0], (B, L, DIM), jnp.float32), 'Wq': jax.random.normal(ks[1], (DIM, DIM), jnp.float32) * s, 'Wk': jax.random.normal(ks[2], (DIM, DIM), jnp.float32) * s, 'Wv': jax.random.normal(ks[3], (DIM, DIM), jnp.float32) * s, 'Wlr': jax.random.normal(ks[4], (DIM, 2 * H), jnp.float32) * s, 'Wo': jax.random.normal(ks[5], (DIM, DIM), jnp.float32) * s, 'conv_q': jax.random.normal(ks[6], (DIM, KSIZE), jnp.float32) * cs, 'conv_k': jax.random.normal(ks[7], (DIM, KSIZE), jnp.float32) * cs, 'conv_v': jax.random.normal(ks[8], (DIM, KSIZE), jnp.float32) * cs, 'W_in_init': jax.random.normal(ks[9], (1, D_INNER, H, HD), jnp.float32) * HD ** (-0.5), 'W_out_init': jax.random.normal(ks[10], (1, D_INNER, H, HD), jnp.float32) * D_INNER ** (-0.5)}
    _L0_attn_all = _L0_attn_setup()
    _L0_attn_in = {k: v for k, v in _L0_attn_all.items() if k in ('Wq', 'Wk', 'Wv', 'Wlr', 'Wo', 'conv_q', 'conv_k', 'conv_v', 'W_in_init', 'W_out_init')}
    del _L0_attn_all

    def _L0_ffn_setup():
        import jax, jax.numpy as jnp
        import numpy as np
        B, S, H, E = (2, 4096, 512, 8)
        SCALE = 0.5
        key = jax.random.key(seed)
        k1, k2 = jax.random.split(key)
        x = jax.random.normal(k1, (B, S, H), dtype=jnp.float32)
        gate_w = jax.random.normal(k2, (E, H), dtype=jnp.float32) * 0.02
        coeff = SCALE * (1.0 + 0.05 * jnp.arange(E, dtype=jnp.float32))
        expert_w = coeff[:, None, None] * jnp.eye(H, dtype=jnp.float32)
        return {'x': x, 'gate_w': gate_w, 'expert_w': expert_w}
    _L0_ffn_all = _L0_ffn_setup()
    _L0_ffn_in = {k: v for k, v in _L0_ffn_all.items() if k in ('gate_w', 'expert_w')}
    del _L0_ffn_all
    return {'x': x, 'ctx_1024': ctx_1024, 'mask_BxS2_if0': mask_BxS2_if0, 'L0_xattn_Wk': _L0_xattn_in['Wk'], 'L0_xattn_bk': _L0_xattn_in['bk'], 'L0_xattn_Wv': _L0_xattn_in['Wv'], 'L0_xattn_bv': _L0_xattn_in['bv'], 'L0_xattn_Wq': _L0_xattn_in['Wq'], 'L0_xattn_bq': _L0_xattn_in['bq'], 'L0_xattn_Woff': _L0_xattn_in['Woff'], 'L0_xattn_boff': _L0_xattn_in['boff'], 'L0_xattn_Wo': _L0_xattn_in['Wo'], 'L0_xattn_bo': _L0_xattn_in['bo'], 'L0_attn_Wq': _L0_attn_in['Wq'], 'L0_attn_Wk': _L0_attn_in['Wk'], 'L0_attn_Wv': _L0_attn_in['Wv'], 'L0_attn_Wlr': _L0_attn_in['Wlr'], 'L0_attn_Wo': _L0_attn_in['Wo'], 'L0_attn_conv_q': _L0_attn_in['conv_q'], 'L0_attn_conv_k': _L0_attn_in['conv_k'], 'L0_attn_conv_v': _L0_attn_in['conv_v'], 'L0_attn_W_in_init': _L0_attn_in['W_in_init'], 'L0_attn_W_out_init': _L0_attn_in['W_out_init'], 'L0_ffn_gate_w': _L0_ffn_in['gate_w'], 'L0_ffn_expert_w': _L0_ffn_in['expert_w']}

def reference(x, ctx_1024, mask_BxS2_if0, L0_xattn_Wk, L0_xattn_bk, L0_xattn_Wv, L0_xattn_bv, L0_xattn_Wq, L0_xattn_bq, L0_xattn_Woff, L0_xattn_boff, L0_xattn_Wo, L0_xattn_bo, L0_attn_Wq, L0_attn_Wk, L0_attn_Wv, L0_attn_Wlr, L0_attn_Wo, L0_attn_conv_q, L0_attn_conv_k, L0_attn_conv_v, L0_attn_W_in_init, L0_attn_W_out_init, L0_ffn_gate_w, L0_ffn_expert_w):
    import jax
    import jax.numpy as jnp

    def _L0_xattn_ref(k, v, q, mask, Wk, bk, Wv, bv, Wq, bq, Woff, boff, Wo, bo):
        import jax, jax.numpy as jnp
        import numpy as np
        import math
        B, M, D, H, NK = (4, 1024, 512, 16, 5)
        HD = D // H

        def _gather_pad0(x, idx):
            Bx, Hx, W, hd = x.shape
            valid = (idx >= 0) & (idx < W)
            idxc = jnp.clip(idx, 0, W - 1).reshape(Bx, Hx, -1)
            g = jnp.take_along_axis(x, idxc[..., None], axis=2)
            g = g.reshape(idx.shape + (hd,))
            return g * valid[..., None].astype(x.dtype)
        Bq, Q, _ = q.shape
        key_len = k.shape[1]
        K = jnp.einsum('bmd,ed->bme', k, Wk) + bk
        V = jnp.einsum('bmd,ed->bme', v, Wv) + bv
        Qp = jnp.einsum('bqd,ed->bqe', q, Wq) + bq
        off = jnp.einsum('bqd,ed->bqe', Qp, Woff) + boff
        off = off.reshape(Bq, Q, H, NK).transpose(0, 2, 1, 3)
        Kh = K.reshape(Bq, key_len, H, HD).transpose(0, 2, 1, 3)
        Vh = V.reshape(Bq, key_len, H, HD).transpose(0, 2, 1, 3)
        Qh = Qp.reshape(Bq, Q, H, HD).transpose(0, 2, 1, 3)
        loc = jnp.arange(Q, dtype=jnp.float32)[:, None]
        left = -NK // 2
        ref = jnp.arange(left, NK + left, dtype=jnp.float32)
        sign_lens = (1 - mask).sum(-1).astype(jnp.float32) - 1.0
        loc_x = jnp.mod(ref + off + loc, sign_lens[:, None, None, None])
        xg = loc_x / (key_len - 1) * 2.0 - 1.0
        ix = ((xg + 1.0) * key_len - 1.0) / 2.0
        x0 = jnp.floor(ix)
        dx = ix - x0
        i0 = x0.astype(jnp.int32)
        i1 = i0 + 1
        w0 = (1.0 - dx)[..., None]
        w1 = dx[..., None]
        sk = 0.5 * (w0 * _gather_pad0(Kh, i0) + w1 * _gather_pad0(Kh, i1))
        sv = 0.5 * (w0 * _gather_pad0(Vh, i0) + w1 * _gather_pad0(Vh, i1))
        scores = jnp.einsum('bhqd,bhqkd->bhqk', Qh / math.sqrt(HD), sk)
        attn = jax.nn.softmax(scores, axis=-1)
        ctx = jnp.einsum('bhqk,bhqkd->bhqd', attn, sv)
        ctx = ctx.transpose(0, 2, 1, 3).reshape(Bq, Q, H * HD)
        return jnp.einsum('bqd,ed->bqe', ctx, Wo) + bo

    def _L0_attn_ref(hidden_states, Wq, Wk, Wv, Wlr, Wo, conv_q, conv_k, conv_v, W_in_init, W_out_init):
        import jax, jax.numpy as jnp
        import numpy as np
        B, L, DIM, H, D_INNER, CHUNK, KSIZE = (4, 1024, 512, 16, 4, 16, 4)
        HD = DIM // H
        BASE_LR = 0.001

        def short_conv(x, w):
            l = x.shape[1]
            xp = jnp.pad(x, ((0, 0), (KSIZE - 1, 0), (0, 0)))
            y = sum((w[:, j] * xp[:, j:j + l, :] for j in range(KSIZE)))
            return y + x

        def _semilinear(hidden_states, Wq, Wk, Wv, Wlr, Wo, conv_q, conv_k, conv_v, W_in_init, W_out_init):
            b, l, _ = hidden_states.shape
            n = l // CHUNK
            q = short_conv(hidden_states @ Wq, conv_q).reshape(b, l, H, HD)
            k = short_conv(hidden_states @ Wk, conv_k).reshape(b, l, H, HD)
            v = short_conv(hidden_states @ Wv, conv_v).reshape(b, l, H, HD)
            lr = jax.nn.softplus(hidden_states @ Wlr + BASE_LR).reshape(b, l, H, 2)
            to_chunks = lambda t: jnp.moveaxis(t.reshape(b, n, CHUNK, H, t.shape[-1]), 1, 0)
            qc, kc, vc, lrc = (to_chunks(t) for t in (q, k, v, lr))
            mask = jnp.tril(jnp.ones((CHUNK, CHUNK), bool))
            scale = 1.0 / np.sqrt(HD).astype(np.float32)

            def step(carry, chunk):
                W_in, W_out = carry
                qch, kch, vch, lrch = chunk
                k_h = jax.nn.softmax(jnp.einsum('blhd,bDhd->blhD', kch, W_in), axis=-1) * lrch[..., 1:]
                q_h = jax.nn.softmax(jnp.einsum('blhd,bDhd->blhD', qch, W_in), axis=-1)
                qk = jnp.where(mask, jnp.einsum('bqhD,bkhD->bhqk', q_h, k_h), 0.0)
                o = jnp.einsum('bqhD,bDhd->bqhd', q_h, W_out) + jnp.einsum('bhqk,bkhd->bqhd', qk, vch)
                W_out = W_out + jnp.einsum('bnhD,bnhd->bDhd', k_h, vch)
                for _ in range(2):
                    Wc = jnp.concatenate([W_in, W_out], axis=2)
                    Kc = jnp.concatenate([kch, vch], axis=2)
                    Vc = jnp.concatenate([vch, kch], axis=2)
                    attn = jax.nn.softmax(jnp.einsum('bqhd,bkhd->bhqk', Wc, Kc) * scale, axis=-1)
                    G = jnp.einsum('bhqk,bkhd->bqhd', attn, Vc)
                    G_out, G_in = jnp.split(-G, 2, axis=2)
                    W_in = W_in - lrch[:, :1, :, :1] * G_in
                    W_out = W_out - lrch[:, :1, :, 1:] * G_out
                return ((W_in, W_out), o)
            W_in0 = jnp.broadcast_to(W_in_init, (b, D_INNER, H, HD)) + 0.0
            W_out0 = jnp.broadcast_to(W_out_init, (b, D_INNER, H, HD)) + 0.0
            _, o = jax.lax.scan(step, (W_in0, W_out0), (qc, kc, vc, lrc))
            o = jnp.moveaxis(o, 0, 1).reshape(b, l, H * HD)
            return o @ Wo
        return _semilinear(hidden_states, Wq, Wk, Wv, Wlr, Wo, conv_q, conv_k, conv_v, W_in_init, W_out_init)

    def _L0_ffn_ref(x, gate_w, expert_w):
        import jax, jax.numpy as jnp
        import numpy as np
        B, S, H, E = (2, 4096, 512, 8)
        SCALE = 0.5
        scores = jnp.einsum('bsh,eh->bse', x, gate_w)
        chosen = jnp.argmax(scores, axis=-1)
        onehot = jax.nn.one_hot(chosen, gate_w.shape[0], dtype=x.dtype)
        expert_out = jnp.einsum('bsh,efh->bsef', x, expert_w)
        return x + jnp.einsum('bsef,bse->bsf', expert_out, onehot)
    x = x + _L0_xattn_ref(ctx_1024, ctx_1024, _layernorm(x, axis=-1), mask_BxS2_if0, L0_xattn_Wk, L0_xattn_bk, L0_xattn_Wv, L0_xattn_bv, L0_xattn_Wq, L0_xattn_bq, L0_xattn_Woff, L0_xattn_boff, L0_xattn_Wo, L0_xattn_bo)
    x = x + _L0_attn_ref(_layernorm(x, axis=-1), L0_attn_Wq, L0_attn_Wk, L0_attn_Wv, L0_attn_Wlr, L0_attn_Wo, L0_attn_conv_q, L0_attn_conv_k, L0_attn_conv_v, L0_attn_W_in_init, L0_attn_W_out_init)
    x = x + _L0_ffn_ref(_layernorm(x, axis=-1), L0_ffn_gate_w, L0_ffn_expert_w)
    return x

_drawn_inputs = setup_inputs


def setup_inputs(seed=0):
    import zlib

    import numpy as np

    out = dict(_drawn_inputs(seed))
    spreads = {'L0_xattn_bk': (0.0, 0.8),
     'L0_xattn_bv': (0.0, 0.1),
     'L0_xattn_bq': (0.0, 0.576),
     'L0_xattn_boff': (0.0, 0.374),
     'L0_xattn_bo': (0.0, 0.1)}
    factors = {'L0_xattn_Wk': 5.878, 'L0_ffn_gate_w': 4.477}
    for name, (base, spread) in spreads.items():
        noise = np.random.default_rng([zlib.crc32(name.encode()), seed]).standard_normal(out[name].shape)
        drawn = base * np.exp(spread * noise) if base else spread * noise
        out[name] = jnp.asarray(drawn.astype(out[name].dtype))
    for name, factor in factors.items():
        out[name] = (out[name] * factor).astype(out[name].dtype)
    return out
```

```python
from contextlib import ExitStack

import numpy as np

import concourse.bass as bass
from concourse import mybir

F32 = mybir.dt.float32
I32 = mybir.dt.int32
ALU = mybir.AluOpType
ACT = mybir.ActivationFunctionType
AX = mybir.AxisListType.X

P = 128
B, L, D = 64, 32, 512
M = 257
H, HD = 16, 32
NK = 5
KC = D // P
HQ = P // HD
BG = 8
NG = B // BG
GT = BG * L
TT = GT // P
C = 16
DI = 4
E = 8
TAIL, HEAD = 8, 36
W = TAIL + HEAD
PAIRS = BG // 2
EPS = 1e-5
NEG = -1e30
ATT_SCALE = float(HD) ** -0.5
MAGIC = 12582912.0

CI, CNEG, CBM, CHM, CCA, CMC = 0, P, 2 * P, 3 * P, 4 * P, 5 * P
CREF = CMC + M
CQ = CREF + 2 * NK
CONE = CQ + 1
CORD = CONE + 1
CN = CORD + E


def shape_constants():
    c = np.zeros((P, CN), np.float32)
    p = np.arange(P)
    c[:, CI:CI + P] = np.eye(P)
    row_b, row_h = (p // DI) % BG, p // HD
    tok_t, tok_b = p // BG, p % BG
    same = row_b[:, None] == tok_b[None, :]
    c[:, CNEG:CNEG + P] = np.where(same, 0.0, NEG)
    c[:, CBM:CBM + BG] = tok_b[:, None] == np.arange(BG)[None, :]
    c[:, CHM:CHM + P] = (p // HD)[:, None] == row_h[None, :]
    c[:, CCA:CCA + P] = (tok_b[:, None] == tok_b[None, :]) & (tok_t[:, None] <= tok_t[None, :])
    c[:, CMC:CMC + M] = ((np.arange(M) - TAIL) % M)[None, :]
    left = -NK // 2
    c[:, CREF:CREF + 2 * NK] = np.tile(np.arange(left, NK + left), 2)[None, :]
    c[:, CQ] = p % L
    c[:, CONE] = 1.0
    c[:, CORD:CORD + E] = np.arange(E, 0, -1)[None, :]
    return c


class Count:

    def __init__(self, sem, per=1):
        self.sem, self.per = sem, per
        self.base = 16 if per == 16 else 1

    def at(self, i, j):
        return i * self.per + j + self.base


class Chain:

    def __init__(self, eng, count, i, settle=None):
        self.eng, self.count, self.i, self.n, self.settle = eng, count, i, 0, settle

    def link(self, instruction):
        self.n += 1
        instruction.then_inc(self.count.sem, 1)
        self.eng.wait_ge(self.count.sem, self.count.at(self.i, self.n))
        if self.settle:
            self.settle(self.eng)

    def close(self):
        assert self.n == self.count.per, (self.n, self.count.per)


def bc(ap, axis, n):
    shape = list(ap.shape)
    return ap.unsqueeze(axis).broadcast_to(shape[:axis] + [n] + shape[axis:])


def act_deviation(nc, act, i, mv, rstd, var, std):
    act.wait_ge(var.sem, var.at(i, 1))
    nc.scalar.activation(rstd, mv[:, :, 1], ACT.Sqrt, bias=EPS).then_inc(std.sem, 1)


def layer_norm(nc, m, chain, x, h, stats, mv, rstd, var, std, tiles):
    for t in range(tiles):
        chain.link(nc.vector.bn_stats(stats[:, t, :], x[:, t, :]))
    m.settle(chain.eng)
    for t in range(tiles):
        last = nc.vector.bn_aggr(mv[:, t, :], stats[:, t, :])
    last.then_inc(var.sem, 1)
    chain.eng.wait_ge(std.sem, std.at(chain.i, 1))
    chain.link(nc.vector.reciprocal(rstd[:, 0:tiles], rstd[:, 0:tiles]))
    last = None
    for t in range(tiles):
        last = nc.vector.tensor_scalar(h[:, t, :], x[:, t, :], mv[:, t, 0:1], rstd[:, t:t + 1],
                                       ALU.subtract, ALU.mult)
    return last


LN_LINKS = TT + 1


class Ring:

    def __init__(self, m, name, banks, plan):
        self.ps = m.ps(name, [P, banks, 512])
        self.names = [n for n, _ in plan]
        self.reader = dict(plan)
        self.banks = banks
        assert len(self.reader) == len(plan)
        self.filled = m.count(f"{name}_filled", len(plan))
        self.read = {e: m.count(f"{name}_read_{e}", sum(r == e for _, r in plan)) for e in sorted(set(self.reader.values()))}

        for c in self.read.values():
            c.base = c.per

    def bank(self, name, parts=None):
        ps = self.ps[:, self.names.index(name) % self.banks, :]
        return ps if parts is None else ps.rearrange("p (g n) -> p g n", g=parts)

    def full(self, i, name):
        return self.filled.sem, self.filled.at(i, self.names.index(name) + 1)

    def used(self, i, name):
        n, e = self.names.index(name), self.reader[name]
        return self.read[e].sem, self.read[e].at(i, sum(self.reader[x] == e for x in self.names[:n + 1]))

    def free(self, i, name):
        n = self.names.index(name)
        if n >= self.banks:
            return self.used(i, self.names[n - self.banks])
        last = max(x for x in range(len(self.names)) if x % self.banks == n)
        sem, value = self.used(i, self.names[last])
        return sem, value - self.read[self.reader[self.names[last]]].per


class Mem:

    def __init__(self, nc, ctx, tag):
        self.nc, self.ctx, self.tag = nc, ctx, tag
        self.counts, self.passed = [], None

    def sb(self, name, shape, dt=F32):
        return self.ctx.enter_context(self.nc.sbuf_tensor(f"{self.tag}_{name}", shape, dt))

    def ps(self, name, shape, dt=F32):
        return self.ctx.enter_context(self.nc.psum_tensor(f"{self.tag}_psum_{name}", shape, dt))

    def count(self, name, per=1):
        self.counts.append(Count(self.ctx.enter_context(self.nc.semaphore(f"{self.tag}_sem_{name}")), per))
        return self.counts[-1]

    def start(self, eng):
        for c in self.counts:
            eng.sem_inc(c.sem, c.base)

    def settle(self, eng):
        if self.passed is None:
            self.passed = self.ctx.enter_context(self.nc.semaphore(f"{self.tag}_sem_passed"))
        eng.sem_inc(self.passed, 1)


def project_phase(nc, a, k):
    with ExitStack() as ctx:
        m = Mem(nc, ctx, "pj")
        xs = m.sb("x", [P, TT, D])
        h = m.sb("h", [P, TT, D])
        hT = m.sb("hT", [P, KC, GT])
        QT = m.sb("QT", [P, KC, GT])
        off = m.sb("off", [P, TT, H * NK])
        stats, mv, rstd = m.sb("st", [P, TT, 6]), m.sb("mv", [P, TT, 2]), m.sb("rs", [P, TT])
        Wq, bq = m.sb("Wq", [P, KC, D]), m.sb("bq", [P, KC])
        Woff, boff = m.sb("Woff", [P, KC, H * NK]), m.sb("boff", [P, H * NK])
        mask_i, mask_f = m.sb("mi", [B, M], I32), m.sb("mf", [B, M])
        length, length_all = m.sb("len", [B, 1]), m.sb("lena", [P, 2, B])
        wide = [m.sb(f"wide{j}", [P, B // 2, KC, 2 * NK]) for j in range(4)]
        bad = m.sb("bad", [P, 2])
        ps_t, ps_q, ps_o = m.ps("t", [P, TT, D]), m.ps("q", [P, KC, GT]), m.ps("o", [P, TT, H * NK])
        ps_l = m.ps("l", [P, 512])

        x_in, w_in, q_out = m.count("x_in", 16), m.count("w_in"), m.count("q_out", 16)
        h_done = m.count("h_done")
        tr_done, hT_done = m.count("tr"), m.count("hT", TT)
        q_done, qT_done = m.count("q"), m.count("qT", KC)
        o_done, off_done = m.count("o"), m.count("off")
        link = m.count("link", LN_LINKS + 1)
        plink = m.count("plink")
        len_ps, len_in, bad_done, bad_ps = m.count("lps"), m.count("lin"), m.count("bd"), m.count("bp")
        flag_done, var, std = m.count("flag"), m.count("var"), m.count("std")
        block = ctx.enter_context(nc.Block())

        @block.sync
        def _(sp):
            sp.dma_start(mask_i[:], a["mask"]).then_inc(w_in.sem, 16)
            sp.dma_start(Wq[:], a["xWq"]).then_inc(w_in.sem, 16)
            sp.dma_start(Woff[:], a["xWoff"]).then_inc(w_in.sem, 16)
            sp.dma_start(bq[:], a["xbq"]).then_inc(w_in.sem, 16)
            sp.dma_start(boff[:], a["xboff"].partition_broadcast(P)).then_inc(w_in.sem, 16)
            sp.dma_start(k["const"][:], a["const"]).then_inc(w_in.sem, 16)
            with sp.Fori(0, NG) as i:
                sp.wait_ge(h_done.sem, h_done.at(i, 0))
                sp.dma_start(xs[:], a["x_tok"][bass.ds(i, 1)].rearrange("o t p d -> (o p) t d")).then_inc(x_in.sem, 16)
                sp.wait_ge(qT_done.sem, qT_done.at(i, KC))
                sp.dma_start(a["q_scr"][bass.ds(i, 1)].rearrange("o p k t -> (o p) k t"), QT[:]).then_inc(q_out.sem, 16)
            sp.wait_ge(q_out.sem, q_out.at(NG, 0))

        @block.gpsimd
        def _(pool):
            m.start(pool)
            pool.wait_ge(flag_done.sem, flag_done.at(0, 1))

        @block.vector
        def _(dve):
            dve.wait_ge(w_in.sem, w_in.at(0, 96))
            with dve.Fori(0, NG) as i:
                chain = Chain(dve, link, i)
                dve.wait_ge(x_in.sem, x_in.at(i, 16))
                dve.wait_ge(tr_done.sem, tr_done.at(i, 0))
                layer_norm(nc, m, chain, xs, h, stats, mv, rstd, var, std, TT).then_inc(h_done.sem, 1)
                dve.wait_ge(o_done.sem, o_done.at(i, 1))
                chain.link(nc.vector.tensor_tensor(off[:], ps_o[:], bc(boff[:], 1, TT), ALU.add))
                for b in range(P // L):
                    for hq in range(HQ):
                        src = off[b * L:(b + 1) * L].rearrange("p t (g h k) -> p t g h k", g=KC, h=HQ)[:, :, :, hq, :]
                        dst = k["ix"][hq * L:(hq + 1) * L, bass.ds(i * PAIRS, PAIRS)].rearrange(
                            "p (t u) g v k -> p t u g v k", t=TT)[:, :, b // 2, :, b % 2]
                        last = nc.vector.tensor_copy(dst, src)
                last.then_inc(off_done.sem, 1)
                chain.close()

            step = Chain(dve, plink, 0)
            step.link(nc.vector.tensor_copy(mask_f[:], mask_i[:]))
            step.link(nc.vector.tensor_scalar(mask_f[:], mask_f[:], -1.0, 1.0, ALU.mult, ALU.add))
            step.link(nc.vector.tensor_reduce(length[:], mask_f[:], AX, ALU.add))
            nc.vector.tensor_scalar_add(length[:], length[:], -1.0).then_inc(len_in.sem, 1)
            dve.wait_ge(len_ps.sem, len_ps.at(0, 1))
            step.link(nc.vector.tensor_copy(length_all[:, 0, :], ps_l[:, 0:B]))
            step.link(nc.vector.reciprocal(length_all[:, 1, :], length_all[:, 0, :]))
            n_, rn = wide[2][:], wide[3][:]
            for j, full in enumerate((n_, rn)):
                pairs = bc(length_all[:, j, :], 2, NK).rearrange("p (u v) k -> p u v k", v=2)
                for g in range(KC):
                    last = nc.vector.tensor_copy(full[:, :, g, :].rearrange("p u (v k) -> p u v k", v=2), pairs)
            step.link(last)
            dve.wait_ge(off_done.sem, off_done.at(NG, 0))
            ix, t0, t1 = k["ix"].rearrange("p u g v k -> p u g (v k)"), wide[0][:], wide[1][:]
            flat = "p u g v -> p (u g v)"
            step.link(nc.vector.tensor_tensor(ix.rearrange("p u g v -> p (u g) v"), ix.rearrange("p u g v -> p (u g) v"),
                                              bc(k["const"][:, CREF:CREF + 2 * NK], 1, B // 2 * KC), ALU.add))
            ix, t0, t1, n_, rn = (v.rearrange(flat) for v in (ix, t0, t1, n_, rn))
            step.link(nc.vector.tensor_scalar(ix, ix, k["const"][:, CQ:CQ + 1], None, ALU.add))
            step.link(nc.vector.tensor_tensor(t0, ix, rn, ALU.mult))
            step.link(nc.vector.tensor_scalar(t0, t0, MAGIC, None, ALU.add))
            step.link(nc.vector.tensor_scalar(t0, t0, -MAGIC, None, ALU.add))
            step.link(nc.vector.tensor_tensor(t0, t0, n_, ALU.mult))
            step.link(nc.vector.tensor_tensor(ix, ix, t0, ALU.subtract))
            step.link(nc.vector.tensor_tensor(t0, ix, n_, ALU.mult))
            step.link(nc.vector.tensor_scalar(t0, t0, 0.0, None, ALU.is_lt))
            step.link(nc.vector.tensor_tensor(t0, t0, n_, ALU.mult))
            step.link(nc.vector.tensor_tensor(ix, ix, t0, ALU.add))
            step.link(nc.vector.tensor_scalar(ix, ix, 1.0 / (M - 1), 2.0, ALU.mult, ALU.mult))
            step.link(nc.vector.tensor_scalar(ix, ix, -1.0, 1.0, ALU.add, ALU.add))
            step.link(nc.vector.tensor_scalar(ix, ix, float(M), -1.0, ALU.mult, ALU.add))
            step.link(nc.vector.tensor_scalar(ix, ix, 0.5, None, ALU.mult))
            step.link(nc.vector.tensor_scalar(t0, ix, float(HEAD - 1), None, ALU.is_ge))
            step.link(nc.vector.tensor_scalar(t1, ix, float(M - TAIL), None, ALU.is_lt))
            step.link(nc.vector.tensor_tensor(t0, t0, t1, ALU.mult))
            nc.vector.tensor_reduce(bad[:, 0:1], t0, AX, ALU.max).then_inc(bad_done.sem, 1)
            dve.wait_ge(bad_ps.sem, bad_ps.at(0, 1))
            nc.vector.tensor_copy(k["flag"], ps_l[0:1, 256:257]).then_inc(flag_done.sem, 1)

        @block.tensor
        def _(pe):
            pe.wait_ge(w_in.sem, w_in.at(0, 96))
            with pe.Fori(0, NG) as i:
                pe.wait_ge(h_done.sem, h_done.at(i, 1))
                pe.wait_ge(hT_done.sem, hT_done.at(i, 0))
                for t in range(TT):
                    for c in range(KC):
                        last = nc.tensor.transpose(ps_t[:, t, c * P:(c + 1) * P], h[:, t, c * P:(c + 1) * P], k["ident"])
                last.then_inc(tr_done.sem, 1)
                pe.wait_ge(hT_done.sem, hT_done.at(i, TT))
                pe.wait_ge(qT_done.sem, qT_done.at(i, 0))
                for e in range(KC):
                    for c in range(KC):
                        last = nc.tensor.matmul(ps_q[:, e, :], Wq[:, c, e * P:(e + 1) * P], hT[:, c, :],
                                                start=(c == 0), stop=(c == KC - 1))
                last.then_inc(q_done.sem, 1)
                pe.wait_ge(qT_done.sem, qT_done.at(i, KC))
                pe.wait_ge(off_done.sem, off_done.at(i, 0))
                for t in range(TT):
                    for c in range(KC):
                        last = nc.tensor.matmul(ps_o[:, t, :], QT[:, c, t * P:(t + 1) * P], Woff[:, c, :],
                                                start=(c == 0), stop=(c == KC - 1))
                last.then_inc(o_done.sem, 1)
            pe.wait_ge(len_in.sem, len_in.at(0, 1))
            nc.tensor.matmul(ps_l[:, 0:B], length[:].broadcast_to([B, P]), k["const"][0:B, CI:CI + B],
                             start=True, stop=True).then_inc(len_ps.sem, 1)
            pe.wait_ge(bad_done.sem, bad_done.at(0, 1))
            nc.tensor.matmul(ps_l[0:1, 256:257], bad[:, 0:1], k["ones"], start=True, stop=True).then_inc(bad_ps.sem, 1)

        @block.scalar
        def _(act):
            act.wait_ge(w_in.sem, w_in.at(0, 96))
            with act.Fori(0, NG) as i:
                act_deviation(nc, act, i, mv, rstd[:], var, std)
                act.wait_ge(tr_done.sem, tr_done.at(i, 1))
                act.wait_ge(q_done.sem, q_done.at(i, 0))
                for t in range(TT):
                    nc.scalar.activation(hT[:, :, t * P:(t + 1) * P], ps_t[:, t, :].rearrange("p (c n) -> p c n", c=KC),
                                         ACT.Copy).then_inc(hT_done.sem, 1)
                act.wait_ge(q_done.sem, q_done.at(i, 1))
                act.wait_ge(q_out.sem, q_out.at(i, 0))
                act.wait_ge(o_done.sem, o_done.at(i, 0))
                for e in range(KC):
                    nc.scalar.activation(QT[:, e, :], ps_q[:, e, :], ACT.Identity,
                                         bias=bq[:, e:e + 1]).then_inc(qT_done.sem, 1)


class Interpolation:

    def __init__(self, m, nu, wr, ring, stride):
        self.nu, self.wr = nu, wr
        self.tent = [m.sb(f"tent{r}", [P, nu * NK, wr]) for r in range(ring)]
        self.prod = m.sb("prod", [P, nu * NK, wr])
        self.A = m.sb("A", [P, nu, stride])
        self.s, self.e = m.sb("s", [P, nu, NK]), m.sb("e", [P, nu, NK])
        self.top, self.tot = m.sb("top", [P, nu]), m.sb("tot", [P, nu])

    def pool_difference(self, nc, r, rows, ix):
        return nc.gpsimd.tensor_tensor(self.tent[r][:], bc(rows, 1, self.nu * NK), bc(ix, 2, self.wr), ALU.subtract)

    def act_abs(self, nc, r):
        return nc.scalar.activation(self.tent[r][:], self.tent[r][:], ACT.Abs)

    def act_tent(self, nc, r):
        return nc.scalar.activation(self.tent[r][:], self.tent[r][:], ACT.Relu, bias=1.0, scale=-1.0)

    def dve_scores(self, nc, chain, r, S):
        v = "p (u k) m -> p u k m"
        chain.link(nc.vector.tensor_tensor(self.prod[:].rearrange(v, k=NK), self.tent[r][:].rearrange(v, k=NK),
                                           bc(S, 2, NK), ALU.mult))
        chain.link(nc.vector.tensor_reduce(self.s[:].rearrange("p u k -> p (u k)"), self.prod[:], AX, ALU.add))
        chain.link(nc.vector.tensor_reduce(self.top[:], self.s[:], AX, ALU.max))
        return nc.vector.tensor_tensor(self.s[:], self.s[:], bc(self.top[:], 2, NK), ALU.subtract)

    def act_exp(self, nc):
        return nc.scalar.activation(self.e[:], self.s[:], ACT.Exp, scale=0.5 * ATT_SCALE)

    def dve_weights(self, nc, chain, r):
        chain.link(nc.vector.tensor_reduce(self.tot[:], self.e[:], AX, ALU.add))
        chain.link(nc.vector.reciprocal(self.tot[:], self.tot[:]))
        chain.link(nc.vector.scalar_tensor_tensor(self.e[:], self.e[:], 0.5, bc(self.tot[:], 2, NK), ALU.mult, ALU.mult))
        chain.link(nc.vector.tensor_tensor(self.prod[:], self.tent[r][:],
                                           bc(self.e[:].rearrange("p u k -> p (u k)"), 2, self.wr), ALU.mult))
        return nc.vector.tensor_reduce(self.A[:, :, 0:self.wr], self.prod[:].rearrange("p (u k) m -> p u m k", k=NK), AX, ALU.add)

    DVE_LINKS = 3 + 4


def attend_window_phase(nc, a, k):
    U = 2 * KC
    with ExitStack() as ctx:
        m = Mem(nc, ctx, "aw")
        craw, cw = m.sb("craw", [P, KC, W * BG]), m.sb("c", [P, KC, BG, 64])
        Q, Qblk = m.sb("Q", [P, KC, GT]), m.sb("Qb", [P, KC, BG, P])
        KT, V = m.sb("K", [P, KC, BG, W]), m.sb("V", [P, PAIRS, D])
        AT, cT = m.sb("AT", [P, KC, P]), m.sb("cT", [P, KC, GT])
        Wk, Wv = m.sb("Wk", [P, KC, D]), m.sb("Wv", [P, KC, D])
        bk, bv = m.sb("bk", [P, KC]), m.sb("bv", [P, D])
        ip = Interpolation(m, U, W, 2, 64)
        ps_kv, ps_s = m.ps("kv", [P, 2, 512]), m.ps("s", [P, 2, 512])
        ps_at, ps_av = m.ps("at", [P, KC, P]), m.ps("av", [P, 2, KC, P])

        w_in, c_in, q_in, c_out = m.count("w_in"), m.count("c_in", 16), m.count("q_in", 16), m.count("c_out", 16)
        zero, cw_done = m.count("zero"), m.count("cw")
        k_ps, k_cp = m.count("k_ps", KC), m.count("k_cp", KC)
        v_ps, v_cp = m.count("v_ps", PAIRS), m.count("v_cp", PAIRS)
        qb_done, s_ps = m.count("qb"), m.count("s_ps", PAIRS)
        diff, ab, tent = m.count("diff", PAIRS), m.count("ab", PAIRS), m.count("tent", PAIRS)
        sc_done, ex_done = m.count("sc", PAIRS), m.count("ex", PAIRS)
        A_done, at_ps, at_cp = m.count("A", PAIRS), m.count("at_ps", PAIRS), m.count("at_cp", PAIRS)
        av_ps, av_cp = m.count("av_ps", PAIRS), m.count("av_cp", PAIRS)
        link, plink = m.count("link", PAIRS * ip.DVE_LINKS), m.count("plink", HQ)
        block = ctx.enter_context(nc.Block())

        @block.sync
        def _(sp):
            sp.dma_start(Wk[:], a["xWk"]).then_inc(w_in.sem, 16)
            sp.dma_start(Wv[:], a["xWv"]).then_inc(w_in.sem, 16)
            sp.dma_start(bk[:], a["xbk"]).then_inc(w_in.sem, 16)
            sp.dma_start(bv[:], a["xbv"].partition_broadcast(P)).then_inc(w_in.sem, 16)
            with sp.Fori(0, NG) as i:
                sp.wait_ge(cw_done.sem, cw_done.at(i, 0))
                sp.dma_start(craw[:], a["ctx"][bass.ds(i, 1), :, :, 0:W * BG].rearrange("o p c w -> (o p) c w")).then_inc(c_in.sem, 16)
                sp.wait_ge(qb_done.sem, qb_done.at(i, 0))
                sp.dma_start(Q[:], a["q_scr"][bass.ds(i, 1)].rearrange("o p k t -> (o p) k t")).then_inc(q_in.sem, 16)
                sp.wait_ge(av_cp.sem, av_cp.at(i, PAIRS))
                sp.dma_start(a["c_scr"][bass.ds(i, 1)].rearrange("o p k t -> (o p) k t"), cT[:]).then_inc(c_out.sem, 16)
            sp.wait_ge(c_out.sem, c_out.at(NG, 0))

        @block.gpsimd
        def _(pool):
            m.start(pool)
            nc.gpsimd.memset(cw[:], 0.0).then_inc(zero.sem, 1)
            nc.gpsimd.memset(Qblk[:], 0.0).then_inc(zero.sem, 1)
            nc.gpsimd.memset(ip.A[:], 0.0).then_inc(zero.sem, 1)
            pool.wait_ge(zero.sem, zero.at(0, 3))
            with pool.Fori(0, NG) as i:
                pool.wait_ge(c_in.sem, c_in.at(i, 16))
                pool.wait_ge(v_ps.sem, v_ps.at(i, 0))
                m.settle(pool)
                nc.gpsimd.tensor_copy(cw[:, :, :, 0:W], craw[:].rearrange("p c (m b) -> p c b m", b=BG)).then_inc(cw_done.sem, 1)
                pool.wait_ge(cw_done.sem, cw_done.at(i, 1))
                m.settle(pool)
                steps = Chain(pool, plink, i, m.settle)
                pool.wait_ge(q_in.sem, q_in.at(i, 16))
                pool.wait_ge(s_ps.sem, s_ps.at(i, 0))
                m.settle(pool)
                for hq in range(HQ):
                    rows = slice(hq * HD, hq * HD + HD)
                    steps.link(nc.gpsimd.tensor_copy(Qblk[rows, :, :, hq * L:(hq + 1) * L],
                                                     Q[rows].rearrange("p c (b q) -> p c b q", q=L)))
                steps.close()
                pool.sem_inc(qb_done.sem, 1)
                for j in range(PAIRS):
                    if j >= 2:
                        pool.wait_ge(A_done.sem, A_done.at(i, j - 1))
                    else:
                        pool.wait_ge(A_done.sem, A_done.at(i, 0))
                    ix = k["ix"][:, bass.ds(i * PAIRS + j, 1)].rearrange("p u g v k -> p (u g v k)")
                    ip.pool_difference(nc, j % 2, k["const"][:, CMC:CMC + W], ix).then_inc(diff.sem, 1)
                    pool.wait_ge(diff.sem, diff.at(i, j + 1))
                m.settle(pool)

        @block.vector
        def _(dve):
            dve.wait_ge(w_in.sem, w_in.at(0, 64))
            with dve.Fori(0, NG) as i:
                chain = Chain(dve, link, i)
                dve.wait_ge(av_ps.sem, av_ps.at(i, 0))
                for j in range(PAIRS):
                    dve.wait_ge(v_ps.sem, v_ps.at(i, j + 1))
                    nc.vector.tensor_tensor(V[:, j, :], ps_kv[:, j % 2, :], bv[:], ALU.add).then_inc(v_cp.sem, 1)
                for j in range(PAIRS):
                    dve.wait_ge(s_ps.sem, s_ps.at(i, j + 1))
                    dve.wait_ge(tent.sem, tent.at(i, j + 1))
                    dve.wait_ge(A_done.sem, A_done.at(i, j))
                    S = ps_s[:, j % 2, 0:U * W].rearrange("p (u m) -> p u m", m=W)
                    ip.dve_scores(nc, chain, j % 2, S).then_inc(sc_done.sem, 1)
                    dve.wait_ge(ex_done.sem, ex_done.at(i, j + 1))
                    dve.wait_ge(at_ps.sem, at_ps.at(i, j))
                    ip.dve_weights(nc, chain, j % 2).then_inc(A_done.sem, 1)
                chain.close()

        @block.tensor
        def _(pe):
            pe.wait_ge(w_in.sem, w_in.at(0, 64))
            pe.wait_ge(zero.sem, zero.at(0, 3))
            with pe.Fori(0, NG) as i:
                pe.wait_ge(cw_done.sem, cw_done.at(i, 1))
                for e in range(KC):
                    if e < 2:
                        pe.wait_ge(v_cp.sem, v_cp.at(i, 0))
                    else:
                        pe.wait_ge(k_cp.sem, k_cp.at(i, e - 1))
                    for c in range(KC):
                        last = nc.tensor.matmul(ps_kv[:, e % 2, 0:W * BG], Wk[:, c, e * P:(e + 1) * P], cw[:, c, :, 0:W],
                                                start=(c == 0), stop=(c == KC - 1))
                    last.then_inc(k_ps.sem, 1)
                for j in range(PAIRS):
                    if j < 2:
                        pe.wait_ge(k_cp.sem, k_cp.at(i, KC - 1 + j))
                    else:
                        pe.wait_ge(v_cp.sem, v_cp.at(i, j - 1))
                    for c in range(KC):
                        rows = cw[:, c, 2 * j:2 * j + 2, :].rearrange("p b m -> p (b m)")
                        last = nc.tensor.matmul(ps_kv[:, j % 2, :], rows, Wv[:, c, :], start=(c == 0), stop=(c == KC - 1))
                    last.then_inc(v_ps.sem, 1)
                pe.wait_ge(k_cp.sem, k_cp.at(i, KC))
                pe.wait_ge(qb_done.sem, qb_done.at(i, 1))
                for j in range(PAIRS + 1):
                    if j < PAIRS:
                        pe.wait_ge(sc_done.sem, sc_done.at(i, max(j - 1, 0)))
                        for u in range(U):
                            b, g = 2 * j + u % 2, u // 2
                            last = nc.tensor.matmul(ps_s[:, j % 2, u * W:(u + 1) * W], Qblk[:, g, b, :], KT[:, g, b, :],
                                                    start=True, stop=True)
                        last.then_inc(s_ps.sem, 1)
                    if j >= 1:
                        jj = j - 1
                        pe.wait_ge(A_done.sem, A_done.at(i, j))
                        pe.wait_ge(at_cp.sem, at_cp.at(i, jj))
                        for g in range(KC):
                            last = nc.tensor.transpose(ps_at[:, g, :], ip.A[:, 2 * g:2 * g + 2, :].rearrange("p b m -> p (b m)"),
                                                       k["ident"])
                        last.then_inc(at_ps.sem, 1)
                        pe.wait_ge(at_cp.sem, at_cp.at(i, j))
                        pe.wait_ge(v_cp.sem, v_cp.at(i, PAIRS))
                        pe.wait_ge(av_cp.sem, av_cp.at(i, jj))
                        for u in range(U):
                            b, g = u % 2, u // 2
                            rows = slice(b * 64, b * 64 + W)
                            last = nc.tensor.matmul(ps_av[:, b, g, :], V[rows, jj, g * P:(g + 1) * P], AT[rows, g, :],
                                                    start=True, stop=True)
                        last.then_inc(av_ps.sem, 1)

        @block.scalar
        def _(act):
            act.wait_ge(w_in.sem, w_in.at(0, 64))
            with act.Fori(0, NG) as i:
                act.wait_ge(s_ps.sem, s_ps.at(i, 0))
                for e in range(KC):
                    act.wait_ge(k_ps.sem, k_ps.at(i, e + 1))
                    nc.scalar.activation(KT[:, e], ps_kv[:, e % 2, 0:W * BG].rearrange("p (b m) -> p b m", b=BG),
                                         ACT.Identity, bias=bk[:, e:e + 1]).then_inc(k_cp.sem, 1)

                def tents(j):
                    act.wait_ge(diff.sem, diff.at(i, j + 1))
                    ip.act_abs(nc, j % 2).then_inc(ab.sem, 1)
                    act.wait_ge(ab.sem, ab.at(i, j + 1))
                    ip.act_tent(nc, j % 2).then_inc(tent.sem, 1)

                tents(0)
                for j in range(PAIRS):
                    if j + 1 < PAIRS:
                        tents(j + 1)
                    act.wait_ge(sc_done.sem, sc_done.at(i, j + 1))
                    ip.act_exp(nc).then_inc(ex_done.sem, 1)
                    act.wait_ge(at_ps.sem, at_ps.at(i, j + 1))
                    act.wait_ge(av_ps.sem, av_ps.at(i, j))
                    nc.scalar.activation(AT[:], ps_at[:], ACT.Copy).then_inc(at_cp.sem, 1)
                    act.wait_ge(av_ps.sem, av_ps.at(i, j + 1))
                    if j == 0:
                        act.wait_ge(c_out.sem, c_out.at(i, 0))
                    for hq in range(HQ):
                        rows = slice(hq * HD, (hq + 1) * HD)
                        last = nc.scalar.activation(
                            cT[rows].rearrange("p c (q b) -> p b c q", q=L)[:, 2 * j:2 * j + 2],
                            ps_av[rows, :, :, hq * L:(hq + 1) * L], ACT.Copy)
                    last.then_inc(av_cp.sem, 1)


def attend_all_phase(nc, a, k):
    MT = [(0, P), (P, P), (2 * P, M - 2 * P)]
    with ExitStack() as ctx:
        m = Mem(nc, ctx, "aa")
        craw, cb = m.sb("craw", [P, KC, M * BG]), m.sb("cb", [P, KC, M])
        Q, Qblk = m.sb("Q", [P, KC, GT]), m.sb("Qb", [P, KC, P])
        KT, V = m.sb("K", [P, KC, M]), m.sb("V", [P, len(MT), D])
        AT, cT = m.sb("AT", [P, len(MT), P]), m.sb("cT", [P, KC, GT])
        Wk, Wv = m.sb("Wk", [P, KC, D]), m.sb("Wv", [P, KC, D])
        bk, bv = m.sb("bk", [P, KC]), m.sb("bv", [P, D])
        ip = Interpolation(m, 1, M, 1, M)
        ps, ps_at, ps_av = m.ps("big", [P, KC, 512]), m.ps("at", [P, len(MT), P]), m.ps("av", [P, 512])

        w_in, c_in, q_in, c_out = m.count("w_in"), m.count("c_in", 16), m.count("q_in", 16), m.count("c_out", 16)
        zero, cb_done, qb_done = m.count("zero"), m.count("cb"), m.count("qb")
        k_ps, k_cp, v_ps, v_cp, s_ps = m.count("kp"), m.count("kc"), m.count("vp"), m.count("vc"), m.count("sp")
        diff, ab, tent = m.count("diff", KC), m.count("ab", KC), m.count("tent", KC)
        sc_done, ex_done, A_done = m.count("sc", KC), m.count("ex", KC), m.count("A", KC)
        at_ps, at_cp, av_ps, av_cp = m.count("atp", KC), m.count("atc", KC), m.count("avp", KC), m.count("avc", KC)
        link, plink = m.count("link", KC * ip.DVE_LINKS), m.count("plink", HQ)
        block = ctx.enter_context(nc.Block())

        @block.sync
        def _(sp):
            sp.dma_start(Wk[:], a["xWk"]).then_inc(w_in.sem, 16)
            sp.dma_start(Wv[:], a["xWv"]).then_inc(w_in.sem, 16)
            sp.dma_start(bk[:], a["xbk"]).then_inc(w_in.sem, 16)
            sp.dma_start(bv[:], a["xbv"].partition_broadcast(P)).then_inc(w_in.sem, 16)
            with sp.Fori(0, NG) as i:
                sp.wait_ge(av_cp.sem, av_cp.at(i * BG, 0))
                sp.dma_start(craw[:], a["ctx"][bass.ds(i, 1)].rearrange("o p c w -> (o p) c w")).then_inc(c_in.sem, 16)
                sp.dma_start(Q[:], a["q_scr"][bass.ds(i, 1)].rearrange("o p k t -> (o p) k t")).then_inc(q_in.sem, 16)
                sp.wait_ge(av_cp.sem, av_cp.at(i * BG + BG, 0))
                sp.dma_start(a["c_scr"][bass.ds(i, 1)].rearrange("o p k t -> (o p) k t"), cT[:]).then_inc(c_out.sem, 16)
            sp.wait_ge(c_out.sem, c_out.at(NG, 0))

        @block.gpsimd
        def _(pool):
            m.start(pool)
            nc.gpsimd.memset(Qblk[:], 0.0).then_inc(zero.sem, 1)
            pool.wait_ge(zero.sem, zero.at(0, 1))
            with pool.Fori(0, NG) as i:
                pool.wait_ge(q_in.sem, q_in.at(i, 16))
                m.settle(pool)
                with pool.Fori(0, PAIRS) as u:
                    for v in range(2):
                        r = i * BG + u * 2 + v
                        pool.wait_ge(s_ps.sem, s_ps.at(r, 0))
                        m.settle(pool)
                        steps = Chain(pool, plink, r, m.settle)
                        for hq in range(HQ):
                            rows = slice(hq * HD, hq * HD + HD)
                            steps.link(nc.gpsimd.tensor_copy(Qblk[rows, :, hq * L:(hq + 1) * L],
                                                             Q[rows, :, bass.ds(u * 2 * L + v * L, L)]))
                        pool.sem_inc(qb_done.sem, 1)
                        for g in range(KC):
                            pool.wait_ge(A_done.sem, A_done.at(r, g))
                            ix = k["ix"][:, bass.ds(i * PAIRS + u, 1), g, v, :].rearrange("p b k -> p (b k)")
                            ip.pool_difference(nc, 0, k["const"][:, CMC:CMC + M], ix).then_inc(diff.sem, 1)
                            pool.wait_ge(diff.sem, diff.at(r, g + 1))

        @block.vector
        def _(dve):
            dve.wait_ge(w_in.sem, w_in.at(0, 64))
            with dve.Fori(0, B) as r:
                chain = Chain(dve, link, r)
                dve.wait_ge(v_ps.sem, v_ps.at(r, 1))
                for t, (_, n) in enumerate(MT):
                    last = nc.vector.tensor_tensor(V[0:n, t, :], ps[0:n, t, :], bv[0:n, :], ALU.add)
                last.then_inc(v_cp.sem, 1)
                for g in range(KC):
                    dve.wait_ge(s_ps.sem, s_ps.at(r, 1))
                    dve.wait_ge(tent.sem, tent.at(r, g + 1))
                    dve.wait_ge(A_done.sem, A_done.at(r, g))
                    ip.dve_scores(nc, chain, 0, ps[:, g:g + 1, 0:M]).then_inc(sc_done.sem, 1)
                    dve.wait_ge(ex_done.sem, ex_done.at(r, g + 1))
                    dve.wait_ge(at_ps.sem, at_ps.at(r, g))
                    ip.dve_weights(nc, chain, 0).then_inc(A_done.sem, 1)
                chain.close()

        @block.tensor
        def _(pe):
            pe.wait_ge(w_in.sem, w_in.at(0, 64))
            with pe.Fori(0, B) as r:
                pe.wait_ge(cb_done.sem, cb_done.at(r, 1))
                pe.wait_ge(sc_done.sem, sc_done.at(r, 0))
                for e in range(KC):
                    for c in range(KC):
                        last = nc.tensor.matmul(ps[:, e, 0:M], Wk[:, c, e * P:(e + 1) * P], cb[:, c, :],
                                                start=(c == 0), stop=(c == KC - 1))
                last.then_inc(k_ps.sem, 1)
                pe.wait_ge(k_cp.sem, k_cp.at(r, 1))
                for t, (at, n) in enumerate(MT):
                    for c in range(KC):
                        last = nc.tensor.matmul(ps[0:n, t, :], cb[:, c, at:at + n], Wv[:, c, :],
                                                start=(c == 0), stop=(c == KC - 1))
                last.then_inc(v_ps.sem, 1)
                pe.wait_ge(v_cp.sem, v_cp.at(r, 1))
                pe.wait_ge(qb_done.sem, qb_done.at(r, 1))
                for g in range(KC):
                    last = nc.tensor.matmul(ps[:, g, 0:M], Qblk[:, g, :], KT[:, g, :], start=True, stop=True)
                last.then_inc(s_ps.sem, 1)
                for g in range(KC):
                    pe.wait_ge(A_done.sem, A_done.at(r, g + 1))
                    pe.wait_ge(at_cp.sem, at_cp.at(r, g))
                    for t, (at, n) in enumerate(MT):
                        last = nc.tensor.transpose(ps_at[0:n, t, :], ip.A[:, 0, at:at + n], k["ident"])
                    last.then_inc(at_ps.sem, 1)
                    pe.wait_ge(at_cp.sem, at_cp.at(r, g + 1))
                    pe.wait_ge(av_cp.sem, av_cp.at(r, g))
                    for t, (_, n) in enumerate(MT):
                        last = nc.tensor.matmul(ps_av[:, 0:P], V[0:n, t, g * P:(g + 1) * P], AT[0:n, t, :],
                                                start=(t == 0), stop=(t == len(MT) - 1))
                    last.then_inc(av_ps.sem, 1)

        @block.scalar
        def _(act):
            act.wait_ge(w_in.sem, w_in.at(0, 64))
            with act.Fori(0, NG) as i:
                act.wait_ge(c_in.sem, c_in.at(i, 16))
                act.wait_ge(c_out.sem, c_out.at(i, 0))
                with act.Fori(0, BG) as b:
                    r = i * BG + b
                    act.wait_ge(v_ps.sem, v_ps.at(r, 0))
                    raw = craw[:].rearrange("p c (m b) -> p c m b", b=BG)[:, :, :, bass.ds(b, 1)]
                    nc.scalar.activation(cb[:].unsqueeze(3), raw, ACT.Copy).then_inc(cb_done.sem, 1)
                    act.wait_ge(k_ps.sem, k_ps.at(r, 1))
                    act.wait_ge(s_ps.sem, s_ps.at(r, 0))
                    for e in range(KC):
                        last = nc.scalar.activation(KT[:, e, :], ps[:, e, 0:M], ACT.Identity, bias=bk[:, e:e + 1])
                    last.then_inc(k_cp.sem, 1)
                    for g in range(KC):
                        act.wait_ge(diff.sem, diff.at(r, g + 1))
                        ip.act_abs(nc, 0).then_inc(ab.sem, 1)
                        act.wait_ge(ab.sem, ab.at(r, g + 1))
                        ip.act_tent(nc, 0).then_inc(tent.sem, 1)
                        act.wait_ge(sc_done.sem, sc_done.at(r, g + 1))
                        ip.act_exp(nc).then_inc(ex_done.sem, 1)
                        act.wait_ge(at_ps.sem, at_ps.at(r, g + 1))
                        act.wait_ge(av_ps.sem, av_ps.at(r, g))
                        nc.scalar.activation(AT[:, 0:2, :], ps_at[:, 0:2, :], ACT.Copy)
                        nc.scalar.activation(AT[0:1, 2, :], ps_at[0:1, 2, :], ACT.Copy).then_inc(at_cp.sem, 1)
                        act.wait_ge(av_ps.sem, av_ps.at(r, g + 1))
                        for hq in range(HQ):
                            rows = slice(hq * HD, (hq + 1) * HD)
                            last = nc.scalar.activation(cT[rows, g, :].rearrange("p (q b) -> p q b", b=BG)[:, :, bass.ds(b, 1)],
                                                        ps_av[rows, hq * L:(hq + 1) * L].unsqueeze(2),
                                                        ACT.Copy)
                        last.then_inc(av_cp.sem, 1)


FRONT = ([("y0", "dve"), ("y1", "dve"), ("t0", "act"), ("t1", "act")]
         + [(f"{n}{e}", "dve") for n in "qkv" for e in range(KC)] + [("lr", "dve")])


def chunk_fills(c):
    return ([(f"sk{c}", "dve"), (f"sq{c}", "dve"), (f"vt{c}", "act")] + [("kt0", "act")] * (c == 0)
            + [(f"khT{c}", "act"), (f"qhT{c}", "act")] + [(f"qk{c}{h}", "dve") for h in range(HQ)]
            + [(f"o{c}", "act")])


LINKS = 1 + LN_LINKS + 3 * KC * 2 + 1 + 2 * 6 + 2 * 4
BACK = (chunk_fills(0) + [("up", "dve")]
        + [(f"{n}{it}", e) for it in range(2) for n, e in
           (("si", "dve"), ("so", "dve"), ("ti", "act"), ("to", "act"), ("gi", "dve"), ("go", "dve"))]
        + [("wo", "act")] + chunk_fills(1) + [("z0", "dve"), ("z1", "dve")])


def fast_phase(nc, a, k):
    S2 = 2 * KC
    with ExitStack() as ctx:
        m = Mem(nc, ctx, "fw")
        front, back = Ring(m, "front", 4, FRONT), Ring(m, "back", 4, BACK)
        cT, xs = m.sb("cT", [P, KC, GT]), m.sb("x", [P, TT, D])
        x1, h, x2 = m.sb("x1", [P, TT, D]), m.sb("h", [P, TT, D]), m.sb("x2", [P, TT, D])
        stats, mv, rstd = m.sb("st", [P, TT, 6]), m.sb("mv", [P, TT, 2]), m.sb("rs", [P, TT])
        hT, hx = m.sb("hT", [P, KC, GT]), m.sb("hx", [P, KC, P])
        f = {n: m.sb(f"{n}T", [P, KC, GT]) for n in "qkv"}
        lr, lrs, lrf = m.sb("lr", [P, 3, 2 * H]), m.sb("lrs", [P, 3, 2 * H]), m.sb("lrf", [P, KC, 2])
        vt, kt = m.sb("vt", [P, KC, P]), m.sb("kt", [P, KC, P])
        e, top, tot = m.sb("e", [P, 2, 512]), m.sb("top", [P, 2, P]), m.sb("tot", [P, 2, P])
        kh, qh = e[:, 0, :], e[:, 1, :]
        khT, qhT = m.sb("khT", [P, KC, P]), m.sb("qhT", [P, KC, P])
        qk = m.sb("qk", [P, HQ, KC, P])
        oT = m.sb("oT", [P, KC, GT])
        win0, wout0, wrow0 = m.sb("win0", [P, KC, P]), m.sb("wout0", [P, KC, P]), m.sb("wrow0", [P, KC, P])
        win, wout, wrow = m.sb("win", [P, KC, P]), m.sb("wout", [P, KC, P]), m.sb("wrow", [P, KC, P])
        grad = m.sb("grad", [P, 2, 512])
        at, atT = m.sb("at", [P, 2, KC, P]), m.sb("atT", [P, 2, KC, P])
        atop, asum = m.sb("atop", [P, S2]), m.sb("asum", [P, S2])
        Wo, Wp = m.sb("Wo", [P, KC, D]), {n: m.sb(f"W{n}", [P, KC, D]) for n in "qkv"}
        Wo2, Wlr = m.sb("Wo2", [P, KC, D]), m.sb("Wlr", [P, KC, 2 * H])
        bo, conv = m.sb("bo", [P, D]), m.sb("conv", [P, 3, KC, 4])
        wi, wr, wsum = m.sb("wi", [P, KC, DI]), m.sb("wr", [P, KC, HD]), m.sb("wsum", [P, 3, KC])
        wt = m.sb("wt", [P, KC, DI])
        const = k["const"]
        neg, own = const[:, CNEG:CNEG + P], const[:, CBM:CBM + BG]
        head, causal = const[:, CHM:CHM + P], const[:, CCA:CCA + P]

        w_in, c_in, x_in, x_out = m.count("w_in"), m.count("c_in", 16), m.count("x_in", 16), m.count("x_out", 16)
        setup = m.count("setup")
        x1_done, h_done, var, std = m.count("x1"), m.count("h"), m.count("var"), m.count("std")
        hT_done, hx_done = m.count("hT"), m.count("hx")
        base_done, conv_done = m.count("base", 3 * KC), m.count("conv", 3 * KC)
        z_done, za, ze, zp, zl, lr_done = (m.count(n) for n in ("z", "za", "ze", "zp", "zl", "lrd"))
        d_done, e_done, p_done = m.count("d", 2), m.count("e", 2), m.count("p", 2)
        qk_done = m.count("qkd", 2)
        s_done, a_done, n_done, w_done = m.count("s", 2), m.count("a", 2), m.count("n", 2), m.count("w", 3)
        x2_done = m.count("x2")
        link, slink = m.count("link", LINKS), m.count("slink", 3)
        block = ctx.enter_context(nc.Block())

        @block.sync
        def _(sp):
            loads = [(Wo, "xWo"), (Wp["q"], "aWq"), (Wp["k"], "aWk"), (Wp["v"], "aWv"), (Wo2, "aWo"), (Wlr, "aWlr"),
                     (conv, "conv"), (wi, "aWin"), (wt, "aWout"), (wr, "aWout_rows")]
            for dst, name in loads:
                sp.dma_start(dst[:], a[name]).then_inc(w_in.sem, 16)
            sp.dma_start(bo[:], a["xbo"].partition_broadcast(P)).then_inc(w_in.sem, 16)
            with sp.Fori(0, NG) as i:
                sp.wait_ge(x1_done.sem, x1_done.at(i, 0))
                sp.dma_start(cT[:], a["c_scr"][bass.ds(i, 1)].rearrange("o p k t -> (o p) k t")).then_inc(c_in.sem, 16)
                sp.dma_start(xs[:], a["x_lb"][bass.ds(i, 1)].rearrange("o p t d -> (o p) t d")).then_inc(x_in.sem, 16)
                sp.wait_ge(x2_done.sem, x2_done.at(i, 1))
                sp.dma_start(a["x2_scr"][bass.ds(i, 1)].rearrange("o p t d -> (o p) t d"), x2[:]).then_inc(x_out.sem, 16)
            sp.wait_ge(x_out.sem, x_out.at(NG, 0))

        @block.gpsimd
        def _(pool):
            m.start(pool)
            with pool.Fori(0, NG) as i:
                pool.wait_ge(hT_done.sem, hT_done.at(i, 1))
                pool.wait_ge(*front.full(i, "y0"))
                m.settle(pool)
                for c in range(KC):
                    src = bc(bc(hT[:, c, 0:BG], 1, HQ), 3, DI)
                    last = nc.gpsimd.tensor_copy(hx[:, c, :].rearrange("p (h b d) -> p h b d", h=HQ, b=BG), src)
                last.then_inc(hx_done.sem, 1)

        @block.vector
        def _(dve):
            dve.wait_ge(w_in.sem, w_in.at(0, 11 * 16))
            st = Chain(dve, slink, 0)
            for w in (win0, wout0, wrow0):
                last = nc.vector.memset(w[:], 0.0)
            st.link(last)
            for hq in range(HQ):
                rows, cols = slice(hq * HD, (hq + 1) * HD), slice(hq * HD, (hq + 1) * HD)
                for dst, src in ((win0, wi), (wout0, wt)):
                    nc.vector.tensor_copy(dst[rows, :, cols].rearrange("p g (b d) -> p g b d", b=BG), bc(src[rows], 2, BG))
                last = nc.vector.tensor_copy(wrow0[rows, :, cols], wr[rows])
            st.link(last)
            st.link(nc.vector.tensor_scalar_add(wsum[:], conv[:, :, :, 3], 1.0))
            nc.vector.memset(top[:], 0.0).then_inc(setup.sem, 1)

            def enter(i, ch):
                dve.wait_ge(x_in.sem, x_in.at(i, 16))
                for t in range(TT):
                    dve.wait_ge(*front.full(i, f"y{t}"))
                    last = nc.vector.tensor_tensor(x1[:, t, :], front.bank(f"y{t}"), xs[:, t, :], ALU.add)
                    last.then_inc(front.read["dve"].sem, 1)
                dve.wait_ge(*front.used(i, "y1"))
                ch.link(nc.vector.tensor_tensor(x1[:], x1[:], bc(bo[:], 1, TT), ALU.add))
                dve.sem_inc(x1_done.sem, 1)
                layer_norm(nc, m, ch, x1, h, stats, mv, rstd, var, std, TT).then_inc(h_done.sem, 1)

            def convolve(i, ch):
                for n, name in enumerate("qkv"):
                    for b in range(KC):
                        fill, y = f"{name}{b}", f[name][:, b, :]
                        dve.wait_ge(base_done.sem, base_done.at(i, n * KC + b + 1))
                        for s_ in (1, 2, 3):
                            last = nc.vector.scalar_tensor_tensor(
                                y[:, s_ * BG:], front.bank(fill)[:, 0:GT - s_ * BG], conv[:, n, b, 3 - s_:4 - s_],
                                y[:, s_ * BG:], ALU.mult, ALU.add)
                            if s_ < 3:
                                ch.link(last)
                        last.then_inc(front.read["dve"].sem, 1)
                dve.wait_ge(*front.used(i, "v3"))
                dve.sem_inc(conv_done.sem, 3 * KC)

            def rates(i, ch):
                dve.wait_ge(*front.full(i, "lr"))
                nc.vector.tensor_scalar(lr[:], front.bank("lr")[:, 0:6 * H].rearrange("p (c n) -> p c n", c=3), 0.001, None,
                                        ALU.add).then_inc(z_done.sem, 1)
                dve.wait_ge(ze.sem, ze.at(i, 1))
                nc.vector.tensor_scalar_add(lrs[:], lrs[:], 1.0).then_inc(zp.sem, 1)
                dve.wait_ge(zl.sem, zl.at(i, 1))
                ch.link(nc.vector.scalar_tensor_tensor(lrs[:], lr[:], 0.0, lrs[:], ALU.max, ALU.add))
                for hq in range(HQ):
                    rows = slice(hq * HD, (hq + 1) * HD)
                    src = lrs[rows, 2, :].rearrange("p (g h j) -> p g h j", g=KC, h=HQ)[:, :, hq, :]
                    last = nc.vector.tensor_copy(lrf[rows], src)
                last.then_inc(lr_done.sem, 1)
                dve.wait_ge(lr_done.sem, lr_done.at(i, 1))
                dve.sem_inc(front.read["dve"].sem, 1)

            def chunk(i, ch, c):
                for j, n in enumerate((f"sk{c}", f"sq{c}")):
                    dve.wait_ge(*back.full(i, n))
                    s = back.bank(n).rearrange("p (n d) -> p n d", d=DI)
                    ch.link(nc.vector.tensor_reduce(top[:, j, :], s, AX, ALU.max))
                    nc.vector.tensor_tensor(e[:, j, :].rearrange("p (n d) -> p n d", d=DI), s, bc(top[:, j, :], 2, DI),
                                            ALU.subtract).then_inc(back.read["dve"].sem, 1)
                dve.wait_ge(*back.used(i, f"sq{c}"))
                dve.sem_inc(d_done.sem, 1)
                dve.wait_ge(e_done.sem, e_done.at(i, c + 1))
                rows = e[:].rearrange("p j (n d) -> p (j n) d", d=DI)
                flat = tot[:].rearrange("p j n -> p (j n)")
                ch.link(nc.vector.tensor_reduce(flat, rows, AX, ALU.add))
                ch.link(nc.vector.reciprocal(flat, flat))
                by = tot[:].rearrange("p j (h b) -> p (j h) b", b=BG)
                ch.link(nc.vector.tensor_tensor(by, by, bc(own, 1, 2 * H), ALU.mult))
                rate = lrs[:, c, :].rearrange("p (h j) -> p h j", j=2)[:, :, 1]
                k_by = tot[:, 0, :].rearrange("p (h b) -> p h b", b=BG)
                ch.link(nc.vector.tensor_tensor(k_by, k_by, bc(rate, 2, BG), ALU.mult))
                nc.vector.tensor_tensor(rows, rows, bc(flat, 2, DI), ALU.mult).then_inc(p_done.sem, 1)

            def causal_products(i, c):
                for h_ in range(HQ):
                    n = f"qk{c}{h_}"
                    dve.wait_ge(*back.full(i, n))
                    nc.vector.tensor_tensor(qk[:, h_], back.bank(n, KC), bc(causal, 1, KC),
                                            ALU.mult).then_inc(back.read["dve"].sem, 1)
                dve.wait_ge(*back.used(i, f"qk{c}{HQ - 1}"))
                dve.sem_inc(qk_done.sem, 1)

            def add_own_heads(i, ch, fill, j, old, new):
                dve.wait_ge(*back.full(i, fill))
                g4 = grad[:, j, :].rearrange("p (g n) -> p g n", g=KC)
                nc.vector.tensor_tensor(g4, back.bank(fill, KC), bc(head, 1, KC), ALU.mult).then_inc(back.read["dve"].sem, 1)
                dve.wait_ge(*back.used(i, fill))
                return nc.vector.tensor_tensor(new[:], old[:], g4, ALU.add)

            def attention(i, ch, it):
                for j, n in enumerate((f"si{it}", f"so{it}")):
                    dve.wait_ge(*back.full(i, n))
                    nc.vector.tensor_tensor(at[:, j], back.bank(n, KC), bc(neg, 1, KC), ALU.add).then_inc(back.read["dve"].sem, 1)
                dve.wait_ge(*back.used(i, f"so{it}"))
                ch.link(nc.vector.tensor_reduce(atop[:], at[:].rearrange("p j g n -> p (j g) n"), AX, ALU.max))
                nc.vector.tensor_scalar(atop[:], atop[:], -ATT_SCALE, None, ALU.mult).then_inc(s_done.sem, 1)
                dve.wait_ge(a_done.sem, a_done.at(i, it + 1))
                ch.link(nc.vector.reciprocal(asum[:], asum[:]))
                for j in range(2):
                    part = asum[:, j * KC:(j + 1) * KC]
                    last = nc.vector.tensor_tensor(part, part, lrf[:, :, 1 - j], ALU.mult)
                ch.link(last)
                by = at[:].rearrange("p j g n -> p (j g) n")
                nc.vector.tensor_tensor(by, by, bc(asum[:], 2, P), ALU.mult).then_inc(n_done.sem, 1)
                o = (wout, wout)
                ch.link(add_own_heads(i, ch, f"gi{it}", 0, *o))
                last = add_own_heads(i, ch, f"go{it}", 1, win0 if it == 0 else win, win)
                last.then_inc(w_done.sem, 1)

            def leave(i):
                dve.wait_ge(x_out.sem, x_out.at(i, 0))
                for t in range(TT):
                    dve.wait_ge(*back.full(i, f"z{t}"))
                    nc.vector.tensor_tensor(x2[:, t, :], back.bank(f"z{t}"), x1[:, t, :], ALU.add).then_inc(back.read["dve"].sem, 1)
                dve.wait_ge(*back.used(i, "z1"))
                dve.sem_inc(x2_done.sem, 1)

            with dve.Fori(0, NG) as i:
                ch = Chain(dve, link, i)
                enter(i, ch)
                convolve(i, ch)
                rates(i, ch)
                chunk(i, ch, 0)
                causal_products(i, 0)
                add_own_heads(i, ch, "up", 0, wout0, wout).then_inc(w_done.sem, 1)
                attention(i, ch, 0)
                attention(i, ch, 1)
                chunk(i, ch, 1)
                causal_products(i, 1)
                leave(i)
                ch.close()

        @block.tensor
        def _(pe):
            pe.wait_ge(w_in.sem, w_in.at(0, 11 * 16))
            pe.wait_ge(setup.sem, setup.at(0, 1))

            def blocks(i, ring, fill, parts, pairs):
                pe.wait_ge(*ring.free(i, fill))
                out = ring.bank(fill, parts)
                for g, (lhsT, rhs) in enumerate(pairs):
                    last = nc.tensor.matmul(out[:, g, :], lhsT, rhs, start=True, stop=True)
                last.then_inc(ring.filled.sem, 1)

            def transposes(i, ring, fill, parts):
                pe.wait_ge(*ring.free(i, fill))
                out = ring.bank(fill, len(parts))
                for g, x in enumerate(parts):
                    last = nc.tensor.transpose(out[:, g, :], x, k["ident"])
                last.then_inc(ring.filled.sem, 1)

            def deep(i, ring, fill, n, lhsT, rhs):
                pe.wait_ge(*ring.free(i, fill))
                for c in range(KC):
                    last = nc.tensor.matmul(ring.bank(fill)[:, 0:n], lhsT(c), rhs(c), start=(c == 0), stop=(c == KC - 1))
                last.then_inc(ring.filled.sem, 1)

            def enter(i):
                pe.wait_ge(c_in.sem, c_in.at(i, 16))
                for t in range(TT):
                    deep(i, front, f"y{t}", D, lambda c: cT[:, c, t * P:(t + 1) * P], lambda c: Wo[:, c, :])
                pe.wait_ge(h_done.sem, h_done.at(i, 1))
                for t in range(TT):
                    transposes(i, front, f"t{t}", [h[:, t, c * P:(c + 1) * P] for c in range(KC)])
                pe.wait_ge(hT_done.sem, hT_done.at(i, 1))
                for n in "qkv":
                    for e_ in range(KC):
                        deep(i, front, f"{n}{e_}", GT, lambda c: Wp[n][:, c, e_ * P:(e_ + 1) * P], lambda c: hT[:, c, :])
                pe.wait_ge(*front.free(i, "lr"))
                pe.wait_ge(hx_done.sem, hx_done.at(i, 1))
                for j in range(3):
                    for c in range(KC):
                        tokens = hx[:, c, :] if j == 2 else hT[:, c, j * P:(j + 1) * P]
                        last = nc.tensor.matmul(front.bank("lr")[:, j * 2 * H:(j + 1) * 2 * H], tokens, Wlr[:, c, :],
                                                start=(c == 0), stop=(c == KC - 1))
                last.then_inc(front.filled.sem, 1)

            def chunk(i, c):
                tok = slice(c * P, (c + 1) * P)
                w_in_, w_row = (win0, wrow0) if c == 0 else (win, wrow)
                if c == 0:
                    pe.wait_ge(conv_done.sem, conv_done.at(i, 3 * KC))
                blocks(i, back, f"sk{c}", KC, [(f["k"][:, g, tok], w_in_[:, g, :]) for g in range(KC)])
                blocks(i, back, f"sq{c}", KC, [(f["q"][:, g, tok], w_in_[:, g, :]) for g in range(KC)])
                transposes(i, back, f"vt{c}", [f["v"][:, g, tok] for g in range(KC)])
                if c == 0:
                    transposes(i, back, "kt0", [f["k"][:, g, tok] for g in range(KC)])
                pe.wait_ge(p_done.sem, p_done.at(i, c + 1))
                transposes(i, back, f"khT{c}", [kh[:, g * P:(g + 1) * P] for g in range(KC)])
                transposes(i, back, f"qhT{c}", [qh[:, g * P:(g + 1) * P] for g in range(KC)])
                pe.wait_ge(*back.used(i, f"qhT{c}"))
                for h_ in range(HQ):
                    r = slice(h_ * HD, (h_ + 1) * HD)
                    blocks(i, back, f"qk{c}{h_}", KC, [(khT[r, g, :], qhT[r, g, :]) for g in range(KC)])
                pe.wait_ge(*back.free(i, f"o{c}"))
                pe.wait_ge(qk_done.sem, qk_done.at(i, c + 1))
                if c == 1:
                    pe.wait_ge(*back.used(i, "wo"))
                out = back.bank(f"o{c}", KC)
                for g in range(KC):
                    nc.tensor.matmul(out[:, g, :], w_row[:, g, :], qhT[:, g, :], start=True, stop=False)
                    for h_ in range(HQ):
                        r = slice(h_ * HD, (h_ + 1) * HD)
                        last = nc.tensor.matmul(out[r, g, :], vt[:, g, r], qk[:, h_, g, :], start=False, stop=True)
                last.then_inc(back.filled.sem, 1)

            def iteration(i, it):
                tok = slice(0, P)
                w = win0 if it == 0 else win
                blocks(i, back, f"si{it}", KC, [(w[:, g, :], f["k"][:, g, tok]) for g in range(KC)])
                pe.wait_ge(w_done.sem, w_done.at(i, it + 1))
                blocks(i, back, f"so{it}", KC, [(wout[:, g, :], f["v"][:, g, tok]) for g in range(KC)])
                pe.wait_ge(n_done.sem, n_done.at(i, it + 1))
                transposes(i, back, f"ti{it}", [at[:, 0, g, :] for g in range(KC)])
                transposes(i, back, f"to{it}", [at[:, 1, g, :] for g in range(KC)])
                pe.wait_ge(*back.used(i, f"ti{it}"))
                blocks(i, back, f"gi{it}", KC, [(vt[:, g, :], atT[:, 0, g, :]) for g in range(KC)])
                pe.wait_ge(*back.used(i, f"to{it}"))
                blocks(i, back, f"go{it}", KC, [(kt[:, g, :], atT[:, 1, g, :]) for g in range(KC)])

            with pe.Fori(0, NG) as i:
                enter(i)
                chunk(i, 0)
                blocks(i, back, "up", KC, [(vt[:, g, :], kh[:, g * P:(g + 1) * P]) for g in range(KC)])
                iteration(i, 0)
                pe.wait_ge(w_done.sem, w_done.at(i, 2))
                iteration(i, 1)
                pe.wait_ge(w_done.sem, w_done.at(i, 3))
                transposes(i, back, "wo", [wout[:, g, :] for g in range(KC)])
                chunk(i, 1)
                pe.wait_ge(*back.used(i, "o1"))
                for t in range(TT):
                    deep(i, back, f"z{t}", D, lambda c: oT[:, c, t * P:(t + 1) * P], lambda c: Wo2[:, c, :])

        @block.scalar
        def _(act):
            act.wait_ge(setup.sem, setup.at(0, 1))

            def take(i, fill, dst, parts=KC):
                act.wait_ge(*back.full(i, fill))
                nc.scalar.activation(dst, back.bank(fill, parts), ACT.Copy).then_inc(back.read["act"].sem, 1)

            def enter(i):
                act_deviation(nc, act, i, mv, rstd[:], var, std)
                for t in range(TT):
                    act.wait_ge(*front.full(i, f"t{t}"))
                    nc.scalar.activation(hT[:, :, t * P:(t + 1) * P], front.bank(f"t{t}", KC), ACT.Copy).then_inc(front.read["act"].sem, 1)
                act.wait_ge(*front.used(i, "t1"))
                act.sem_inc(hT_done.sem, 1)
                for n, name in enumerate("qkv"):
                    for b in range(KC):
                        act.wait_ge(*front.full(i, f"{name}{b}"))
                        nc.scalar.activation(f[name][:, b, :], front.bank(f"{name}{b}")[:, 0:GT], ACT.Copy,
                                             scale=wsum[:, n, b:b + 1]).then_inc(base_done.sem, 1)
                act.wait_ge(z_done.sem, z_done.at(i, 1))
                nc.scalar.activation(lrs[:], lr[:], ACT.Abs).then_inc(za.sem, 1)
                act.wait_ge(za.sem, za.at(i, 1))
                nc.scalar.activation(lrs[:], lrs[:], ACT.Exp, scale=-1.0).then_inc(ze.sem, 1)
                act.wait_ge(zp.sem, zp.at(i, 1))
                nc.scalar.activation(lrs[:], lrs[:], ACT.Ln).then_inc(zl.sem, 1)

            def chunk(i, c):
                take(i, f"vt{c}", vt[:])
                if c == 0:
                    take(i, "kt0", kt[:])
                act.wait_ge(d_done.sem, d_done.at(i, c + 1))
                nc.scalar.activation(e[:], e[:], ACT.Exp).then_inc(e_done.sem, 1)
                take(i, f"khT{c}", khT[:])
                take(i, f"qhT{c}", qhT[:])
                take(i, f"o{c}", oT[:, :, c * P:(c + 1) * P])

            with act.Fori(0, NG) as i:
                enter(i)
                chunk(i, 0)
                for it in range(2):
                    act.wait_ge(s_done.sem, s_done.at(i, it + 1))
                    for n in range(S2):
                        last = nc.scalar.activation(at[:, n // KC, n % KC, :], at[:, n // KC, n % KC, :], ACT.Exp,
                                                    bias=atop[:, n:n + 1], scale=ATT_SCALE, accum_out=asum[:, n:n + 1])
                    last.then_inc(a_done.sem, 1)
                    take(i, f"ti{it}", atT[:, 0])
                    take(i, f"to{it}", atT[:, 1])
                take(i, "wo", wrow[:])
                chunk(i, 1)


def experts_phase(nc, a, k):
    with ExitStack() as ctx:
        m = Mem(nc, ctx, "ex")
        fills = [(f"{n}{t}", r) for t in range(TT) for n, r in
                 [("t", "act"), ("g", "dve")] + [(f"y{e}_", "dve") for e in range(E)]]
        ring = Ring(m, "ring", 8, fills)
        x2, h, acc = m.sb("x", [P, TT, D]), m.sb("h", [P, TT, D]), m.sb("acc", [P, TT, D])
        stats, mv, rstd = m.sb("st", [P, TT, 6]), m.sb("mv", [P, TT, 2]), m.sb("rs", [P, TT])
        hT = m.sb("hT", [P, TT, KC, P])
        We, Wg = m.sb("We", [P, E, KC, D]), m.sb("Wg", [P, KC, E])
        sc, pick, best = m.sb("sc", [P, E]), m.sb("pick", [P, TT, E]), m.sb("best", [P, 2])
        order = k["const"][:, CORD:CORD + E]
        w_in, x_in, x_out = m.count("w_in"), m.count("x_in", 16), m.count("x_out", 16)
        h_done, var, std = m.count("h"), m.count("var"), m.count("std")
        x_done, o_done = m.count("x"), m.count("o")
        link = m.count("link", LN_LINKS + TT * 4 + 1)
        block = ctx.enter_context(nc.Block())

        @block.sync
        def _(sp):
            sp.dma_start(Wg[:], a["gate"]).then_inc(w_in.sem, 16)
            sp.dma_start(We[:], a["expert"].rearrange("e p c d -> p e c d")).then_inc(w_in.sem, 16)
            with sp.Fori(0, NG) as i:
                sp.wait_ge(x_done.sem, x_done.at(i, 0))
                sp.dma_start(x2[:], a["x2_scr"][bass.ds(i, 1)].rearrange("o p t d -> (o p) t d")).then_inc(x_in.sem, 16)
                sp.wait_ge(o_done.sem, o_done.at(i, 1))
                sp.dma_start(a["out"][bass.ds(i, 1)].rearrange("o p t d -> (o p) t d"), acc[:]).then_inc(x_out.sem, 16)
            sp.wait_ge(x_out.sem, x_out.at(NG, 0))

        @block.gpsimd
        def _(pool):
            m.start(pool)

        @block.vector
        def _(dve):
            with dve.Fori(0, NG) as i:
                ch = Chain(dve, link, i)
                dve.wait_ge(x_in.sem, x_in.at(i, 16))
                layer_norm(nc, m, ch, x2, h, stats, mv, rstd, var, std, TT).then_inc(h_done.sem, 1)
                dve.wait_ge(h_done.sem, h_done.at(i, 1))
                dve.wait_ge(x_out.sem, x_out.at(i, 0))
                ch.link(nc.vector.tensor_tensor(acc[:], x2[:], h[:], ALU.add))
                dve.sem_inc(x_done.sem, 1)
                for t in range(TT):
                    dve.wait_ge(*ring.full(i, f"g{t}"))
                    s = ring.bank(f"g{t}")[:, 0:E]
                    ch.link(nc.vector.tensor_reduce(best[:, 0:1], s, AX, ALU.max))
                    nc.vector.tensor_scalar(sc[:], s, best[:, 0:1], None, ALU.is_ge).then_inc(ring.read["dve"].sem, 1)
                    dve.wait_ge(*ring.used(i, f"g{t}"))
                    ch.link(nc.vector.tensor_tensor(sc[:], sc[:], order, ALU.mult))
                    ch.link(nc.vector.tensor_reduce(best[:, 1:2], sc[:], AX, ALU.max))
                    ch.link(nc.vector.tensor_scalar(pick[:, t, :], sc[:], best[:, 1:2], None, ALU.is_equal))
                    for e in range(E):
                        dve.wait_ge(*ring.full(i, f"y{e}_{t}"))
                        nc.vector.scalar_tensor_tensor(acc[:, t, :], ring.bank(f"y{e}_{t}"), pick[:, t, e:e + 1], acc[:, t, :],
                                                       ALU.mult, ALU.add).then_inc(ring.read["dve"].sem, 1)
                        dve.wait_ge(*ring.used(i, f"y{e}_{t}"))
                dve.sem_inc(o_done.sem, 1)
                ch.close()

        @block.tensor
        def _(pe):
            pe.wait_ge(w_in.sem, w_in.at(0, 2 * 16))
            with pe.Fori(0, NG) as i:
                pe.wait_ge(h_done.sem, h_done.at(i, 1))
                for t in range(TT):
                    pe.wait_ge(*ring.free(i, f"t{t}"))
                    for c in range(KC):
                        last = nc.tensor.transpose(ring.bank(f"t{t}", KC)[:, c, :], h[:, t, c * P:(c + 1) * P], k["ident"])
                    last.then_inc(ring.filled.sem, 1)
                    pe.wait_ge(*ring.used(i, f"t{t}"))
                    pe.wait_ge(*ring.free(i, f"g{t}"))
                    for c in range(KC):
                        last = nc.tensor.matmul(ring.bank(f"g{t}")[:, 0:E], hT[:, t, c, :], Wg[:, c, :], start=(c == 0), stop=(c == KC - 1))
                    last.then_inc(ring.filled.sem, 1)
                    for e in range(E):
                        pe.wait_ge(*ring.free(i, f"y{e}_{t}"))
                        for c in range(KC):
                            last = nc.tensor.matmul(ring.bank(f"y{e}_{t}"), hT[:, t, c, :], We[:, e, c, :], start=(c == 0), stop=(c == KC - 1))
                        last.then_inc(ring.filled.sem, 1)

        @block.scalar
        def _(act):
            with act.Fori(0, NG) as i:
                act_deviation(nc, act, i, mv, rstd[:], var, std)
                for t in range(TT):
                    act.wait_ge(*ring.full(i, f"t{t}"))
                    nc.scalar.activation(hT[:, t], ring.bank(f"t{t}", KC), ACT.Copy).then_inc(ring.read["act"].sem, 1)


def layer(nc, a, upto=9, force_all=False):
    with ExitStack() as ctx:
        m = Mem(nc, ctx, "all")
        k = {"const": m.sb("const", [P, CN]), "ix": m.sb("ix", [P, B // 2, KC, 2, NK])[:]}
        k["flag"] = m.sb("flag", [1, 1], I32)[:]
        k["ident"] = k["const"][:, CI:CI + P]
        k["ones"] = k["const"][:, CONE:CONE + 1]
        project_phase(nc, a, k)
        outside = nc.values_load(k["flag"], min_val=0, max_val=P)
        with nc.If(outside < 1 if not force_all else outside > 1000):
            attend_window_phase(nc, a, k)
        with nc.Else():
            attend_all_phase(nc, a, k)
        if upto > 1:
            fast_phase(nc, a, k)
            experts_phase(nc, a, k)


def feature_blocks(w):
    return np.ascontiguousarray(w.reshape(KC, P, -1).transpose(1, 0, 2))


def layouts(v):
    out = {
        "x_tok": v["x"].reshape(NG, TT, P, D),
        "x_lb": v["x"].reshape(NG, BG, TT, C, D).transpose(0, 3, 1, 2, 4).reshape(NG, P, TT, D),
        "ctx": np.roll(v["ctx_1024"], TAIL, axis=1).reshape(NG, BG, M, KC, P).transpose(0, 4, 3, 2, 1).reshape(NG, P, KC, M * BG),
        "mask": v["mask_BxS2_if0"],
        "const": shape_constants(),
        "xWoff": feature_blocks(v["L0_xattn_Woff"].T), "xboff": v["L0_xattn_boff"],
        "xbo": v["L0_xattn_bo"], "xbv": v["L0_xattn_bv"],
    }
    for n in ("Wq", "Wk", "Wv", "Wo"):
        out["x" + n] = feature_blocks(v["L0_xattn_" + n].T)
        out["a" + n] = feature_blocks(v["L0_attn_" + n])
    for n in ("bq", "bk"):
        out["x" + n] = v["L0_xattn_" + n].reshape(KC, P).T
    out["aWlr"] = feature_blocks(v["L0_attn_Wlr"])
    out["conv"] = np.stack([v["L0_attn_conv_" + n].reshape(KC, P, 4) for n in "qkv"]).transpose(2, 0, 1, 3)
    for n in ("in", "out"):
        w = v[f"L0_attn_W_{n}_init"][0].reshape(DI, KC, HQ, HD)
        out["aW" + n] = w.transpose(2, 3, 1, 0).reshape(P, KC, DI)
    out["aWout_rows"] = np.repeat(v["L0_attn_W_out_init"][0].reshape(DI, KC, HQ, 1, HD).transpose(2, 3, 0, 1, 4), BG,
                                  axis=1).reshape(P, KC, HD)
    out["gate"] = feature_blocks(v["L0_ffn_gate_w"].T)
    out["expert"] = v["L0_ffn_expert_w"].transpose(0, 2, 1).reshape(E, KC, P, D).transpose(0, 2, 1, 3)
    return {n: np.ascontiguousarray(w) for n, w in out.items()}


SCRATCH = {"q_scr": (NG, P, KC, GT), "c_scr": (NG, P, KC, GT), "x2_scr": (NG, P, TT, D)}


def kernel(**inputs):
    import concourse.bacc as bacc
    from concourse.bass_utils import run_bass_kernel_spmd

    nc = bacc.Bacc("TRN2", target_bir_lowering=False, num_devices=1)
    arrays = layouts({n: np.asarray(w) for n, w in inputs.items()})
    a = {n: nc.dram_tensor(n, w.shape, mybir.dt.from_np(w.dtype), kind="ExternalInput").ap() for n, w in arrays.items()}
    for n, shape in SCRATCH.items():
        a[n] = nc.dram_tensor(n, shape, F32).ap()
    a["out"] = nc.dram_tensor("out", (NG, P, TT, D), F32, kind="ExternalOutput").ap()
    layer(nc, a)
    r = run_bass_kernel_spmd(nc, [arrays], core_ids=[0])
    return r.results[0]["out"].reshape(NG, C, BG, TT, D).transpose(0, 2, 3, 1, 4).reshape(B, L, D)
```

```python
from contextlib import ExitStack

import numpy as np

import concourse.bass as bass
from concourse import mybir

F32 = mybir.dt.float32
I32 = mybir.dt.int32
ALU = mybir.AluOpType
ACT = mybir.ActivationFunctionType
AX = mybir.AxisListType.X

P = 128
B, L, D = 64, 32, 512
M = 257
H, HD = 16, 32
NK = 5
KC = D // P
HQ = P // HD
BG = 8
NG = B // BG
GT = BG * L
TT = GT // P
C = 16
DI = 4
E = 8
TAIL, HEAD = 8, 36
W = TAIL + HEAD
PAIRS = BG // 2
EPS = 1e-5
NEG = -1e30
ATT_SCALE = float(HD) ** -0.5
MAGIC = 12582912.0

CI, CNEG, CBM, CHM, CCA, CMC = 0, P, 2 * P, 3 * P, 4 * P, 5 * P
CREF = CMC + M
CQ = CREF + 2 * NK
CONE = CQ + 1
CORD = CONE + 1
CN = CORD + E


def shape_constants():
    c = np.zeros((P, CN), np.float32)
    p = np.arange(P)
    c[:, CI:CI + P] = np.eye(P)
    row_b, row_h = (p // DI) % BG, p // HD
    tok_t, tok_b = p // BG, p % BG
    same = row_b[:, None] == tok_b[None, :]
    c[:, CNEG:CNEG + P] = np.where(same, 0.0, NEG)
    c[:, CBM:CBM + BG] = tok_b[:, None] == np.arange(BG)[None, :]
    c[:, CHM:CHM + P] = (p // HD)[:, None] == row_h[None, :]
    c[:, CCA:CCA + P] = (tok_b[:, None] == tok_b[None, :]) & (tok_t[:, None] <= tok_t[None, :])
    c[:, CMC:CMC + M] = ((np.arange(M) - TAIL) % M)[None, :]
    left = -NK // 2
    c[:, CREF:CREF + 2 * NK] = np.tile(np.arange(left, NK + left), 2)[None, :]
    c[:, CQ] = p % L
    c[:, CONE] = 1.0
    c[:, CORD:CORD + E] = np.arange(E, 0, -1)[None, :]
    return c


class Count:

    def __init__(self, sem, per=1):
        self.sem, self.per = sem, per
        self.base = 32 if per == 16 else per + 1

    def at(self, i, j):
        return i * self.per + j + self.base


class Round:

    def __init__(self, i, p):
        self.i, self.p, self.r = i, p, 2 * i + p

    def next(self):
        return Round(self.i + self.p, 1 - self.p)


def rounds(eng, n, emit):
    with eng.Fori(0, n // 2 - 1) as i:
        emit(Round(i, 0), False)
        emit(Round(i, 1), False)
    emit(Round(n // 2 - 1, 0), False)
    emit(Round(n // 2 - 1, 1), True)


class Chain:

    def __init__(self, eng, count, i, settle=None):
        self.eng, self.count, self.i, self.n, self.settle = eng, count, i, 0, settle

    def link(self, instruction):
        self.n += 1
        instruction.then_inc(self.count.sem, 1)
        self.eng.wait_ge(self.count.sem, self.count.at(self.i, self.n))
        if self.settle:
            self.settle(self.eng)

    def close(self):
        assert self.n == self.count.per, (self.n, self.count.per)


def bc(ap, axis, n):
    shape = list(ap.shape)
    return ap.unsqueeze(axis).broadcast_to(shape[:axis] + [n] + shape[axis:])


def act_deviation(nc, act, i, mv, rstd, var, std):
    act.wait_ge(var.sem, var.at(i, 1))
    nc.scalar.activation(rstd, mv[:, :, 1], ACT.Sqrt, bias=EPS).then_inc(std.sem, 1)


def layer_norm(nc, m, chain, x, h, stats, mv, rstd, var, std, tiles):
    for t in range(tiles):
        chain.link(nc.vector.bn_stats(stats[:, t, :], x[:, t, :]))
    m.settle(chain.eng)
    for t in range(tiles):
        last = nc.vector.bn_aggr(mv[:, t, :], stats[:, t, :])
    last.then_inc(var.sem, 1)
    chain.eng.wait_ge(std.sem, std.at(chain.i, 1))
    chain.link(nc.vector.reciprocal(rstd[:, 0:tiles], rstd[:, 0:tiles]))
    last = None
    for t in range(tiles):
        last = nc.vector.tensor_scalar(h[:, t, :], x[:, t, :], mv[:, t, 0:1], rstd[:, t:t + 1],
                                       ALU.subtract, ALU.mult)
    return last


LN_LINKS = TT + 1


class Ring:

    def __init__(self, m, name, banks, plan):
        self.ps = m.ps(name, [P, banks, 512])
        self.names = [n for n, _ in plan]
        self.reader = dict(plan)
        self.banks = banks
        assert len(self.reader) == len(plan)
        self.filled = m.count(f"{name}_filled", len(plan))
        self.read = {e: m.count(f"{name}_read_{e}", sum(r == e for _, r in plan)) for e in sorted(set(self.reader.values()))}

        for c in self.read.values():
            assert c.base >= c.per

    def bank(self, name, parts=None):
        ps = self.ps[:, self.names.index(name) % self.banks, :]
        return ps if parts is None else ps.rearrange("p (g n) -> p g n", g=parts)

    def full(self, i, name):
        return self.filled.sem, self.filled.at(i, self.names.index(name) + 1)

    def used(self, i, name):
        n, e = self.names.index(name), self.reader[name]
        return self.read[e].sem, self.read[e].at(i, sum(self.reader[x] == e for x in self.names[:n + 1]))

    def free(self, i, name):
        n = self.names.index(name)
        if n >= self.banks:
            return self.used(i, self.names[n - self.banks])
        last = max(x for x in range(len(self.names)) if x % self.banks == n)
        sem, value = self.used(i, self.names[last])
        return sem, value - self.read[self.reader[self.names[last]]].per


class Mem:

    def __init__(self, nc, ctx, tag):
        self.nc, self.ctx, self.tag = nc, ctx, tag
        self.counts, self.passed = [], None

    def sb(self, name, shape, dt=F32):
        return self.ctx.enter_context(self.nc.sbuf_tensor(f"{self.tag}_{name}", shape, dt))

    def ps(self, name, shape, dt=F32):
        return self.ctx.enter_context(self.nc.psum_tensor(f"{self.tag}_psum_{name}", shape, dt))

    def count(self, name, per=1):
        self.counts.append(Count(self.ctx.enter_context(self.nc.semaphore(f"{self.tag}_sem_{name}")), per))
        return self.counts[-1]

    def start(self, eng):
        for c in self.counts:
            eng.sem_inc(c.sem, c.base)

    def settle(self, eng):
        if self.passed is None:
            self.passed = self.ctx.enter_context(self.nc.semaphore(f"{self.tag}_sem_passed"))
        eng.sem_inc(self.passed, 1)


def project_phase(nc, a, k):
    with ExitStack() as ctx:
        m = Mem(nc, ctx, "pj")
        xs = [m.sb(f"x{p}", [P, TT, D]) for p in range(2)]
        h = m.sb("h", [P, TT, D])
        hT = [m.sb(f"hT{p}", [P, KC, GT]) for p in range(2)]
        QT = [m.sb(f"QT{p}", [P, KC, GT]) for p in range(2)]
        off = m.sb("off", [P, TT, H * NK])
        stats, mv, rstd = m.sb("st", [P, TT, 6]), m.sb("mv", [P, TT, 2]), m.sb("rs", [P, TT])
        Wq, bq = m.sb("Wq", [P, KC, D]), m.sb("bq", [P, KC])
        Woff, boff = m.sb("Woff", [P, KC, H * NK]), m.sb("boff", [P, H * NK])
        mask_i, mask_f = m.sb("mi", [B, M], I32), m.sb("mf", [B, M])
        length, length_all = m.sb("len", [B, 1]), m.sb("lena", [P, 2, B])
        wide = [m.sb(f"wide{j}", [P, B // 2, KC, 2 * NK]) for j in range(4)]
        bad = m.sb("bad", [P, 1])
        ps_t, ps_q, ps_o = m.ps("t", [P, TT, D]), m.ps("q", [P, KC, GT]), m.ps("o", [P, TT, H * NK])
        ps_l = m.ps("l", [P, 512])

        x_in = [m.count(f"x_in{p}", 16) for p in range(2)]
        q_out = [m.count(f"q_out{p}", 16) for p in range(2)]
        w_in, wq_in = m.count("w_in"), m.count("wq_in")
        h_done = m.count("h_done")
        tr_done, hT_done = m.count("tr"), m.count("hT", TT)
        q_done, qT_done = m.count("q"), m.count("qT", KC)
        o_done, off_done = m.count("o"), m.count("off")
        link, olink = m.count("link", LN_LINKS), m.count("olink")
        plink = m.count("plink")
        len_ps, len_in, bad_done, bad_ps = m.count("lps"), m.count("lin"), m.count("bd"), m.count("bp")
        flag_done, var, std = m.count("flag"), m.count("var"), m.count("std")
        block = ctx.enter_context(nc.Block())

        @block.sync
        def _(sp):
            def load(t):
                sp.wait_ge(h_done.sem, h_done.at(t.r - 1, 0))
                sp.dma_start(xs[t.p][:], a["x_tok"][bass.ds(t.r, 1)].rearrange("o t p d -> (o p) t d")).then_inc(x_in[t.p].sem, 16)

            load(Round(0, 0))
            sp.dma_start(k["const"][:], a["const"]).then_inc(w_in.sem, 16)
            sp.dma_start(Wq[:], a["xWq"]).then_inc(wq_in.sem, 16)
            sp.dma_start(bq[:], a["xbq"]).then_inc(wq_in.sem, 16)
            sp.dma_start(Woff[:], a["xWoff"]).then_inc(wq_in.sem, 16)
            sp.dma_start(boff[:], a["xboff"].partition_broadcast(P)).then_inc(wq_in.sem, 16)
            sp.dma_start(mask_i[:], a["mask"]).then_inc(wq_in.sem, 16)
            rounds(sp, NG, lambda t, last: None if last else load(t.next()))
            for name, w in k["weights"].items():
                src = a[name].partition_broadcast(P) if len(a[name].shape) == 1 else a[name]
                sp.dma_start(w[:], src).then_inc(w_in.sem, 16)
            sp.wait_ge(w_in.sem, w_in.at(0, 16 * (1 + len(k["weights"]))))

        @block.gpsimd
        def _(pool):
            m.start(pool)

        @block.vector
        def _(dve):
            def norm(t):
                chain = Chain(dve, link, t.r)
                dve.wait_ge(x_in[t.p].sem, x_in[t.p].at(t.i, 16))
                dve.wait_ge(tr_done.sem, tr_done.at(t.r, 0))
                layer_norm(nc, m, chain, xs[t.p], h, stats, mv, rstd, var, std, TT).then_inc(h_done.sem, 1)

            def offsets(t, chain):
                dve.wait_ge(o_done.sem, o_done.at(t.r, 1))
                dve.wait_ge(off_done.sem, off_done.at(t.r, 0))
                chain.link(nc.vector.tensor_tensor(off[:], ps_o[:], bc(boff[:], 1, TT), ALU.add))
                for b in range(P // L):
                    for hq in range(HQ):
                        src = off[b * L:(b + 1) * L].rearrange("p t (g h k) -> p t g h k", g=KC, h=HQ)[:, :, :, hq, :]
                        dst = k["ix"][hq * L:(hq + 1) * L, bass.ds(t.r * PAIRS, PAIRS)].rearrange(
                            "p (t u) g v k -> p t u g v k", t=TT)[:, :, b // 2, :, b % 2]
                        last = nc.vector.tensor_copy(dst, src)
                last.then_inc(off_done.sem, 1)

            def group(t, last):
                if not last:
                    norm(t.next())
                offsets(t, Chain(dve, olink, t.r))

            norm(Round(0, 0))
            dve.wait_ge(wq_in.sem, wq_in.at(0, 5 * 16))
            rounds(dve, NG, group)

            step = Chain(dve, plink, 0)
            step.link(nc.vector.tensor_copy(mask_f[:], mask_i[:]))
            step.link(nc.vector.tensor_scalar(mask_f[:], mask_f[:], -1.0, 1.0, ALU.mult, ALU.add))
            step.link(nc.vector.tensor_reduce(length[:], mask_f[:], AX, ALU.add))
            nc.vector.tensor_scalar_add(length[:], length[:], -1.0).then_inc(len_in.sem, 1)
            dve.wait_ge(len_ps.sem, len_ps.at(0, 1))
            step.link(nc.vector.tensor_copy(length_all[:, 0, :], ps_l[:, 0:B]))
            step.link(nc.vector.reciprocal(length_all[:, 1, :], length_all[:, 0, :]))
            n_, rn = wide[2][:], wide[3][:]
            for j, full in enumerate((n_, rn)):
                pairs = bc(length_all[:, j, :], 2, NK).rearrange("p (u v) k -> p u v k", v=2)
                for g in range(KC):
                    last = nc.vector.tensor_copy(full[:, :, g, :].rearrange("p u (v k) -> p u v k", v=2), pairs)
            step.link(last)
            dve.wait_ge(off_done.sem, off_done.at(NG, 0))
            ix, t0, t1 = k["ix"].rearrange("p u g v k -> p u g (v k)"), wide[0][:], wide[1][:]
            flat = "p u g v -> p (u g v)"
            step.link(nc.vector.tensor_tensor(ix.rearrange("p u g v -> p (u g) v"), ix.rearrange("p u g v -> p (u g) v"),
                                              bc(k["const"][:, CREF:CREF + 2 * NK], 1, B // 2 * KC), ALU.add))
            ix, t0, t1, n_, rn = (v.rearrange(flat) for v in (ix, t0, t1, n_, rn))
            step.link(nc.vector.tensor_scalar(ix, ix, k["const"][:, CQ:CQ + 1], None, ALU.add))
            step.link(nc.vector.tensor_tensor(t0, ix, rn, ALU.mult))
            step.link(nc.vector.tensor_scalar(t0, t0, MAGIC, None, ALU.add))
            step.link(nc.vector.tensor_scalar(t0, t0, -MAGIC, None, ALU.add))
            step.link(nc.vector.tensor_tensor(t0, t0, n_, ALU.mult))
            step.link(nc.vector.tensor_tensor(ix, ix, t0, ALU.subtract))
            step.link(nc.vector.tensor_tensor(t0, ix, n_, ALU.mult))
            step.link(nc.vector.tensor_scalar(t0, t0, 0.0, None, ALU.is_lt))
            step.link(nc.vector.tensor_tensor(t0, t0, n_, ALU.mult))
            step.link(nc.vector.tensor_tensor(ix, ix, t0, ALU.add))
            step.link(nc.vector.tensor_scalar(ix, ix, 1.0 / (M - 1), 2.0, ALU.mult, ALU.mult))
            step.link(nc.vector.tensor_scalar(ix, ix, -1.0, 1.0, ALU.add, ALU.add))
            step.link(nc.vector.tensor_scalar(ix, ix, float(M), -1.0, ALU.mult, ALU.add))
            step.link(nc.vector.tensor_scalar(ix, ix, 0.5, None, ALU.mult))
            step.link(nc.vector.tensor_scalar(t0, ix, float(HEAD - 1), None, ALU.is_ge))
            step.link(nc.vector.tensor_scalar(t1, ix, float(M - TAIL), None, ALU.is_lt))
            step.link(nc.vector.tensor_tensor(t0, t0, t1, ALU.mult))
            nc.vector.tensor_reduce(bad[:, 0:1], t0, AX, ALU.max).then_inc(bad_done.sem, 1)
            dve.wait_ge(bad_ps.sem, bad_ps.at(0, 1))
            nc.vector.tensor_copy(k["flag"], ps_l[0:1, 256:257]).then_inc(flag_done.sem, 1)

        @block.tensor
        def _(pe):
            def transposes(t):
                pe.wait_ge(h_done.sem, h_done.at(t.r, 1))
                pe.wait_ge(hT_done.sem, hT_done.at(t.r, 0))
                for j in range(TT):
                    for c in range(KC):
                        last = nc.tensor.transpose(ps_t[:, j, c * P:(c + 1) * P], h[:, j, c * P:(c + 1) * P], k["ident"])
                last.then_inc(tr_done.sem, 1)

            def group(t, last):
                if not last:
                    transposes(t.next())
                pe.wait_ge(hT_done.sem, hT_done.at(t.r, TT))
                pe.wait_ge(qT_done.sem, qT_done.at(t.r, 0))
                for e in range(KC):
                    for c in range(KC):
                        mm = nc.tensor.matmul(ps_q[:, e, :], Wq[:, c, e * P:(e + 1) * P], hT[t.p][:, c, :],
                                              start=(c == 0), stop=(c == KC - 1))
                mm.then_inc(q_done.sem, 1)
                pe.wait_ge(qT_done.sem, qT_done.at(t.r, KC))
                pe.wait_ge(off_done.sem, off_done.at(t.r, 0))
                for j in range(TT):
                    for c in range(KC):
                        mm = nc.tensor.matmul(ps_o[:, j, :], QT[t.p][:, c, j * P:(j + 1) * P], Woff[:, c, :],
                                              start=(c == 0), stop=(c == KC - 1))
                mm.then_inc(o_done.sem, 1)

            pe.wait_ge(w_in.sem, w_in.at(0, 16))
            transposes(Round(0, 0))
            pe.wait_ge(wq_in.sem, wq_in.at(0, 5 * 16))
            rounds(pe, NG, group)
            pe.wait_ge(len_in.sem, len_in.at(0, 1))
            nc.tensor.matmul(ps_l[:, 0:B], length[:].broadcast_to([B, P]), k["const"][0:B, CI:CI + B],
                             start=True, stop=True).then_inc(len_ps.sem, 1)
            pe.wait_ge(bad_done.sem, bad_done.at(0, 1))
            nc.tensor.matmul(ps_l[0:1, 256:257], bad[:, 0:1], k["ones"], start=True, stop=True).then_inc(bad_ps.sem, 1)

        @block.scalar
        def _(act):
            def turned(t):
                act_deviation(nc, act, t.r, mv, rstd[:], var, std)
                act.wait_ge(tr_done.sem, tr_done.at(t.r, 1))
                act.wait_ge(q_done.sem, q_done.at(t.r - 1, 0))
                for j in range(TT):
                    nc.scalar.activation(hT[t.p][:, :, j * P:(j + 1) * P], ps_t[:, j, :].rearrange("p (c n) -> p c n", c=KC),
                                         ACT.Copy).then_inc(hT_done.sem, 1)

            def group(t, last):
                if not last:
                    turned(t.next())
                act.wait_ge(q_done.sem, q_done.at(t.r, 1))
                act.wait_ge(q_out[t.p].sem, q_out[t.p].at(t.i, 0))
                act.wait_ge(o_done.sem, o_done.at(t.r - 1, 0))
                for e in range(KC):
                    nc.scalar.activation(QT[t.p][:, e, :], ps_q[:, e, :], ACT.Identity,
                                         bias=bq[:, e:e + 1]).then_inc(qT_done.sem, 1)
                act.wait_ge(qT_done.sem, qT_done.at(t.r, KC))
                act.dma_start(a["q_scr"][bass.ds(t.r, 1)].rearrange("o p k t -> (o p) k t"), QT[t.p][:]).then_inc(q_out[t.p].sem, 16)

            act.wait_ge(wq_in.sem, wq_in.at(0, 5 * 16))
            turned(Round(0, 0))
            rounds(act, NG, group)
            for q in q_out:
                act.wait_ge(q.sem, q.at(NG // 2, 0))


class Interpolation:

    def __init__(self, m, nu, wr, ring, stride):
        self.nu, self.wr = nu, wr
        self.tent = [m.sb(f"tent{r}", [P, nu * NK, wr]) for r in range(ring)]
        self.prod = m.sb("prod", [P, nu * NK, wr])
        self.wtent = m.sb("wtent", [P, nu * NK, wr])
        self.A = m.sb("A", [P, nu, stride])
        self.s = m.sb("s", [P, nu, NK])
        self.e = m.sb("e", [P, nu, NK])
        self.top, self.tot = m.sb("top", [P, nu]), m.sb("tot", [P, nu])

    def pool_difference(self, nc, r, rows, ix):
        return nc.gpsimd.tensor_tensor(self.tent[r][:], bc(rows, 1, self.nu * NK), bc(ix, 2, self.wr), ALU.subtract)

    def act_abs(self, nc, r):
        return nc.scalar.activation(self.tent[r][:], self.tent[r][:], ACT.Abs)

    def act_tent(self, nc, r):
        return nc.scalar.activation(self.tent[r][:], self.tent[r][:], ACT.Relu, bias=1.0, scale=-1.0)

    def dve_scores(self, nc, chain, r, S):
        v = "p (u k) m -> p u k m"
        chain.link(nc.vector.tensor_tensor(self.prod[:].rearrange(v, k=NK), self.tent[r][:].rearrange(v, k=NK),
                                           bc(S, 2, NK), ALU.mult))
        chain.link(nc.vector.tensor_reduce(self.s[:].rearrange("p u k -> p (u k)"), self.prod[:], AX, ALU.add))
        chain.link(nc.vector.tensor_reduce(self.top[:], self.s[:], AX, ALU.max))
        return nc.vector.tensor_tensor(self.s[:], self.s[:], bc(self.top[:], 2, NK), ALU.subtract)

    def act_exp(self, nc):
        return nc.scalar.activation(self.e[:], self.s[:], ACT.Exp, scale=0.5 * ATT_SCALE)

    def dve_softmax(self, nc, chain):
        chain.link(nc.vector.tensor_reduce(self.tot[:], self.e[:], AX, ALU.add))
        chain.link(nc.vector.reciprocal(self.tot[:], self.tot[:]))
        return nc.vector.scalar_tensor_tensor(self.e[:], self.e[:], 0.5, bc(self.tot[:], 2, NK), ALU.mult, ALU.mult)

    def weigh(self, eng, r):
        return eng.tensor_tensor(self.wtent[:], self.tent[r][:], bc(self.e[:].rearrange("p u k -> p (u k)"), 2, self.wr),
                                 ALU.mult)

    def dve_sum(self, nc):
        return nc.vector.tensor_reduce(self.A[:, :, 0:self.wr], self.wtent[:].rearrange("p (u k) m -> p u m k", k=NK), AX, ALU.add)

    def dve_weights(self, nc, chain, r):
        chain.link(self.dve_softmax(nc, chain))
        chain.link(self.weigh(nc.vector, r))
        return self.dve_sum(nc)

    DVE_LINKS = 3 + 4


def attend_window_phase(nc, a, k):
    U = 2 * KC
    with ExitStack() as ctx:
        m = Mem(nc, ctx, "aw")
        two = range(2)
        craw = m.sb("craw", [P, KC, W * BG])
        cw = [m.sb(f"c{p}", [P, KC, BG, 64]) for p in two]
        Qblk = [m.sb(f"Qb{p}", [P, KC, BG, P]) for p in two]
        KT, V = [m.sb(f"K{p}", [P, KC, BG, W]) for p in two], [m.sb(f"V{p}", [P, PAIRS, D]) for p in two]
        AT, cT = m.sb("AT", [P, KC, P]), [m.sb(f"cT{p}", [P, KC, GT]) for p in two]
        Wk, Wv, bk, bv = (k["weights"][n] for n in ("xWk", "xWv", "xbk", "xbv"))
        ip = Interpolation(m, U, W, 2, 64)
        ps_kv, ps_s = m.ps("kv", [P, 2, 512]), m.ps("s", [P, 2, 512])
        ps_at, ps_av = m.ps("at", [P, KC, P]), m.ps("av", [P, 2, KC, P])

        c_in = m.count("c_in", 16)
        q_in = [m.count(f"q_in{p}", 16 * HQ) for p in two]
        c_out = [m.count(f"c_out{p}", 16) for p in two]
        zero, cw_done = m.count("zero"), m.count("cw")
        k_ps, k_cp = m.count("k_ps", KC), m.count("k_cp", KC)
        v_ps, v_cp = m.count("v_ps", PAIRS), m.count("v_cp", PAIRS)
        s_ps = m.count("s_ps", PAIRS)
        diff, ab, tent = m.count("diff", PAIRS), m.count("ab", PAIRS), m.count("tent", PAIRS)
        sc_done, ex_done = m.count("sc", PAIRS), m.count("ex", PAIRS)
        wt_done, wp_done = m.count("wt", PAIRS), m.count("wp", PAIRS)
        A_done, at_ps, at_cp = m.count("A", PAIRS), m.count("at_ps", PAIRS), m.count("at_cp", PAIRS)
        av_ps, av_cp = m.count("av_ps", PAIRS), m.count("av_cp", PAIRS)
        av_ps.base = 2 * PAIRS + 1
        link, xlink = m.count("link", 3), m.count("xlink", 2)
        block = ctx.enter_context(nc.Block())

        @block.sync
        def _(sp):
            sp.wait_ge(zero.sem, zero.at(0, 5))
            def load(t, last):
                sp.wait_ge(cw_done.sem, cw_done.at(t.r, 0))
                sp.dma_start(craw[:], a["ctx"][bass.ds(t.r, 1), :, :, 0:W * BG].rearrange("o p c w -> (o p) c w")).then_inc(c_in.sem, 16)
                sp.wait_ge(s_ps.sem, s_ps.at(t.r - 1, 0))
                for hq in range(HQ):
                    rows = slice(hq * HD, (hq + 1) * HD)
                    sp.dma_start(Qblk[t.p][rows, :, :, hq * L:(hq + 1) * L],
                                 a["q_scr"][bass.ds(t.r, 1), rows].rearrange("o p k (b q) -> (o p) k b q", q=L)
                                 ).then_inc(q_in[t.p].sem, 16)

            rounds(sp, NG, load)

        @block.gpsimd
        def _(pool):
            m.start(pool)
            for buf in (*cw, *Qblk, ip.A):
                nc.gpsimd.memset(buf[:], 0.0).then_inc(zero.sem, 1)
            pool.wait_ge(zero.sem, zero.at(0, 5))

            def reorder(t):
                pool.wait_ge(c_in.sem, c_in.at(t.r, 16))
                pool.wait_ge(v_ps.sem, v_ps.at(t.r - 1, 0))
                m.settle(pool)
                nc.gpsimd.tensor_copy(cw[t.p][:, :, :, 0:W], craw[:].rearrange("p c (m b) -> p c b m", b=BG)).then_inc(cw_done.sem, 1)

            def difference(t, j):
                pool.wait_ge(wp_done.sem, wp_done.at(t.r, j - 1))
                ix = k["ix"][:, bass.ds(t.r * PAIRS + j, 1)].rearrange("p u g v k -> p (u g v k)")
                ip.pool_difference(nc, j % 2, k["const"][:, CMC:CMC + W], ix).then_inc(diff.sem, 1)

            def group(t, last):
                for j in range(PAIRS):
                    pool.wait_ge(wt_done.sem, wt_done.at(t.r, j + 1))
                    pool.wait_ge(A_done.sem, A_done.at(t.r, j))
                    m.settle(pool)
                    ip.weigh(nc.gpsimd, j % 2).then_inc(wp_done.sem, 1)
                    if j + 2 < PAIRS:
                        difference(t, j + 2)
                    elif not last:
                        difference(t.next(), j + 2 - PAIRS)
                    if j == 0 and not last:
                        reorder(t.next())

            reorder(Round(0, 0))
            difference(Round(0, 0), 0)
            difference(Round(0, 0), 1)
            rounds(pool, NG, group)

        @block.vector
        def _(dve):
            def values(t, j):
                dve.wait_ge(v_ps.sem, v_ps.at(t.r, j + 1))
                dve.wait_ge(av_ps.sem, av_ps.at(t.r - 1, j + 1 - PAIRS))
                nc.vector.tensor_tensor(V[t.p][:, j, :], ps_kv[:, j % 2, :], bv[:], ALU.add).then_inc(v_cp.sem, 1)

            def scores(t, j):
                dve.wait_ge(s_ps.sem, s_ps.at(t.r, j + 1))
                dve.wait_ge(tent.sem, tent.at(t.r, j + 1))
                S = ps_s[:, j % 2, 0:U * W].rearrange("p (u m) -> p u m", m=W)
                ip.dve_scores(nc, Chain(dve, link, t.r * PAIRS + j), j % 2, S).then_inc(sc_done.sem, 1)

            def group(t, last):
                for j in range(PAIRS):
                    dve.wait_ge(ex_done.sem, ex_done.at(t.r, j + 1))
                    ip.dve_softmax(nc, Chain(dve, xlink, t.r * PAIRS + j)).then_inc(wt_done.sem, 1)
                    if j + 1 < PAIRS:
                        scores(t, j + 1)
                    elif not last:
                        scores(t.next(), 0)
                    for v in ((1, 2), (3,), (), ())[j]:
                        values(t, v)
                    if j == PAIRS - 1 and not last:
                        values(t.next(), 0)
                    dve.wait_ge(wp_done.sem, wp_done.at(t.r, j + 1))
                    dve.wait_ge(at_ps.sem, at_ps.at(t.r, j))
                    ip.dve_sum(nc).then_inc(A_done.sem, 1)

            values(Round(0, 0), 0)
            scores(Round(0, 0), 0)
            rounds(dve, NG, group)

        @block.tensor
        def _(pe):
            def keys(t, e):
                pe.wait_ge(v_cp.sem, v_cp.at(t.r, 0))
                pe.wait_ge(k_cp.sem, k_cp.at(t.r, max(e - 1, 0)))
                for c in range(KC):
                    mm = nc.tensor.matmul(ps_kv[:, e % 2, 0:W * BG], Wk[:, c, e * P:(e + 1) * P], cw[t.p][:, c, :, 0:W],
                                          start=(c == 0), stop=(c == KC - 1))
                mm.then_inc(k_ps.sem, 1)

            def values(t, j):
                if j < 2:
                    pe.wait_ge(k_cp.sem, k_cp.at(t.r, KC - 1 + j))
                else:
                    pe.wait_ge(v_cp.sem, v_cp.at(t.r, j - 1))
                for c in range(KC):
                    rows = cw[t.p][:, c, 2 * j:2 * j + 2, :].rearrange("p b m -> p (b m)")
                    mm = nc.tensor.matmul(ps_kv[:, j % 2, :], rows, Wv[:, c, :], start=(c == 0), stop=(c == KC - 1))
                mm.then_inc(v_ps.sem, 1)

            def scores(t, j):
                if j == 0:
                    pe.wait_ge(q_in[t.p].sem, q_in[t.p].at(t.i, 16 * HQ))
                pe.wait_ge(k_cp.sem, k_cp.at(t.r, KC))
                pe.wait_ge(sc_done.sem, sc_done.at(t.r, j - 1))
                for u in range(U):
                    b, g = 2 * j + u % 2, u // 2
                    mm = nc.tensor.matmul(ps_s[:, j % 2, u * W:(u + 1) * W], Qblk[t.p][:, g, b, :], KT[t.p][:, g, b, :],
                                          start=True, stop=True)
                mm.then_inc(s_ps.sem, 1)

            def turn(t, j):
                pe.wait_ge(A_done.sem, A_done.at(t.r, j + 1))
                pe.wait_ge(at_cp.sem, at_cp.at(t.r, j))
                for g in range(KC):
                    mm = nc.tensor.transpose(ps_at[:, g, :], ip.A[:, 2 * g:2 * g + 2, :].rearrange("p b m -> p (b m)"),
                                             k["ident"])
                mm.then_inc(at_ps.sem, 1)

            def context(t, j):
                pe.wait_ge(at_cp.sem, at_cp.at(t.r, j + 1))
                pe.wait_ge(v_cp.sem, v_cp.at(t.r, j + 1))
                pe.wait_ge(av_cp.sem, av_cp.at(t.r, j))
                for u in range(U):
                    b, g = u % 2, u // 2
                    rows = slice(b * 64, b * 64 + W)
                    mm = nc.tensor.matmul(ps_av[:, b, g, :], V[t.p][rows, j, g * P:(g + 1) * P], AT[rows, g, :],
                                          start=True, stop=True)
                mm.then_inc(av_ps.sem, 1)

            def group(t, last):
                n = t.next()
                for j in range(PAIRS):
                    turn(t, j)
                    if j + 2 < PAIRS:
                        scores(t, j + 2)
                    elif not last:
                        scores(n, j + 2 - PAIRS)
                    context(t, j)
                    if not last:
                        if j == 0:
                            pe.wait_ge(cw_done.sem, cw_done.at(n.r, 1))
                        for e in (2 * j, 2 * j + 1):
                            keys(n, e) if e < KC else values(n, e - KC)

            pe.wait_ge(zero.sem, zero.at(0, 5))
            first = Round(0, 0)
            pe.wait_ge(cw_done.sem, cw_done.at(0, 1))
            for e in range(KC):
                keys(first, e)
            values(first, 0)
            values(first, 1)
            scores(first, 0)
            scores(first, 1)
            values(first, 2)
            values(first, 3)
            rounds(pe, NG, group)

        @block.scalar
        def _(act):
            def keys(t, e):
                act.wait_ge(k_ps.sem, k_ps.at(t.r, e + 1))
                act.wait_ge(s_ps.sem, s_ps.at(t.r - 1, 0))
                nc.scalar.activation(KT[t.p][:, e], ps_kv[:, e % 2, 0:W * BG].rearrange("p (b m) -> p b m", b=BG),
                                     ACT.Identity, bias=bk[:, e:e + 1]).then_inc(k_cp.sem, 1)

            def tents(t, j):
                act.wait_ge(diff.sem, diff.at(t.r, j + 1))
                ip.act_abs(nc, j % 2).then_inc(ab.sem, 1)
                act.wait_ge(ab.sem, ab.at(t.r, j + 1))
                ip.act_tent(nc, j % 2).then_inc(tent.sem, 1)

            def weights(t, j):
                act.wait_ge(sc_done.sem, sc_done.at(t.r, j + 1))
                act.wait_ge(wp_done.sem, wp_done.at(t.r, j))
                ip.act_exp(nc).then_inc(ex_done.sem, 1)

            def group(t, last):
                n = t.next()
                for j in range(PAIRS):
                    if j in (1, 2) and not last:
                        keys(n, 2 * j - 2)
                        keys(n, 2 * j - 1)
                    act.wait_ge(at_ps.sem, at_ps.at(t.r, j + 1))
                    act.wait_ge(av_ps.sem, av_ps.at(t.r, j))
                    nc.scalar.activation(AT[:], ps_at[:], ACT.Copy).then_inc(at_cp.sem, 1)
                    if j + 2 < PAIRS:
                        weights(t, j + 2)
                    elif not last:
                        weights(n, j + 2 - PAIRS)
                    act.wait_ge(av_ps.sem, av_ps.at(t.r, j + 1))
                    if j == 0:
                        act.wait_ge(c_out[t.p].sem, c_out[t.p].at(t.i, 0))
                    for hq in range(HQ):
                        rows = slice(hq * HD, (hq + 1) * HD)
                        mm = nc.scalar.activation(
                            cT[t.p][rows].rearrange("p c (q b) -> p b c q", b=BG)[:, 2 * j:2 * j + 2],
                            ps_av[rows, :, :, hq * L:(hq + 1) * L], ACT.Copy)
                    mm.then_inc(av_cp.sem, 1)
                    if j + 3 < PAIRS:
                        tents(t, j + 3)
                    elif not last:
                        tents(n, j + 3 - PAIRS)
                act.wait_ge(av_cp.sem, av_cp.at(t.r, PAIRS))
                act.dma_start(a["c_scr"][bass.ds(t.r, 1)].rearrange("o p k t -> (o p) k t"), cT[t.p][:]).then_inc(c_out[t.p].sem, 16)

            for e in range(KC):
                keys(Round(0, 0), e)
            tents(Round(0, 0), 0)
            tents(Round(0, 0), 1)
            weights(Round(0, 0), 0)
            weights(Round(0, 0), 1)
            tents(Round(0, 0), 2)
            rounds(act, NG, group)
            for c in c_out:
                act.wait_ge(c.sem, c.at(NG // 2, 0))


def attend_all_phase(nc, a, k):
    MT = [(0, P), (P, P), (2 * P, M - 2 * P)]
    with ExitStack() as ctx:
        m = Mem(nc, ctx, "aa")
        craw, cb = m.sb("craw", [P, KC, M * BG]), m.sb("cb", [P, KC, M])
        Q, Qblk = m.sb("Q", [P, KC, GT]), m.sb("Qb", [P, KC, P])
        KT, V = m.sb("K", [P, KC, M]), m.sb("V", [P, len(MT), D])
        AT, cT = m.sb("AT", [P, len(MT), P]), m.sb("cT", [P, KC, GT])
        Wk, Wv, bk, bv = (k["weights"][n] for n in ("xWk", "xWv", "xbk", "xbv"))
        ip = Interpolation(m, 1, M, 1, M)
        ps, ps_at, ps_av = m.ps("big", [P, KC, 512]), m.ps("at", [P, len(MT), P]), m.ps("av", [P, 512])

        c_in, q_in, c_out = m.count("c_in", 16), m.count("q_in", 16), m.count("c_out", 16)
        zero, cb_done, qb_done = m.count("zero"), m.count("cb"), m.count("qb")
        k_ps, k_cp, v_ps, v_cp, s_ps = m.count("kp"), m.count("kc"), m.count("vp"), m.count("vc"), m.count("sp")
        diff, ab, tent = m.count("diff", KC), m.count("ab", KC), m.count("tent", KC)
        sc_done, ex_done, A_done = m.count("sc", KC), m.count("ex", KC), m.count("A", KC)
        at_ps, at_cp, av_ps, av_cp = m.count("atp", KC), m.count("atc", KC), m.count("avp", KC), m.count("avc", KC)
        link, plink = m.count("link", KC * ip.DVE_LINKS), m.count("plink", HQ)
        block = ctx.enter_context(nc.Block())

        @block.sync
        def _(sp):
            with sp.Fori(0, NG) as i:
                sp.wait_ge(av_cp.sem, av_cp.at(i * BG, 0))
                sp.dma_start(craw[:], a["ctx"][bass.ds(i, 1)].rearrange("o p c w -> (o p) c w")).then_inc(c_in.sem, 16)
                sp.dma_start(Q[:], a["q_scr"][bass.ds(i, 1)].rearrange("o p k t -> (o p) k t")).then_inc(q_in.sem, 16)
                sp.wait_ge(av_cp.sem, av_cp.at(i * BG + BG, 0))
                sp.dma_start(a["c_scr"][bass.ds(i, 1)].rearrange("o p k t -> (o p) k t"), cT[:]).then_inc(c_out.sem, 16)
            sp.wait_ge(c_out.sem, c_out.at(NG, 0))

        @block.gpsimd
        def _(pool):
            m.start(pool)
            nc.gpsimd.memset(Qblk[:], 0.0).then_inc(zero.sem, 1)
            pool.wait_ge(zero.sem, zero.at(0, 1))
            with pool.Fori(0, NG) as i:
                pool.wait_ge(q_in.sem, q_in.at(i, 16))
                m.settle(pool)
                with pool.Fori(0, PAIRS) as u:
                    for v in range(2):
                        r = i * BG + u * 2 + v
                        pool.wait_ge(s_ps.sem, s_ps.at(r, 0))
                        m.settle(pool)
                        steps = Chain(pool, plink, r, m.settle)
                        for hq in range(HQ):
                            rows = slice(hq * HD, hq * HD + HD)
                            steps.link(nc.gpsimd.tensor_copy(Qblk[rows, :, hq * L:(hq + 1) * L],
                                                             Q[rows, :, bass.ds(u * 2 * L + v * L, L)]))
                        pool.sem_inc(qb_done.sem, 1)
                        for g in range(KC):
                            pool.wait_ge(A_done.sem, A_done.at(r, g))
                            ix = k["ix"][:, bass.ds(i * PAIRS + u, 1), g, v, :].rearrange("p b k -> p (b k)")
                            ip.pool_difference(nc, 0, k["const"][:, CMC:CMC + M], ix).then_inc(diff.sem, 1)
                            pool.wait_ge(diff.sem, diff.at(r, g + 1))

        @block.vector
        def _(dve):
            with dve.Fori(0, B) as r:
                chain = Chain(dve, link, r)
                dve.wait_ge(v_ps.sem, v_ps.at(r, 1))
                for t, (_, n) in enumerate(MT):
                    last = nc.vector.tensor_tensor(V[0:n, t, :], ps[0:n, t, :], bv[0:n, :], ALU.add)
                last.then_inc(v_cp.sem, 1)
                for g in range(KC):
                    dve.wait_ge(s_ps.sem, s_ps.at(r, 1))
                    dve.wait_ge(tent.sem, tent.at(r, g + 1))
                    dve.wait_ge(A_done.sem, A_done.at(r, g))
                    ip.dve_scores(nc, chain, 0, ps[:, g:g + 1, 0:M]).then_inc(sc_done.sem, 1)
                    dve.wait_ge(ex_done.sem, ex_done.at(r, g + 1))
                    dve.wait_ge(at_ps.sem, at_ps.at(r, g))
                    ip.dve_weights(nc, chain, 0).then_inc(A_done.sem, 1)
                chain.close()

        @block.tensor
        def _(pe):
            with pe.Fori(0, B) as r:
                pe.wait_ge(cb_done.sem, cb_done.at(r, 1))
                pe.wait_ge(sc_done.sem, sc_done.at(r, 0))
                for e in range(KC):
                    for c in range(KC):
                        last = nc.tensor.matmul(ps[:, e, 0:M], Wk[:, c, e * P:(e + 1) * P], cb[:, c, :],
                                                start=(c == 0), stop=(c == KC - 1))
                last.then_inc(k_ps.sem, 1)
                pe.wait_ge(k_cp.sem, k_cp.at(r, 1))
                for t, (at, n) in enumerate(MT):
                    for c in range(KC):
                        last = nc.tensor.matmul(ps[0:n, t, :], cb[:, c, at:at + n], Wv[:, c, :],
                                                start=(c == 0), stop=(c == KC - 1))
                last.then_inc(v_ps.sem, 1)
                pe.wait_ge(v_cp.sem, v_cp.at(r, 1))
                pe.wait_ge(qb_done.sem, qb_done.at(r, 1))
                for g in range(KC):
                    last = nc.tensor.matmul(ps[:, g, 0:M], Qblk[:, g, :], KT[:, g, :], start=True, stop=True)
                last.then_inc(s_ps.sem, 1)
                for g in range(KC):
                    pe.wait_ge(A_done.sem, A_done.at(r, g + 1))
                    pe.wait_ge(at_cp.sem, at_cp.at(r, g))
                    for t, (at, n) in enumerate(MT):
                        last = nc.tensor.transpose(ps_at[0:n, t, :], ip.A[:, 0, at:at + n], k["ident"])
                    last.then_inc(at_ps.sem, 1)
                    pe.wait_ge(at_cp.sem, at_cp.at(r, g + 1))
                    pe.wait_ge(av_cp.sem, av_cp.at(r, g))
                    for t, (_, n) in enumerate(MT):
                        last = nc.tensor.matmul(ps_av[:, 0:P], V[0:n, t, g * P:(g + 1) * P], AT[0:n, t, :],
                                                start=(t == 0), stop=(t == len(MT) - 1))
                    last.then_inc(av_ps.sem, 1)

        @block.scalar
        def _(act):
            with act.Fori(0, NG) as i:
                act.wait_ge(c_in.sem, c_in.at(i, 16))
                act.wait_ge(c_out.sem, c_out.at(i, 0))
                with act.Fori(0, BG) as b:
                    r = i * BG + b
                    act.wait_ge(v_ps.sem, v_ps.at(r, 0))
                    raw = craw[:].rearrange("p c (m b) -> p c m b", b=BG)[:, :, :, bass.ds(b, 1)]
                    nc.scalar.activation(cb[:].unsqueeze(3), raw, ACT.Copy).then_inc(cb_done.sem, 1)
                    act.wait_ge(k_ps.sem, k_ps.at(r, 1))
                    act.wait_ge(s_ps.sem, s_ps.at(r, 0))
                    for e in range(KC):
                        last = nc.scalar.activation(KT[:, e, :], ps[:, e, 0:M], ACT.Identity, bias=bk[:, e:e + 1])
                    last.then_inc(k_cp.sem, 1)
                    for g in range(KC):
                        act.wait_ge(diff.sem, diff.at(r, g + 1))
                        ip.act_abs(nc, 0).then_inc(ab.sem, 1)
                        act.wait_ge(ab.sem, ab.at(r, g + 1))
                        ip.act_tent(nc, 0).then_inc(tent.sem, 1)
                        act.wait_ge(sc_done.sem, sc_done.at(r, g + 1))
                        ip.act_exp(nc).then_inc(ex_done.sem, 1)
                        act.wait_ge(at_ps.sem, at_ps.at(r, g + 1))
                        act.wait_ge(av_ps.sem, av_ps.at(r, g))
                        nc.scalar.activation(AT[:, 0:2, :], ps_at[:, 0:2, :], ACT.Copy)
                        nc.scalar.activation(AT[0:1, 2, :], ps_at[0:1, 2, :], ACT.Copy).then_inc(at_cp.sem, 1)
                        act.wait_ge(av_ps.sem, av_ps.at(r, g + 1))
                        for hq in range(HQ):
                            rows = slice(hq * HD, (hq + 1) * HD)
                            last = nc.scalar.activation(cT[rows, g, :].rearrange("p (q b) -> p q b", b=BG)[:, :, bass.ds(b, 1)],
                                                        ps_av[rows, hq * L:(hq + 1) * L].unsqueeze(2),
                                                        ACT.Copy)
                        last.then_inc(av_cp.sem, 1)


FRONT = ([("y0", "dve"), ("y1", "dve"), ("t0", "act"), ("t1", "act")]
         + [(f"{n}{e}", "dve") for n in "qkv" for e in range(KC)] + [("lr", "dve")])


LINKS = 2 * (2 + 4) + 2 * 4
BACK = ([("sk0", "dve"), ("sq0", "dve"), ("vt0", "act"), ("kt0", "act"), ("si0", "dve"), ("khT0", "act"), ("qhT0", "act"),
         ("up", "dve")] + [(f"qk0{h}", "dve") for h in range(HQ)]
        + [("so0", "dve"), ("ti0", "act"), ("to0", "act"), ("o0", "act"), ("gi0", "dve"), ("go0", "dve"),
           ("si1", "dve"), ("so1", "dve"), ("ti1", "act"), ("to1", "act"), ("gi1", "dve"), ("go1", "dve"),
           ("sk1", "dve"), ("sq1", "dve"), ("vt1", "act"), ("wo", "act"), ("khT1", "act"), ("qhT1", "act")]
        + [(f"qk1{h}", "dve") for h in range(HQ)] + [("o1", "act"), ("z0", "dve"), ("z1", "dve")])


def fast_phase(nc, a, k):
    S2 = 2 * KC
    with ExitStack() as ctx:
        m = Mem(nc, ctx, "fw")
        front, back = Ring(m, "front", 4, FRONT), Ring(m, "back", 4, BACK)
        cT, xs = m.sb("cT", [P, KC, GT]), m.sb("x", [P, TT, D])
        x1 = [m.sb(f"x1{p}", [P, TT, D]) for p in range(2)]
        h, x2 = m.sb("h", [P, TT, D]), m.sb("x2", [P, TT, D])
        stats, mv, rstd = m.sb("st", [P, TT, 6]), m.sb("mv", [P, TT, 2]), m.sb("rs", [P, TT])
        hT, hx = m.sb("hT", [P, KC, GT]), m.sb("hx", [P, KC, P])
        f = [{n: m.sb(f"{n}T{p}", [P, KC, GT]) for n in "qkv"} for p in range(2)]
        lr = m.sb("lr", [P, 3, 2 * H])
        lrs = [m.sb(f"lrs{p}", [P, 3, 2 * H]) for p in range(2)]
        lrf = [m.sb(f"lrf{p}", [P, KC, 2]) for p in range(2)]
        vt, kt = m.sb("vt", [P, KC, P]), m.sb("kt", [P, KC, P])
        e, top, tot = m.sb("e", [P, 2, 512]), m.sb("top", [P, 2, P]), m.sb("tot", [P, 2, P])
        kh, qh = e[:, 0, :], e[:, 1, :]
        khT, qhT = m.sb("khT", [P, KC, P]), m.sb("qhT", [P, KC, P])
        qk = m.sb("qk", [P, HQ, KC, P])
        oT = m.sb("oT", [P, KC, GT])
        win0, wout0, wrow0 = m.sb("win0", [P, KC, P]), m.sb("wout0", [P, KC, P]), m.sb("wrow0", [P, KC, P])
        win, wout, wrow = m.sb("win", [P, KC, P]), m.sb("wout", [P, KC, P]), m.sb("wrow", [P, KC, P])
        grad = m.sb("grad", [P, 2, 512])
        at, atT = m.sb("at", [P, 2, KC, P]), m.sb("atT", [P, 2, KC, P])
        atop, asum = m.sb("atop", [P, S2]), m.sb("asum", [P, S2])
        w = k["weights"]
        Wo, Wp, Wo2, Wlr = w["xWo"], {n: w[f"aW{n}"] for n in "qkv"}, w["aWo"], w["aWlr"]
        bo, conv, wi, wt, wr = w["xbo"], w["conv"], w["aWin"], w["aWout"], w["aWout_rows"]
        wsum = m.sb("wsum", [P, 3, KC])
        const = k["const"]
        neg, own = const[:, CNEG:CNEG + P], const[:, CBM:CBM + BG]
        head, causal = const[:, CHM:CHM + P], const[:, CCA:CCA + P]

        c_in, x_in, x_out = m.count("c_in", 16), m.count("x_in", 16), m.count("x_out", 16)
        setup = m.count("setup")
        x1_done, h_done, var, std = m.count("x1"), m.count("h"), m.count("var"), m.count("std")
        hT_done, hx_done = m.count("hT"), m.count("hx")
        base_done, conv_done = m.count("base", 3 * KC), m.count("conv", 3 * KC)
        z_done, za, ze, zp, zl, lr_done = (m.count(n) for n in ("z", "za", "ze", "zp", "zl", "lrd"))
        flink, clink, rlink = m.count("flink", LN_LINKS + 1), m.count("clink", 3 * KC * 2), m.count("rlink")
        d_done, e_done, p_done = m.count("d", 2), m.count("e", 2), m.count("p", 2)
        qk_done = m.count("qkd", 2)
        s_done, a_done, n_done, w_done = m.count("s", 2), m.count("a", 2), m.count("n", 2), m.count("w", 3)
        x2_done = m.count("x2")
        link, slink = m.count("link", LINKS), m.count("slink", 3)
        block = ctx.enter_context(nc.Block())

        @block.sync
        def _(sp):
            def load(t):
                sp.wait_ge(x1_done.sem, x1_done.at(t.r, 0))
                sp.dma_start(cT[:], a["c_scr"][bass.ds(t.r, 1)].rearrange("o p k t -> (o p) k t")).then_inc(c_in.sem, 16)
                sp.dma_start(xs[:], a["x_lb"][bass.ds(t.r, 1)].rearrange("o p t d -> (o p) t d")).then_inc(x_in.sem, 16)

            def group(t, last):
                if not last:
                    load(t.next())
                sp.wait_ge(x2_done.sem, x2_done.at(t.r, 1))
                sp.dma_start(a["x2_scr"][bass.ds(t.r, 1)].rearrange("o p t d -> (o p) t d"), x2[:]).then_inc(x_out.sem, 16)

            load(Round(0, 0))
            rounds(sp, NG, group)
            sp.wait_ge(x_out.sem, x_out.at(NG, 0))

        @block.gpsimd
        def _(pool):
            m.start(pool)
            with pool.Fori(0, NG) as i:
                pool.wait_ge(hT_done.sem, hT_done.at(i, 1))
                pool.wait_ge(*front.full(i, "y0"))
                m.settle(pool)
                for c in range(KC):
                    src = bc(bc(hT[:, c, 0:BG], 1, HQ), 3, DI)
                    last = nc.gpsimd.tensor_copy(hx[:, c, :].rearrange("p (h b d) -> p h b d", h=HQ, b=BG), src)
                last.then_inc(hx_done.sem, 1)

        @block.vector
        def _(dve):
            st = Chain(dve, slink, 0)
            for buf in (win0, wout0, wrow0):
                last = nc.vector.memset(buf[:], 0.0)
            st.link(last)
            for hq in range(HQ):
                rows, cols = slice(hq * HD, (hq + 1) * HD), slice(hq * HD, (hq + 1) * HD)
                for dst, src in ((win0, wi), (wout0, wt)):
                    nc.vector.tensor_copy(dst[rows, :, cols].rearrange("p g (b d) -> p g b d", b=BG), bc(src[rows], 2, BG))
                last = nc.vector.tensor_copy(wrow0[rows, :, cols], wr[rows])
            st.link(last)
            st.link(nc.vector.tensor_scalar_add(wsum[:], conv[:, :, :, 3], 1.0))
            nc.vector.memset(top[:], 0.0).then_inc(setup.sem, 1)

            def enter(t):
                ch, x, i = Chain(dve, flink, t.r), x1[t.p], t.r
                dve.wait_ge(x_in.sem, x_in.at(i, 16))
                for j in range(TT):
                    dve.wait_ge(*front.full(i, f"y{j}"))
                    nc.vector.tensor_tensor(x[:, j, :], front.bank(f"y{j}"), xs[:, j, :], ALU.add).then_inc(front.read["dve"].sem, 1)
                dve.wait_ge(*front.used(i, "y1"))
                ch.link(nc.vector.tensor_tensor(x[:], x[:], bc(bo[:], 1, TT), ALU.add))
                dve.sem_inc(x1_done.sem, 1)
                layer_norm(nc, m, ch, x, h, stats, mv, rstd, var, std, TT).then_inc(h_done.sem, 1)
                ch.close()

            def convolve(t, fills):
                for fill in fills:
                    n, b = "qkv".index(fill[0]), int(fill[1])
                    y, at_ = f[t.p][fill[0]][:, b, :], n * KC + b
                    ch = Chain(dve, clink, t.r)
                    ch.n = 2 * at_
                    dve.wait_ge(base_done.sem, base_done.at(t.r, at_ + 1))
                    for s_ in (1, 2, 3):
                        tap = nc.vector.scalar_tensor_tensor(
                            y[:, s_ * BG:], front.bank(fill)[:, 0:GT - s_ * BG], conv[:, n, b, 3 - s_:4 - s_],
                            y[:, s_ * BG:], ALU.mult, ALU.add)
                        if s_ < 3:
                            ch.link(tap)
                    tap.then_inc(front.read["dve"].sem, 1)
                    if fill == "v3":
                        dve.wait_ge(*front.used(t.r, fill))
                        dve.sem_inc(conv_done.sem, 3 * KC)

            def rates(t):
                i, out = t.r, lrs[t.p]
                dve.wait_ge(*front.full(i, "lr"))
                nc.vector.tensor_scalar(lr[:], front.bank("lr")[:, 0:6 * H].rearrange("p (c n) -> p c n", c=3), 0.001, None,
                                        ALU.add).then_inc(z_done.sem, 1)
                dve.wait_ge(ze.sem, ze.at(i, 1))
                nc.vector.tensor_scalar_add(out[:], out[:], 1.0).then_inc(zp.sem, 1)
                dve.wait_ge(zl.sem, zl.at(i, 1))
                Chain(dve, rlink, i).link(nc.vector.scalar_tensor_tensor(out[:], lr[:], 0.0, out[:], ALU.max, ALU.add))
                for hq in range(HQ):
                    rows = slice(hq * HD, (hq + 1) * HD)
                    src = out[rows, 2, :].rearrange("p (g h j) -> p g h j", g=KC, h=HQ)[:, :, hq, :]
                    copy = nc.vector.tensor_copy(lrf[t.p][rows], src)
                copy.then_inc(lr_done.sem, 1)
                dve.wait_ge(lr_done.sem, lr_done.at(i, 1))
                dve.sem_inc(front.read["dve"].sem, 1)

            def exponents(i, ch, c):
                for j, n in enumerate((f"sk{c}", f"sq{c}")):
                    dve.wait_ge(*back.full(i, n))
                    s = back.bank(n).rearrange("p (n d) -> p n d", d=DI)
                    ch.link(nc.vector.tensor_reduce(top[:, j, :], s, AX, ALU.max))
                    nc.vector.tensor_tensor(e[:, j, :].rearrange("p (n d) -> p n d", d=DI), s, bc(top[:, j, :], 2, DI),
                                            ALU.subtract).then_inc(back.read["dve"].sem, 1)
                dve.wait_ge(*back.used(i, f"sq{c}"))
                dve.sem_inc(d_done.sem, 1)

            def weights(t, ch, c):
                dve.wait_ge(e_done.sem, e_done.at(t.r, c + 1))
                rows = e[:].rearrange("p j (n d) -> p (j n) d", d=DI)
                flat = tot[:].rearrange("p j n -> p (j n)")
                ch.link(nc.vector.tensor_reduce(flat, rows, AX, ALU.add))
                ch.link(nc.vector.reciprocal(flat, flat))
                by = tot[:].rearrange("p j (h b) -> p (j h) b", b=BG)
                ch.link(nc.vector.tensor_tensor(by, by, bc(own, 1, 2 * H), ALU.mult))
                rate = lrs[t.p][:, c, :].rearrange("p (h j) -> p h j", j=2)[:, :, 1]
                k_by = tot[:, 0, :].rearrange("p (h b) -> p h b", b=BG)
                ch.link(nc.vector.tensor_tensor(k_by, k_by, bc(rate, 2, BG), ALU.mult))
                nc.vector.tensor_tensor(rows, rows, bc(flat, 2, DI), ALU.mult).then_inc(p_done.sem, 1)

            def causal_products(i, c):
                for h_ in range(HQ):
                    n = f"qk{c}{h_}"
                    dve.wait_ge(*back.full(i, n))
                    nc.vector.tensor_tensor(qk[:, h_], back.bank(n, KC), bc(causal, 1, KC),
                                            ALU.mult).then_inc(back.read["dve"].sem, 1)
                dve.wait_ge(*back.used(i, f"qk{c}{HQ - 1}"))
                dve.sem_inc(qk_done.sem, 1)

            def add_own_heads(i, ch, fill, j, old, new):
                dve.wait_ge(*back.full(i, fill))
                g4 = grad[:, j, :].rearrange("p (g n) -> p g n", g=KC)
                nc.vector.tensor_tensor(g4, back.bank(fill, KC), bc(head, 1, KC), ALU.mult).then_inc(back.read["dve"].sem, 1)
                dve.wait_ge(*back.used(i, fill))
                return nc.vector.tensor_tensor(new[:], old[:], g4, ALU.add)

            def masked(i, fill, j):
                dve.wait_ge(*back.full(i, fill))
                nc.vector.tensor_tensor(at[:, j], back.bank(fill, KC), bc(neg, 1, KC), ALU.add).then_inc(back.read["dve"].sem, 1)

            def maxima(i, ch, it):
                dve.wait_ge(*back.used(i, f"so{it}"))
                ch.link(nc.vector.tensor_reduce(atop[:], at[:].rearrange("p j g n -> p (j g) n"), AX, ALU.max))
                nc.vector.tensor_scalar(atop[:], atop[:], -ATT_SCALE, None, ALU.mult).then_inc(s_done.sem, 1)

            def normalise(t, ch, it):
                dve.wait_ge(a_done.sem, a_done.at(t.r, it + 1))
                ch.link(nc.vector.reciprocal(asum[:], asum[:]))
                for j in range(2):
                    part = asum[:, j * KC:(j + 1) * KC]
                    mm = nc.vector.tensor_tensor(part, part, lrf[t.p][:, :, 1 - j], ALU.mult)
                ch.link(mm)
                by = at[:].rearrange("p j g n -> p (j g) n")
                nc.vector.tensor_tensor(by, by, bc(asum[:], 2, P), ALU.mult).then_inc(n_done.sem, 1)

            def step_weights(i, ch, it):
                ch.link(add_own_heads(i, ch, f"gi{it}", 0, wout, wout))
                add_own_heads(i, ch, f"go{it}", 1, win0 if it == 0 else win, win).then_inc(w_done.sem, 1)

            def leave(t):
                dve.wait_ge(x_out.sem, x_out.at(t.r, 0))
                for j in range(TT):
                    dve.wait_ge(*back.full(t.r, f"z{j}"))
                    nc.vector.tensor_tensor(x2[:, j, :], back.bank(f"z{j}"), x1[t.p][:, j, :], ALU.add).then_inc(back.read["dve"].sem, 1)
                dve.wait_ge(*back.used(t.r, "z1"))
                dve.sem_inc(x2_done.sem, 1)

            def group(t, last):
                n, i = t.next(), t.r
                ch = Chain(dve, link, i)
                ahead = (lambda *fills: None) if last else (lambda *fills: convolve(n, fills))
                exponents(i, ch, 0)
                masked(i, "si0", 0)
                weights(t, ch, 0)
                if not last:
                    enter(n)
                add_own_heads(i, ch, "up", 0, wout0, wout).then_inc(w_done.sem, 1)
                causal_products(i, 0)
                masked(i, "so0", 1)
                maxima(i, ch, 0)
                normalise(t, ch, 0)
                ahead("q0", "q1", "q2", "q3")
                step_weights(i, ch, 0)
                masked(i, "si1", 0)
                masked(i, "so1", 1)
                maxima(i, ch, 1)
                ahead("k0", "k1")
                normalise(t, ch, 1)
                ahead("k2", "k3", "v0", "v1")
                step_weights(i, ch, 1)
                exponents(i, ch, 1)
                ahead("v2")
                weights(t, ch, 1)
                ahead("v3")
                causal_products(i, 1)
                if not last:
                    rates(n)
                leave(t)
                ch.close()

            first = Round(0, 0)
            enter(first)
            convolve(first, [x for x, _ in FRONT if x[0] in "qkv"])
            rates(first)
            rounds(dve, NG, group)

        @block.tensor
        def _(pe):
            pe.wait_ge(setup.sem, setup.at(0, 1))

            def blocks(i, ring, fill, parts, pairs):
                pe.wait_ge(*ring.free(i, fill))
                out = ring.bank(fill, parts)
                for g, (lhsT, rhs) in enumerate(pairs):
                    last = nc.tensor.matmul(out[:, g, :], lhsT, rhs, start=True, stop=True)
                last.then_inc(ring.filled.sem, 1)

            def transposes(i, ring, fill, parts):
                pe.wait_ge(*ring.free(i, fill))
                out = ring.bank(fill, len(parts))
                for g, x in enumerate(parts):
                    last = nc.tensor.transpose(out[:, g, :], x, k["ident"])
                last.then_inc(ring.filled.sem, 1)

            def deep(i, ring, fill, n, lhsT, rhs):
                pe.wait_ge(*ring.free(i, fill))
                for c in range(KC):
                    last = nc.tensor.matmul(ring.bank(fill)[:, 0:n], lhsT(c), rhs(c), start=(c == 0), stop=(c == KC - 1))
                last.then_inc(ring.filled.sem, 1)

            def ahead(t, *fills):
                i = t.r
                for fill in fills:
                    j = int(fill[1]) if fill[1:].isdigit() else 0
                    if fill[0] == "y":
                        if j == 0:
                            pe.wait_ge(c_in.sem, c_in.at(i, 16))
                        deep(i, front, fill, D, lambda c: cT[:, c, j * P:(j + 1) * P], lambda c: Wo[:, c, :])
                    elif fill[0] == "t":
                        if j == 0:
                            pe.wait_ge(h_done.sem, h_done.at(i, 1))
                        transposes(i, front, fill, [h[:, j, c * P:(c + 1) * P] for c in range(KC)])
                    elif fill[0] in "qkv":
                        if fill == "q0":
                            pe.wait_ge(hT_done.sem, hT_done.at(i, 1))
                        deep(i, front, fill, GT, lambda c: Wp[fill[0]][:, c, j * P:(j + 1) * P], lambda c: hT[:, c, :])
                    else:
                        pe.wait_ge(*front.free(i, "lr"))
                        pe.wait_ge(hx_done.sem, hx_done.at(i, 1))
                        for part in range(3):
                            for c in range(KC):
                                tokens = hx[:, c, :] if part == 2 else hT[:, c, part * P:(part + 1) * P]
                                mm = nc.tensor.matmul(front.bank("lr")[:, part * 2 * H:(part + 1) * 2 * H], tokens, Wlr[:, c, :],
                                                      start=(c == 0), stop=(c == KC - 1))
                        mm.then_inc(front.filled.sem, 1)

            def causal(i, c):
                for h_ in range(HQ):
                    r = slice(h_ * HD, (h_ + 1) * HD)
                    blocks(i, back, f"qk{c}{h_}", KC, [(khT[r, g, :], qhT[r, g, :]) for g in range(KC)])

            def output(i, c):
                pe.wait_ge(*back.free(i, f"o{c}"))
                pe.wait_ge(qk_done.sem, qk_done.at(i, c + 1))
                out, w_row = back.bank(f"o{c}", KC), wrow if c else wrow0
                for g in range(KC):
                    nc.tensor.matmul(out[:, g, :], w_row[:, g, :], qhT[:, g, :], start=True, stop=False)
                    for h_ in range(HQ):
                        r = slice(h_ * HD, (h_ + 1) * HD)
                        mm = nc.tensor.matmul(out[r, g, :], vt[:, g, r], qk[:, h_, g, :], start=False, stop=True)
                mm.then_inc(back.filled.sem, 1)

            def group(t, last):
                n, i = t.next(), t.r
                q, key, v = (f[t.p][x] for x in "qkv")
                by_g, halves = range(KC), [slice(0, P), slice(P, 2 * P)]
                go = (lambda *fills: None) if last else (lambda *fills: ahead(n, *fills))

                pe.wait_ge(conv_done.sem, conv_done.at(i, 3 * KC))
                blocks(i, back, "sk0", KC, [(key[:, g, halves[0]], win0[:, g, :]) for g in by_g])
                blocks(i, back, "sq0", KC, [(q[:, g, halves[0]], win0[:, g, :]) for g in by_g])
                transposes(i, back, "vt0", [v[:, g, halves[0]] for g in by_g])
                transposes(i, back, "kt0", [key[:, g, halves[0]] for g in by_g])
                blocks(i, back, "si0", KC, [(win0[:, g, :], key[:, g, halves[0]]) for g in by_g])
                go("y0", "y1")
                pe.wait_ge(p_done.sem, p_done.at(i, 1))
                transposes(i, back, "khT0", [kh[:, g * P:(g + 1) * P] for g in by_g])
                transposes(i, back, "qhT0", [qh[:, g * P:(g + 1) * P] for g in by_g])
                pe.wait_ge(*back.used(i, "kt0"))
                blocks(i, back, "up", KC, [(vt[:, g, :], kh[:, g * P:(g + 1) * P]) for g in by_g])
                pe.wait_ge(*back.used(i, "qhT0"))
                causal(i, 0)
                pe.wait_ge(w_done.sem, w_done.at(i, 1))
                blocks(i, back, "so0", KC, [(wout[:, g, :], v[:, g, halves[0]]) for g in by_g])
                go("t0", "t1", "q0", "q1", "q2", "q3")
                for it in range(2):
                    pe.wait_ge(n_done.sem, n_done.at(i, it + 1))
                    transposes(i, back, f"ti{it}", [at[:, 0, g, :] for g in by_g])
                    transposes(i, back, f"to{it}", [at[:, 1, g, :] for g in by_g])
                    if it == 0:
                        output(i, 0)
                    pe.wait_ge(*back.used(i, f"ti{it}"))
                    blocks(i, back, f"gi{it}", KC, [(vt[:, g, :], atT[:, 0, g, :]) for g in by_g])
                    pe.wait_ge(*back.used(i, f"to{it}"))
                    blocks(i, back, f"go{it}", KC, [(kt[:, g, :], atT[:, 1, g, :]) for g in by_g])
                    if it == 0:
                        go("k0", "k1")
                        pe.wait_ge(w_done.sem, w_done.at(i, 2))
                        blocks(i, back, "si1", KC, [(win[:, g, :], key[:, g, halves[0]]) for g in by_g])
                        blocks(i, back, "so1", KC, [(wout[:, g, :], v[:, g, halves[0]]) for g in by_g])
                        go("k2", "k3", "v0", "v1")
                go("v2")
                pe.wait_ge(w_done.sem, w_done.at(i, 3))
                blocks(i, back, "sk1", KC, [(key[:, g, halves[1]], win[:, g, :]) for g in by_g])
                blocks(i, back, "sq1", KC, [(q[:, g, halves[1]], win[:, g, :]) for g in by_g])
                transposes(i, back, "vt1", [v[:, g, halves[1]] for g in by_g])
                transposes(i, back, "wo", [wout[:, g, :] for g in by_g])
                go("v3", "lr")
                pe.wait_ge(p_done.sem, p_done.at(i, 2))
                transposes(i, back, "khT1", [kh[:, g * P:(g + 1) * P] for g in by_g])
                transposes(i, back, "qhT1", [qh[:, g * P:(g + 1) * P] for g in by_g])
                pe.wait_ge(*back.used(i, "qhT1"))
                causal(i, 1)
                output(i, 1)
                pe.wait_ge(*back.used(i, "o1"))
                for j in range(TT):
                    deep(i, back, f"z{j}", D, lambda c: oT[:, c, j * P:(j + 1) * P], lambda c: Wo2[:, c, :])

            ahead(Round(0, 0), *[x for x, _ in FRONT])
            rounds(pe, NG, group)

        @block.scalar
        def _(act):
            act.wait_ge(setup.sem, setup.at(0, 1))

            def take(i, fill, dst, parts=KC):
                act.wait_ge(*back.full(i, fill))
                nc.scalar.activation(dst, back.bank(fill, parts), ACT.Copy).then_inc(back.read["act"].sem, 1)

            def deviation(t):
                act_deviation(nc, act, t.r, mv, rstd[:], var, std)

            def turned(t):
                for j in range(TT):
                    act.wait_ge(*front.full(t.r, f"t{j}"))
                    nc.scalar.activation(hT[:, :, j * P:(j + 1) * P], front.bank(f"t{j}", KC), ACT.Copy).then_inc(front.read["act"].sem, 1)
                act.wait_ge(*front.used(t.r, "t1"))
                act.sem_inc(hT_done.sem, 1)

            def base(t, *fills):
                for fill in fills:
                    act.wait_ge(*front.full(t.r, fill))
                    nc.scalar.activation(f[t.p][fill[0]][:, int(fill[1]), :], front.bank(fill)[:, 0:GT], ACT.Copy,
                                         scale=wsum[:, "qkv".index(fill[0]), int(fill[1]):int(fill[1]) + 1]).then_inc(base_done.sem, 1)

            def rates(t):
                i, out = t.r, lrs[t.p]
                act.wait_ge(z_done.sem, z_done.at(i, 1))
                nc.scalar.activation(out[:], lr[:], ACT.Abs).then_inc(za.sem, 1)
                act.wait_ge(za.sem, za.at(i, 1))
                nc.scalar.activation(out[:], out[:], ACT.Exp, scale=-1.0).then_inc(ze.sem, 1)
                act.wait_ge(zp.sem, zp.at(i, 1))
                nc.scalar.activation(out[:], out[:], ACT.Ln).then_inc(zl.sem, 1)

            def exponentials(i, c):
                act.wait_ge(d_done.sem, d_done.at(i, c + 1))
                nc.scalar.activation(e[:], e[:], ACT.Exp).then_inc(e_done.sem, 1)

            def row_exponentials(i, it):
                act.wait_ge(s_done.sem, s_done.at(i, it + 1))
                for n in range(S2):
                    mm = nc.scalar.activation(at[:, n // KC, n % KC, :], at[:, n // KC, n % KC, :], ACT.Exp,
                                              bias=atop[:, n:n + 1], scale=ATT_SCALE, accum_out=asum[:, n:n + 1])
                mm.then_inc(a_done.sem, 1)

            def group(t, last):
                n, i = t.next(), t.r
                ahead = (lambda *fills: None) if last else (lambda *fills: base(n, *fills))
                take(i, "vt0", vt[:])
                take(i, "kt0", kt[:])
                exponentials(i, 0)
                if not last:
                    deviation(n)
                take(i, "khT0", khT[:])
                take(i, "qhT0", qhT[:])
                row_exponentials(i, 0)
                if not last:
                    turned(n)
                ahead("q0", "q1", "q2", "q3")
                take(i, "ti0", atT[:, 0])
                take(i, "to0", atT[:, 1])
                take(i, "o0", oT[:, :, 0:P])
                ahead("k0", "k1")
                row_exponentials(i, 1)
                ahead("k2", "k3", "v0", "v1")
                take(i, "ti1", atT[:, 0])
                take(i, "to1", atT[:, 1])
                ahead("v2")
                take(i, "vt1", vt[:])
                exponentials(i, 1)
                take(i, "wo", wrow[:])
                ahead("v3")
                take(i, "khT1", khT[:])
                take(i, "qhT1", qhT[:])
                if not last:
                    rates(n)
                take(i, "o1", oT[:, :, P:2 * P])

            first = Round(0, 0)
            deviation(first)
            turned(first)
            base(first, *[x for x, _ in FRONT if x[0] in "qkv"])
            rates(first)
            rounds(act, NG, group)


def experts_phase(nc, a, k):
    with ExitStack() as ctx:
        m = Mem(nc, ctx, "ex")
        fills = [(f"{n}{t}", r) for t in range(TT) for n, r in
                 [("t", "act"), ("g", "dve")] + [(f"y{e}_", "dve") for e in range(E)]]
        ring = Ring(m, "ring", 8, fills)
        x2, h, acc = m.sb("x", [P, TT, D]), m.sb("h", [P, TT, D]), m.sb("acc", [P, TT, D])
        stats, mv, rstd = m.sb("st", [P, TT, 6]), m.sb("mv", [P, TT, 2]), m.sb("rs", [P, TT])
        hT = m.sb("hT", [P, TT, KC, P])
        We, Wg = m.sb("We", [P, E, KC, D]), m.sb("Wg", [P, KC, E])
        sc, pick, best = m.sb("sc", [P, E]), m.sb("pick", [P, TT, E]), m.sb("best", [P, 2])
        order = k["const"][:, CORD:CORD + E]
        w_in, x_in, x_out = m.count("w_in"), m.count("x_in", 16), m.count("x_out", 16)
        h_done, var, std = m.count("h"), m.count("var"), m.count("std")
        x_done, o_done = m.count("x"), m.count("o")
        link = m.count("link", LN_LINKS + TT * 4 + 1)
        block = ctx.enter_context(nc.Block())

        @block.sync
        def _(sp):
            sp.dma_start(Wg[:], a["gate"]).then_inc(w_in.sem, 16)
            sp.dma_start(We[:], a["expert"].rearrange("e p c d -> p e c d")).then_inc(w_in.sem, 16)
            with sp.Fori(0, NG) as i:
                sp.wait_ge(x_done.sem, x_done.at(i, 0))
                sp.dma_start(x2[:], a["x2_scr"][bass.ds(i, 1)].rearrange("o p t d -> (o p) t d")).then_inc(x_in.sem, 16)
                sp.wait_ge(o_done.sem, o_done.at(i, 1))
                sp.dma_start(a["out"][bass.ds(i, 1)].rearrange("o p t d -> (o p) t d"), acc[:]).then_inc(x_out.sem, 16)
            sp.wait_ge(x_out.sem, x_out.at(NG, 0))

        @block.gpsimd
        def _(pool):
            m.start(pool)

        @block.vector
        def _(dve):
            with dve.Fori(0, NG) as i:
                ch = Chain(dve, link, i)
                dve.wait_ge(x_in.sem, x_in.at(i, 16))
                layer_norm(nc, m, ch, x2, h, stats, mv, rstd, var, std, TT).then_inc(h_done.sem, 1)
                dve.wait_ge(h_done.sem, h_done.at(i, 1))
                dve.wait_ge(x_out.sem, x_out.at(i, 0))
                ch.link(nc.vector.tensor_tensor(acc[:], x2[:], h[:], ALU.add))
                dve.sem_inc(x_done.sem, 1)
                for t in range(TT):
                    dve.wait_ge(*ring.full(i, f"g{t}"))
                    s = ring.bank(f"g{t}")[:, 0:E]
                    ch.link(nc.vector.tensor_reduce(best[:, 0:1], s, AX, ALU.max))
                    nc.vector.tensor_scalar(sc[:], s, best[:, 0:1], None, ALU.is_ge).then_inc(ring.read["dve"].sem, 1)
                    dve.wait_ge(*ring.used(i, f"g{t}"))
                    ch.link(nc.vector.tensor_tensor(sc[:], sc[:], order, ALU.mult))
                    ch.link(nc.vector.tensor_reduce(best[:, 1:2], sc[:], AX, ALU.max))
                    ch.link(nc.vector.tensor_scalar(pick[:, t, :], sc[:], best[:, 1:2], None, ALU.is_equal))
                    for e in range(E):
                        dve.wait_ge(*ring.full(i, f"y{e}_{t}"))
                        nc.vector.scalar_tensor_tensor(acc[:, t, :], ring.bank(f"y{e}_{t}"), pick[:, t, e:e + 1], acc[:, t, :],
                                                       ALU.mult, ALU.add).then_inc(ring.read["dve"].sem, 1)
                        dve.wait_ge(*ring.used(i, f"y{e}_{t}"))
                dve.sem_inc(o_done.sem, 1)
                ch.close()

        @block.tensor
        def _(pe):
            pe.wait_ge(w_in.sem, w_in.at(0, 2 * 16))
            with pe.Fori(0, NG) as i:
                pe.wait_ge(h_done.sem, h_done.at(i, 1))
                for t in range(TT):
                    pe.wait_ge(*ring.free(i, f"t{t}"))
                    for c in range(KC):
                        last = nc.tensor.transpose(ring.bank(f"t{t}", KC)[:, c, :], h[:, t, c * P:(c + 1) * P], k["ident"])
                    last.then_inc(ring.filled.sem, 1)
                    pe.wait_ge(*ring.used(i, f"t{t}"))
                    pe.wait_ge(*ring.free(i, f"g{t}"))
                    for c in range(KC):
                        last = nc.tensor.matmul(ring.bank(f"g{t}")[:, 0:E], hT[:, t, c, :], Wg[:, c, :], start=(c == 0), stop=(c == KC - 1))
                    last.then_inc(ring.filled.sem, 1)
                    for e in range(E):
                        pe.wait_ge(*ring.free(i, f"y{e}_{t}"))
                        for c in range(KC):
                            last = nc.tensor.matmul(ring.bank(f"y{e}_{t}"), hT[:, t, c, :], We[:, e, c, :], start=(c == 0), stop=(c == KC - 1))
                        last.then_inc(ring.filled.sem, 1)

        @block.scalar
        def _(act):
            with act.Fori(0, NG) as i:
                act_deviation(nc, act, i, mv, rstd[:], var, std)
                for t in range(TT):
                    act.wait_ge(*ring.full(i, f"t{t}"))
                    nc.scalar.activation(hT[:, t], ring.bank(f"t{t}", KC), ACT.Copy).then_inc(ring.read["act"].sem, 1)


def layer(nc, a, upto=9, force_all=False):
    with ExitStack() as ctx:
        m = Mem(nc, ctx, "all")
        k = {"const": m.sb("const", [P, CN]), "ix": m.sb("ix", [P, B // 2, KC, 2, NK])[:]}
        k["flag"] = m.sb("flag", [1, 1], I32)[:]
        k["weights"] = {n: m.sb(n, [P, *a[n].shape[len(a[n].shape) > 1:]]) for n in WEIGHTS}
        k["ident"] = k["const"][:, CI:CI + P]
        k["ones"] = k["const"][:, CONE:CONE + 1]
        project_phase(nc, a, k)
        outside = nc.values_load(k["flag"], min_val=0, max_val=P)
        with nc.If(outside < 1 if not force_all else outside > 1000):
            attend_window_phase(nc, a, k)
        with nc.Else():
            attend_all_phase(nc, a, k)
        if upto > 1:
            fast_phase(nc, a, k)
            experts_phase(nc, a, k)


def feature_blocks(w):
    return np.ascontiguousarray(w.reshape(KC, P, -1).transpose(1, 0, 2))


def layouts(v):
    out = {
        "x_tok": v["x"].reshape(NG, TT, P, D),
        "x_lb": v["x"].reshape(NG, BG, TT, C, D).transpose(0, 3, 1, 2, 4).reshape(NG, P, TT, D),
        "ctx": np.roll(v["ctx_1024"], TAIL, axis=1).reshape(NG, BG, M, KC, P).transpose(0, 4, 3, 2, 1).reshape(NG, P, KC, M * BG),
        "mask": v["mask_BxS2_if0"],
        "const": shape_constants(),
        "xWoff": feature_blocks(v["L0_xattn_Woff"].T), "xboff": v["L0_xattn_boff"],
        "xbo": v["L0_xattn_bo"], "xbv": v["L0_xattn_bv"],
    }
    for n in ("Wq", "Wk", "Wv", "Wo"):
        out["x" + n] = feature_blocks(v["L0_xattn_" + n].T)
        out["a" + n] = feature_blocks(v["L0_attn_" + n])
    for n in ("bq", "bk"):
        out["x" + n] = v["L0_xattn_" + n].reshape(KC, P).T
    out["aWlr"] = feature_blocks(v["L0_attn_Wlr"])
    out["conv"] = np.stack([v["L0_attn_conv_" + n].reshape(KC, P, 4) for n in "qkv"]).transpose(2, 0, 1, 3)
    for n in ("in", "out"):
        w = v[f"L0_attn_W_{n}_init"][0].reshape(DI, KC, HQ, HD)
        out["aW" + n] = w.transpose(2, 3, 1, 0).reshape(P, KC, DI)
    out["aWout_rows"] = np.repeat(v["L0_attn_W_out_init"][0].reshape(DI, KC, HQ, 1, HD).transpose(2, 3, 0, 1, 4), BG,
                                  axis=1).reshape(P, KC, HD)
    out["gate"] = feature_blocks(v["L0_ffn_gate_w"].T)
    out["expert"] = v["L0_ffn_expert_w"].transpose(0, 2, 1).reshape(E, KC, P, D).transpose(0, 2, 1, 3)
    return {n: np.ascontiguousarray(w) for n, w in out.items()}


WEIGHTS = ("xWk", "xWv", "xbk", "xbv", "xWo", "xbo", "aWq", "aWk", "aWv", "aWo", "aWlr", "conv", "aWin", "aWout", "aWout_rows")
SCRATCH = {"q_scr": (NG, P, KC, GT), "c_scr": (NG, P, KC, GT), "x2_scr": (NG, P, TT, D)}


def kernel(**inputs):
    import concourse.bacc as bacc
    from concourse.bass_utils import run_bass_kernel_spmd

    nc = bacc.Bacc("TRN2", target_bir_lowering=False, num_devices=1)
    arrays = layouts({n: np.asarray(w) for n, w in inputs.items()})
    a = {n: nc.dram_tensor(n, w.shape, mybir.dt.from_np(w.dtype), kind="ExternalInput").ap() for n, w in arrays.items()}
    for n, shape in SCRATCH.items():
        a[n] = nc.dram_tensor(n, shape, F32).ap()
    a["out"] = nc.dram_tensor("out", (NG, P, TT, D), F32, kind="ExternalOutput").ap()
    layer(nc, a)
    r = run_bass_kernel_spmd(nc, [arrays], core_ids=[0])
    return r.results[0]["out"].reshape(NG, C, BG, TT, D).transpose(0, 2, 3, 1, 4).reshape(B, L, D)
```

```python
from contextlib import ExitStack

import numpy as np

import concourse.bass as bass
from concourse import mybir

F32 = mybir.dt.float32
I32 = mybir.dt.int32
ALU = mybir.AluOpType
ACT = mybir.ActivationFunctionType
AX = mybir.AxisListType.X

P = 128
B, L, D = 64, 32, 512
M = 257
H, HD = 16, 32
NK = 5
KC = D // P
HQ = P // HD
BG = 8
NG = B // BG
GT = BG * L
TT = GT // P
C = 16
DI = 4
E = 8
TAIL, HEAD = 8, 36
W = TAIL + HEAD
PAIRS = BG // 2
TILES = B * L // P
SLOTS = (B * L + E * (P - 1)) // P
EPS = 1e-5
NEG = -1e30
ATT_SCALE = float(HD) ** -0.5
MAGIC = 12582912.0

CI, CNEG, CBM, CHM, CCA, CMC = 0, P, 2 * P, 3 * P, 4 * P, 5 * P
CREF = CMC + M
CQ = CREF + 2 * NK
CONE = CQ + 1
CORD = CONE + 1
CTRI = CORD + E
CIOTA = CTRI + P
CROW = CIOTA + P
CN = CROW + TILES


def shape_constants():
    c = np.zeros((P, CN), np.float32)
    p = np.arange(P)
    c[:, CI:CI + P] = np.eye(P)
    row_b, row_h = (p // DI) % BG, p // HD
    tok_t, tok_b = p // BG, p % BG
    same = row_b[:, None] == tok_b[None, :]
    c[:, CNEG:CNEG + P] = np.where(same, 0.0, NEG)
    c[:, CBM:CBM + BG] = tok_b[:, None] == np.arange(BG)[None, :]
    c[:, CHM:CHM + P] = (p // HD)[:, None] == row_h[None, :]
    c[:, CCA:CCA + P] = (tok_b[:, None] == tok_b[None, :]) & (tok_t[:, None] <= tok_t[None, :])
    c[:, CMC:CMC + M] = ((np.arange(M) - TAIL) % M)[None, :]
    left = -NK // 2
    c[:, CREF:CREF + 2 * NK] = np.tile(np.arange(left, NK + left), 2)[None, :]
    c[:, CQ] = p % L
    c[:, CONE] = 1.0
    c[:, CORD:CORD + E] = np.arange(E, 0, -1)[None, :]
    c[:, CTRI:CTRI + P] = p[:, None] < p[None, :]
    c[:, CIOTA:CIOTA + P] = p[None, :]
    tile = np.arange(TILES)
    c[:, CROW:CROW + TILES] = (tile // TT * P + p[:, None]) * TT + tile % TT - B * L
    return c


class Count:

    def __init__(self, sem, per=1, base=None):
        self.sem, self.per = sem, per
        self.base = (32 if per == 16 else per + 1) if base is None else base

    def at(self, i, j):
        return i * self.per + j + self.base


class Round:

    def __init__(self, i, p):
        self.i, self.p, self.r = i, p, 2 * i + p

    def next(self):
        return Round(self.i + self.p, 1 - self.p)

    def prev(self):
        return Round(self.i + self.p - 1, 1 - self.p)


def rounds(eng, n, emit, start=0):
    first, p = start // 2, start % 2
    pairs = (n - start - 1) // 2
    with eng.Fori(first, first + pairs) as i:
        emit(Round(i, p), False)
        emit(Round(i, p).next(), False)
    for r in range(start + 2 * pairs, n):
        emit(Round(r // 2, r % 2), r == n - 1)


def runs(t, ahead):
    return not isinstance(t.r, int) or t.r + ahead < NG


class Chain:

    def __init__(self, eng, count, i, settle=None):
        self.eng, self.count, self.i, self.n, self.settle = eng, count, i, 0, settle

    def link(self, instruction):
        self.n += 1
        instruction.then_inc(self.count.sem, 1)
        self.eng.wait_ge(self.count.sem, self.count.at(self.i, self.n))
        if self.settle:
            self.settle(self.eng)

    def close(self):
        assert self.n == self.count.per, (self.n, self.count.per)


def bc(ap, axis, n):
    shape = list(ap.shape)
    return ap.unsqueeze(axis).broadcast_to(shape[:axis] + [n] + shape[axis:])


def act_deviation(nc, act, i, mv, rstd, var, std):
    act.wait_ge(var.sem, var.at(i, 1))
    nc.scalar.activation(rstd, mv[:, :, 1], ACT.Sqrt, bias=EPS).then_inc(std.sem, 1)


def layer_norm(nc, m, chain, x, h, stats, mv, rstd, var, std, tiles):
    for t in range(tiles):
        chain.link(nc.vector.bn_stats(stats[:, t, :], x[:, t, :]))
    m.settle(chain.eng)
    for t in range(tiles):
        last = nc.vector.bn_aggr(mv[:, t, :], stats[:, t, :])
    last.then_inc(var.sem, 1)
    chain.eng.wait_ge(std.sem, std.at(chain.i, 1))
    chain.link(nc.vector.reciprocal(rstd[:, 0:tiles], rstd[:, 0:tiles]))
    last = None
    for t in range(tiles):
        last = nc.vector.tensor_scalar(h[:, t, :], x[:, t, :], mv[:, t, 0:1], rstd[:, t:t + 1],
                                       ALU.subtract, ALU.mult)
    return last


LN_LINKS = TT + 1


class Ring:

    def __init__(self, m, name, banks, plan):
        self.ps = m.ps(name, [P, banks, 512])
        self.names = [n for n, _ in plan]
        self.reader = dict(plan)
        self.banks = banks
        assert len(self.reader) == len(plan)
        self.filled = m.count(f"{name}_filled", len(plan))
        self.read = {e: m.count(f"{name}_read_{e}", sum(r == e for _, r in plan)) for e in sorted(set(self.reader.values()))}
        for c in self.read.values():
            assert c.base >= c.per

    def bank(self, name, parts=None):
        ps = self.ps[:, self.names.index(name) % self.banks, :]
        return ps if parts is None else ps.rearrange("p (g n) -> p g n", g=parts)

    def full(self, i, name):
        return self.filled.sem, self.filled.at(i, self.names.index(name) + 1)

    def used(self, i, name):
        n, e = self.names.index(name), self.reader[name]
        return self.read[e].sem, self.read[e].at(i, sum(self.reader[x] == e for x in self.names[:n + 1]))

    def skip(self, pe, i, *names):
        sem, value = self.full(i, names[0])
        pe.wait_ge(sem, value - 1)
        for name in names:
            pe.wait_ge(*self.free(i, name))
            pe.sem_inc(self.filled.sem, 1)

    def skip_reads(self, eng, engine, i, *names):
        read = [n for n in names if self.reader[n] == engine]
        sem, value = self.used(i, read[0])
        eng.wait_ge(sem, value - 1)
        eng.sem_inc(sem, len(read))

    def free(self, i, name):
        n = self.names.index(name)
        if n >= self.banks:
            return self.used(i, self.names[n - self.banks])
        last = max(x for x in range(len(self.names)) if x % self.banks == n)
        sem, value = self.used(i, self.names[last])
        return sem, value - self.read[self.reader[self.names[last]]].per


class Mem:

    def __init__(self, nc, ctx, tag):
        self.nc, self.ctx, self.tag = nc, ctx, tag
        self.counts, self.passed = [], None

    def sb(self, name, shape, dt=F32):
        return self.ctx.enter_context(self.nc.sbuf_tensor(f"{self.tag}_{name}", shape, dt))

    def ps(self, name, shape, dt=F32):
        return self.ctx.enter_context(self.nc.psum_tensor(f"{self.tag}_psum_{name}", shape, dt))

    def count(self, name, per=1, base=None):
        self.counts.append(Count(self.ctx.enter_context(self.nc.semaphore(f"{self.tag}_sem_{name}")), per, base))
        return self.counts[-1]

    def start(self, eng):
        for c in self.counts:
            if c.base:
                eng.sem_inc(c.sem, c.base)

    def settle(self, eng):
        if self.passed is None:
            self.passed = self.ctx.enter_context(self.nc.semaphore(f"{self.tag}_sem_passed"))
        eng.sem_inc(self.passed, 1)


def project_phase(nc, a, k):
    with ExitStack() as ctx:
        m = Mem(nc, ctx, "pj")
        xs = [m.sb(f"x{p}", [P, TT, D]) for p in range(2)]
        h = m.sb("h", [P, TT, D])
        hT = [m.sb(f"hT{p}", [P, KC, GT]) for p in range(2)]
        QT = [m.sb(f"QT{p}", [P, KC, GT]) for p in range(2)]
        off = m.sb("off", [P, TT, H * NK])
        stats, mv, rstd = m.sb("st", [P, TT, 6]), m.sb("mv", [P, TT, 2]), m.sb("rs", [P, TT])
        Wq, bq = m.sb("Wq", [P, KC, D]), m.sb("bq", [P, KC])
        Woff, boff = m.sb("Woff", [P, KC, H * NK]), m.sb("boff", [P, H * NK])
        mask_i, mask_f = m.sb("mi", [B, M], I32), m.sb("mf", [B, M])
        length, length_all = m.sb("len", [B, 1]), m.sb("lena", [P, 2, B])
        span = [m.sb(f"span{j}", [P, B // 2, KC, 2 * NK]) for j in range(2)]
        t0, t1 = (m.sb(f"t{j}", [P, PAIRS * KC * 2 * NK]) for j in range(2))
        bad = m.sb("bad", [P, NG + 1])
        ps_t, ps_q, ps_o = m.ps("t", [P, TT, D]), m.ps("q", [P, KC, GT]), m.ps("o", [P, TT, H * NK])
        ps_l = m.ps("l", [P, 512])

        x_in = [m.count(f"x_in{p}", 16) for p in range(2)]
        q_out = [m.count(f"q_out{p}", 16) for p in range(2)]
        w_in, wq_in = m.count("w_in"), m.count("wq_in")
        h_done = m.count("h_done")
        tr_done, hT_done = m.count("tr"), m.count("hT", TT)
        q_done, qT_done = m.count("q"), m.count("qT", KC)
        o_done, off_done = m.count("o"), m.count("off")
        link, olink = m.count("link", LN_LINKS), m.count("olink")
        plink, slink = m.count("plink"), m.count("slink", 17)
        len_ps, len_in, bad_done, bad_ps = m.count("lps"), m.count("lin"), m.count("bd"), m.count("bp")
        flag_done, var, std = m.count("flag"), m.count("var"), m.count("std")
        block = ctx.enter_context(nc.Block())

        @block.sync
        def _(sp):
            def load(t):
                sp.wait_ge(h_done.sem, h_done.at(t.r - 1, 0))
                sp.dma_start(xs[t.p][:], a["x_tok"][bass.ds(t.r, 1)].rearrange("o t p d -> (o p) t d")).then_inc(x_in[t.p].sem, 16)

            load(Round(0, 0))
            sp.dma_start(k["const"][:], a["const"]).then_inc(w_in.sem, 16)
            load(Round(0, 1))
            sp.dma_start(Wq[:], a["xWq"]).then_inc(wq_in.sem, 16)
            sp.dma_start(bq[:], a["xbq"]).then_inc(wq_in.sem, 16)
            sp.dma_start(Woff[:], a["xWoff"]).then_inc(wq_in.sem, 16)
            sp.dma_start(boff[:], a["xboff"].partition_broadcast(P)).then_inc(wq_in.sem, 16)
            sp.dma_start(mask_i[:], a["mask"]).then_inc(wq_in.sem, 16)
            rounds(sp, NG, lambda t, last: load(t), 2)
            for name, w in k["weights"].items():
                src = a[name].partition_broadcast(P) if len(a[name].shape) == 1 else a[name]
                sp.dma_start(w[:], src).then_inc(w_in.sem, 16)
            sp.wait_ge(w_in.sem, w_in.at(0, 16 * (1 + len(k["weights"]))))

        @block.gpsimd
        def _(pool):
            m.start(pool)

        @block.vector
        def _(dve):
            def norm(t):
                chain = Chain(dve, link, t.r)
                dve.wait_ge(x_in[t.p].sem, x_in[t.p].at(t.i, 16))
                dve.wait_ge(tr_done.sem, tr_done.at(t.r, 0))
                layer_norm(nc, m, chain, xs[t.p], h, stats, mv, rstd, var, std, TT).then_inc(h_done.sem, 1)

            def offsets(t, chain):
                dve.wait_ge(o_done.sem, o_done.at(t.r, 1))
                dve.wait_ge(off_done.sem, off_done.at(t.r, 0))
                chain.link(nc.vector.tensor_tensor(off[:], ps_o[:], bc(boff[:], 1, TT), ALU.add))
                for b in range(P // L):
                    for hq in range(HQ):
                        src = off[b * L:(b + 1) * L].rearrange("p t (g h k) -> p t g h k", g=KC, h=HQ)[:, :, :, hq, :]
                        dst = k["ix"][hq * L:(hq + 1) * L, bass.ds(t.r * PAIRS, PAIRS)].rearrange(
                            "p (t u) g v k -> p t u g v k", t=TT)[:, :, b // 2, :, b % 2]
                        last = nc.vector.tensor_copy(dst, src)
                last.then_inc(off_done.sem, 1)

            def positions(t):
                step = Chain(dve, slink, t.r)
                dve.wait_ge(off_done.sem, off_done.at(t.r, 1))
                pairs = bass.ds(t.r * PAIRS, PAIRS)
                rows = k["ix"][:, pairs].rearrange("p u g v k -> p (u g) (v k)")
                ix = k["ix"][:, pairs].rearrange("p u g v k -> p (u g v k)")
                n_, rn = (full[:, pairs].rearrange("p u g v -> p (u g v)") for full in span)
                step.link(nc.vector.tensor_tensor(rows, rows, bc(k["const"][:, CREF:CREF + 2 * NK], 1, PAIRS * KC), ALU.add))
                step.link(nc.vector.tensor_scalar(ix, ix, k["const"][:, CQ:CQ + 1], None, ALU.add))
                step.link(nc.vector.tensor_tensor(t0[:], ix, rn, ALU.mult))
                step.link(nc.vector.tensor_scalar(t0[:], t0[:], MAGIC, None, ALU.add))
                step.link(nc.vector.tensor_scalar(t0[:], t0[:], -MAGIC, None, ALU.add))
                step.link(nc.vector.tensor_tensor(t0[:], t0[:], n_, ALU.mult))
                step.link(nc.vector.tensor_tensor(ix, ix, t0[:], ALU.subtract))
                step.link(nc.vector.tensor_tensor(t0[:], ix, n_, ALU.mult))
                step.link(nc.vector.tensor_scalar(t0[:], t0[:], 0.0, None, ALU.is_lt))
                step.link(nc.vector.tensor_tensor(t0[:], t0[:], n_, ALU.mult))
                step.link(nc.vector.tensor_tensor(ix, ix, t0[:], ALU.add))
                step.link(nc.vector.tensor_scalar(ix, ix, 1.0 / (M - 1), 2.0, ALU.mult, ALU.mult))
                step.link(nc.vector.tensor_scalar(ix, ix, -1.0, 1.0, ALU.add, ALU.add))
                step.link(nc.vector.tensor_scalar(ix, ix, float(M), -1.0, ALU.mult, ALU.add))
                step.link(nc.vector.tensor_scalar(ix, ix, 0.5, None, ALU.mult))
                nc.vector.tensor_scalar(t0[:], ix, float(HEAD - 1), None, ALU.is_ge)
                step.link(nc.vector.tensor_scalar(t1[:], ix, float(M - TAIL), None, ALU.is_lt))
                step.link(nc.vector.tensor_tensor(t0[:], t0[:], t1[:], ALU.mult))
                step.close()
                nc.vector.tensor_reduce(bad[:, bass.ds(t.r, 1)], t0[:], AX, ALU.max).then_inc(bad_done.sem, 1)

            def group(t, last):
                if runs(t, 2):
                    norm(t.next().next())
                offsets(t, Chain(dve, olink, t.r))
                positions(t)

            norm(Round(0, 0))
            norm(Round(0, 1))
            dve.wait_ge(wq_in.sem, wq_in.at(0, 5 * 16))
            step = Chain(dve, plink, 0)
            step.link(nc.vector.tensor_copy(mask_f[:], mask_i[:]))
            step.link(nc.vector.tensor_scalar(mask_f[:], mask_f[:], -1.0, 1.0, ALU.mult, ALU.add))
            step.link(nc.vector.tensor_reduce(length[:], mask_f[:], AX, ALU.add))
            nc.vector.tensor_scalar_add(length[:], length[:], -1.0).then_inc(len_in.sem, 1)
            dve.wait_ge(len_ps.sem, len_ps.at(0, 1))
            step.link(nc.vector.tensor_copy(length_all[:, 0, :], ps_l[:, 0:B]))
            step.link(nc.vector.reciprocal(length_all[:, 1, :], length_all[:, 0, :]))
            for j, full in enumerate(span):
                pairs = bc(length_all[:, j, :], 2, NK).rearrange("p (u v) k -> p u v k", v=2)
                for g in range(KC):
                    last = nc.vector.tensor_copy(full[:, :, g, :].rearrange("p u (v k) -> p u v k", v=2), pairs)
            step.link(last)
            rounds(dve, NG, group)
            dve.wait_ge(bad_done.sem, bad_done.at(NG, 0))
            nc.vector.tensor_reduce(bad[:, NG:NG + 1], bad[:, 0:NG], AX, ALU.max).then_inc(bad_done.sem, 1)
            dve.wait_ge(bad_ps.sem, bad_ps.at(0, 1))
            nc.vector.tensor_copy(k["flag"], ps_l[0:1, 256:257]).then_inc(flag_done.sem, 1)

        @block.tensor
        def _(pe):
            def transposes(t):
                pe.wait_ge(h_done.sem, h_done.at(t.r, 1))
                pe.wait_ge(hT_done.sem, hT_done.at(t.r, 0))
                for j in range(TT):
                    for c in range(KC):
                        last = nc.tensor.transpose(ps_t[:, j, c * P:(c + 1) * P], h[:, j, c * P:(c + 1) * P], k["ident"])
                last.then_inc(tr_done.sem, 1)

            def group(t, last):
                pe.wait_ge(hT_done.sem, hT_done.at(t.r, TT))
                pe.wait_ge(qT_done.sem, qT_done.at(t.r, 0))
                for e in range(KC):
                    for c in range(KC):
                        mm = nc.tensor.matmul(ps_q[:, e, :], Wq[:, c, e * P:(e + 1) * P], hT[t.p][:, c, :],
                                              start=(c == 0), stop=(c == KC - 1))
                mm.then_inc(q_done.sem, 1)
                if not last:
                    transposes(t.next())
                pe.wait_ge(qT_done.sem, qT_done.at(t.r, KC))
                pe.wait_ge(off_done.sem, off_done.at(t.r, 0))
                for j in range(TT):
                    for c in range(KC):
                        mm = nc.tensor.matmul(ps_o[:, j, :], QT[t.p][:, c, j * P:(j + 1) * P], Woff[:, c, :],
                                              start=(c == 0), stop=(c == KC - 1))
                mm.then_inc(o_done.sem, 1)

            pe.wait_ge(w_in.sem, w_in.at(0, 16))
            transposes(Round(0, 0))
            pe.wait_ge(wq_in.sem, wq_in.at(0, 5 * 16))
            pe.wait_ge(len_in.sem, len_in.at(0, 1))
            nc.tensor.matmul(ps_l[:, 0:B], length[:].broadcast_to([B, P]), k["const"][0:B, CI:CI + B],
                             start=True, stop=True).then_inc(len_ps.sem, 1)
            rounds(pe, NG, group)
            pe.wait_ge(bad_done.sem, bad_done.at(NG, 1))
            nc.tensor.matmul(ps_l[0:1, 256:257], bad[:, NG:NG + 1], k["ones"], start=True, stop=True).then_inc(bad_ps.sem, 1)

        @block.scalar
        def _(act):
            def deviation(t):
                act_deviation(nc, act, t.r, mv, rstd[:], var, std)

            def turned(t):
                act.wait_ge(tr_done.sem, tr_done.at(t.r, 1))
                act.wait_ge(q_done.sem, q_done.at(t.r - 1, 0))
                for j in range(TT):
                    nc.scalar.activation(hT[t.p][:, :, j * P:(j + 1) * P], ps_t[:, j, :].rearrange("p (c n) -> p c n", c=KC),
                                         ACT.Copy).then_inc(hT_done.sem, 1)

            def group(t, last):
                act.wait_ge(q_done.sem, q_done.at(t.r, 1))
                act.wait_ge(q_out[t.p].sem, q_out[t.p].at(t.i, 0))
                act.wait_ge(o_done.sem, o_done.at(t.r - 1, 0))
                for e in range(KC):
                    nc.scalar.activation(QT[t.p][:, e, :], ps_q[:, e, :], ACT.Identity,
                                         bias=bq[:, e:e + 1]).then_inc(qT_done.sem, 1)
                if not last:
                    turned(t.next())
                if runs(t, 2):
                    deviation(t.next().next())
                act.wait_ge(qT_done.sem, qT_done.at(t.r, KC))
                act.dma_start(a["q_scr"][bass.ds(t.r, 1)].rearrange("o p k t -> (o p) k t"), QT[t.p][:]).then_inc(q_out[t.p].sem, 16)

            deviation(Round(0, 0))
            turned(Round(0, 0))
            deviation(Round(0, 1))
            act.wait_ge(wq_in.sem, wq_in.at(0, 5 * 16))
            rounds(act, NG, group)
            for q in q_out:
                act.wait_ge(q.sem, q.at(NG // 2, 0))


class Interpolation:

    def __init__(self, m, nu, wr, ring, stride):
        self.nu, self.wr = nu, wr
        self.tent = [m.sb(f"tent{r}", [P, nu * NK, wr]) for r in range(ring)]
        self.prod = m.sb("prod", [P, nu * NK, wr])
        self.wtent = m.sb("wtent", [P, nu * NK, wr])
        self.A = m.sb("A", [P, nu, stride])
        self.s = m.sb("s", [P, nu, NK])
        self.e = m.sb("e", [P, nu, NK])
        self.top, self.tot = m.sb("top", [P, nu]), m.sb("tot", [P, nu])

    def pool_difference(self, nc, r, rows, ix):
        return nc.gpsimd.tensor_tensor(self.tent[r][:], bc(rows, 1, self.nu * NK), bc(ix, 2, self.wr), ALU.subtract)

    def act_abs(self, nc, r):
        return nc.scalar.activation(self.tent[r][:], self.tent[r][:], ACT.Abs)

    def act_tent(self, nc, r):
        return nc.scalar.activation(self.tent[r][:], self.tent[r][:], ACT.Relu, bias=1.0, scale=-1.0)

    def dve_scores(self, nc, chain, r, S):
        v = "p (u k) m -> p u k m"
        chain.link(nc.vector.tensor_tensor(self.prod[:].rearrange(v, k=NK), self.tent[r][:].rearrange(v, k=NK),
                                           bc(S, 2, NK), ALU.mult))
        chain.link(nc.vector.tensor_reduce(self.s[:].rearrange("p u k -> p (u k)"), self.prod[:], AX, ALU.add))
        chain.link(nc.vector.tensor_reduce(self.top[:], self.s[:], AX, ALU.max))
        return nc.vector.tensor_tensor(self.s[:], self.s[:], bc(self.top[:], 2, NK), ALU.subtract)

    def act_exp(self, nc):
        return nc.scalar.activation(self.e[:], self.s[:], ACT.Exp, scale=0.5 * ATT_SCALE)

    def dve_softmax(self, nc, chain):
        chain.link(nc.vector.tensor_reduce(self.tot[:], self.e[:], AX, ALU.add))
        chain.link(nc.vector.reciprocal(self.tot[:], self.tot[:]))
        return nc.vector.scalar_tensor_tensor(self.e[:], self.e[:], 0.5, bc(self.tot[:], 2, NK), ALU.mult, ALU.mult)

    def weigh(self, eng, r):
        return eng.tensor_tensor(self.wtent[:], self.tent[r][:], bc(self.e[:].rearrange("p u k -> p (u k)"), 2, self.wr),
                                 ALU.mult)

    def dve_sum(self, nc):
        return nc.vector.tensor_reduce(self.A[:, :, 0:self.wr], self.wtent[:].rearrange("p (u k) m -> p u m k", k=NK), AX, ALU.add)

    def dve_weights(self, nc, chain, r):
        chain.link(self.dve_softmax(nc, chain))
        chain.link(self.weigh(nc.vector, r))
        return self.dve_sum(nc)

    DVE_LINKS = 3 + 4


def attend_window_phase(nc, a, k):
    U = 2 * KC
    with ExitStack() as ctx:
        m = Mem(nc, ctx, "aw")
        two = range(2)
        craw = m.sb("craw", [P, KC, W * BG])
        cw = [m.sb(f"c{p}", [P, KC, BG, 64]) for p in two]
        Qblk = [m.sb(f"Qb{p}", [P, KC, BG, P]) for p in two]
        KT, V = [m.sb(f"K{p}", [P, KC, BG, W]) for p in two], [m.sb(f"V{p}", [P, PAIRS, D]) for p in two]
        AT, cT = m.sb("AT", [P, KC, P]), [m.sb(f"cT{p}", [P, KC, GT]) for p in two]
        Wk, Wv, bk, bv = (k["weights"][n] for n in ("xWk", "xWv", "xbk", "xbv"))
        ip = Interpolation(m, U, W, 2, 64)
        ps_kv, ps_s = m.ps("kv", [P, 2, 512]), m.ps("s", [P, 2, 512])
        ps_at, ps_av = m.ps("at", [P, KC, P]), m.ps("av", [P, 2, KC, P])

        c_in = m.count("c_in", 16)
        q_in = [m.count(f"q_in{p}", 16 * HQ) for p in two]
        c_out = [m.count(f"c_out{p}", 16) for p in two]
        zero, cw_done = m.count("zero"), m.count("cw")
        k_ps, k_cp = m.count("k_ps", KC), m.count("k_cp", KC)
        v_ps, v_cp = m.count("v_ps", PAIRS), m.count("v_cp", PAIRS)
        s_ps = m.count("s_ps", PAIRS)
        diff, ab, tent = m.count("diff", PAIRS), m.count("ab", PAIRS), m.count("tent", PAIRS)
        sc_done, ex_done = m.count("sc", PAIRS), m.count("ex", PAIRS)
        wt_done, wp_done = m.count("wt", PAIRS), m.count("wp", PAIRS)
        A_done, at_ps, at_cp = m.count("A", PAIRS), m.count("at_ps", PAIRS), m.count("at_cp", PAIRS)
        av_ps, av_cp = m.count("av_ps", PAIRS), m.count("av_cp", PAIRS)
        av_ps.base = 2 * PAIRS + 1
        link, xlink = m.count("link", 3), m.count("xlink", 2)
        block = ctx.enter_context(nc.Block())

        @block.sync
        def _(sp):
            def load(t, last=False):
                sp.wait_ge(cw_done.sem, cw_done.at(t.r, 0))
                sp.dma_start(craw[:], a["ctx"][bass.ds(t.r, 1), :, :, 0:W * BG].rearrange("o p c w -> (o p) c w")).then_inc(c_in.sem, 16)
                if isinstance(t.r, int) and t.r == 0:
                    sp.wait_ge(zero.sem, zero.at(0, 5))
                sp.wait_ge(s_ps.sem, s_ps.at(t.r - 1, 0))
                for hq in range(HQ):
                    rows = slice(hq * HD, (hq + 1) * HD)
                    sp.dma_start(Qblk[t.p][rows, :, :, hq * L:(hq + 1) * L],
                                 a["q_scr"][bass.ds(t.r, 1), rows].rearrange("o p k (b q) -> (o p) k b q", q=L)
                                 ).then_inc(q_in[t.p].sem, 16)

            load(Round(0, 0))
            rounds(sp, NG, load, 1)

        @block.gpsimd
        def _(pool):
            m.start(pool)
            for buf in (*(c[:, :, :, W:] for c in cw), Qblk[1][:], ip.A[:]):
                nc.gpsimd.memset(buf, 0.0).then_inc(zero.sem, 1)
            pool.wait_ge(zero.sem, zero.at(0, 5))

            def reorder(t):
                pool.wait_ge(c_in.sem, c_in.at(t.r, 16))
                pool.wait_ge(v_ps.sem, v_ps.at(t.r - 1, 0))
                m.settle(pool)
                nc.gpsimd.tensor_copy(cw[t.p][:, :, :, 0:W], craw[:].rearrange("p c (m b) -> p c b m", b=BG)).then_inc(cw_done.sem, 1)

            def difference(t, j):
                pool.wait_ge(wp_done.sem, wp_done.at(t.r, j - 1))
                ix = k["ix"][:, bass.ds(t.r * PAIRS + j, 1)].rearrange("p u g v k -> p (u g v k)")
                ip.pool_difference(nc, j % 2, k["const"][:, CMC:CMC + W], ix).then_inc(diff.sem, 1)

            def group(t, last):
                for j in range(PAIRS):
                    pool.wait_ge(wt_done.sem, wt_done.at(t.r, j + 1))
                    pool.wait_ge(A_done.sem, A_done.at(t.r, j))
                    m.settle(pool)
                    ip.weigh(nc.gpsimd, j % 2).then_inc(wp_done.sem, 1)
                    if j + 2 < PAIRS:
                        difference(t, j + 2)
                    elif not last:
                        difference(t.next(), j + 2 - PAIRS)
                    if j == 0 and not last:
                        reorder(t.next())

            difference(Round(0, 0), 0)
            difference(Round(0, 0), 1)
            rounds(pool, NG, group)

        @block.vector
        def _(dve):
            def values(t, j):
                dve.wait_ge(v_ps.sem, v_ps.at(t.r, j + 1))
                dve.wait_ge(av_ps.sem, av_ps.at(t.r - 1, j + 1 - PAIRS))
                nc.vector.tensor_tensor(V[t.p][:, j, :], ps_kv[:, j % 2, :], bv[:], ALU.add).then_inc(v_cp.sem, 1)

            def scores(t, j):
                dve.wait_ge(s_ps.sem, s_ps.at(t.r, j + 1))
                dve.wait_ge(tent.sem, tent.at(t.r, j + 1))
                S = ps_s[:, j % 2, 0:U * W].rearrange("p (u m) -> p u m", m=W)
                ip.dve_scores(nc, Chain(dve, link, t.r * PAIRS + j), j % 2, S).then_inc(sc_done.sem, 1)

            def group(t, last):
                for j in range(PAIRS):
                    dve.wait_ge(ex_done.sem, ex_done.at(t.r, j + 1))
                    ip.dve_softmax(nc, Chain(dve, xlink, t.r * PAIRS + j)).then_inc(wt_done.sem, 1)
                    if j + 1 < PAIRS:
                        scores(t, j + 1)
                    elif not last:
                        scores(t.next(), 0)
                    for v in ((1, 2), (3,), (), ())[j]:
                        values(t, v)
                    if j == PAIRS - 1 and not last:
                        values(t.next(), 0)
                    dve.wait_ge(wp_done.sem, wp_done.at(t.r, j + 1))
                    dve.wait_ge(at_ps.sem, at_ps.at(t.r, j))
                    ip.dve_sum(nc).then_inc(A_done.sem, 1)

            nc.vector.memset(Qblk[0][:], 0.0).then_inc(zero.sem, 1)
            dve.wait_ge(c_in.sem, c_in.at(0, 16))
            nc.vector.tensor_copy(cw[0][:, :, :, 0:W], craw[:].rearrange("p c (m b) -> p c b m", b=BG)).then_inc(cw_done.sem, 1)
            values(Round(0, 0), 0)
            scores(Round(0, 0), 0)
            rounds(dve, NG, group)

        @block.tensor
        def _(pe):
            def keys(t, e):
                pe.wait_ge(v_cp.sem, v_cp.at(t.r, 0))
                pe.wait_ge(k_cp.sem, k_cp.at(t.r, max(e - 1, 0)))
                for c in range(KC):
                    mm = nc.tensor.matmul(ps_kv[:, e % 2, 0:W * BG], Wk[:, c, e * P:(e + 1) * P], cw[t.p][:, c, :, 0:W],
                                          start=(c == 0), stop=(c == KC - 1))
                mm.then_inc(k_ps.sem, 1)

            def values(t, j):
                if j < 2:
                    pe.wait_ge(k_cp.sem, k_cp.at(t.r, KC - 1 + j))
                else:
                    pe.wait_ge(v_cp.sem, v_cp.at(t.r, j - 1))
                for c in range(KC):
                    rows = cw[t.p][:, c, 2 * j:2 * j + 2, :].rearrange("p b m -> p (b m)")
                    mm = nc.tensor.matmul(ps_kv[:, j % 2, :], rows, Wv[:, c, :], start=(c == 0), stop=(c == KC - 1))
                mm.then_inc(v_ps.sem, 1)

            def scores(t, j):
                if j == 0:
                    pe.wait_ge(q_in[t.p].sem, q_in[t.p].at(t.i, 16 * HQ))
                pe.wait_ge(k_cp.sem, k_cp.at(t.r, KC))
                pe.wait_ge(sc_done.sem, sc_done.at(t.r, j - 1))
                for u in range(U):
                    b, g = 2 * j + u % 2, u // 2
                    mm = nc.tensor.matmul(ps_s[:, j % 2, u * W:(u + 1) * W], Qblk[t.p][:, g, b, :], KT[t.p][:, g, b, :],
                                          start=True, stop=True)
                mm.then_inc(s_ps.sem, 1)

            def turn(t, j):
                pe.wait_ge(A_done.sem, A_done.at(t.r, j + 1))
                pe.wait_ge(at_cp.sem, at_cp.at(t.r, j))
                for g in range(KC):
                    mm = nc.tensor.transpose(ps_at[:, g, :], ip.A[:, 2 * g:2 * g + 2, :].rearrange("p b m -> p (b m)"),
                                             k["ident"])
                mm.then_inc(at_ps.sem, 1)

            def context(t, j):
                pe.wait_ge(at_cp.sem, at_cp.at(t.r, j + 1))
                pe.wait_ge(v_cp.sem, v_cp.at(t.r, j + 1))
                pe.wait_ge(av_cp.sem, av_cp.at(t.r, j))
                for u in range(U):
                    b, g = u % 2, u // 2
                    rows = slice(b * 64, b * 64 + W)
                    mm = nc.tensor.matmul(ps_av[:, b, g, :], V[t.p][rows, j, g * P:(g + 1) * P], AT[rows, g, :],
                                          start=True, stop=True)
                mm.then_inc(av_ps.sem, 1)

            def group(t, last):
                n = t.next()
                for j in range(PAIRS):
                    turn(t, j)
                    if j + 2 < PAIRS:
                        scores(t, j + 2)
                    elif not last:
                        scores(n, j + 2 - PAIRS)
                    context(t, j)
                    if not last:
                        if j == 0:
                            pe.wait_ge(cw_done.sem, cw_done.at(n.r, 1))
                        for e in (2 * j, 2 * j + 1):
                            keys(n, e) if e < KC else values(n, e - KC)

            pe.wait_ge(zero.sem, zero.at(0, 5))
            first = Round(0, 0)
            pe.wait_ge(cw_done.sem, cw_done.at(0, 1))
            for e in range(KC):
                keys(first, e)
            values(first, 0)
            values(first, 1)
            scores(first, 0)
            scores(first, 1)
            values(first, 2)
            values(first, 3)
            rounds(pe, NG, group)

        @block.scalar
        def _(act):
            def keys(t, e):
                act.wait_ge(k_ps.sem, k_ps.at(t.r, e + 1))
                act.wait_ge(s_ps.sem, s_ps.at(t.r - 1, 0))
                nc.scalar.activation(KT[t.p][:, e], ps_kv[:, e % 2, 0:W * BG].rearrange("p (b m) -> p b m", b=BG),
                                     ACT.Identity, bias=bk[:, e:e + 1]).then_inc(k_cp.sem, 1)

            def tents(t, j):
                act.wait_ge(diff.sem, diff.at(t.r, j + 1))
                ip.act_abs(nc, j % 2).then_inc(ab.sem, 1)
                act.wait_ge(ab.sem, ab.at(t.r, j + 1))
                ip.act_tent(nc, j % 2).then_inc(tent.sem, 1)

            def weights(t, j):
                act.wait_ge(sc_done.sem, sc_done.at(t.r, j + 1))
                act.wait_ge(wp_done.sem, wp_done.at(t.r, j))
                ip.act_exp(nc).then_inc(ex_done.sem, 1)

            def group(t, last):
                n = t.next()
                for j in range(PAIRS):
                    if j in (1, 2) and not last:
                        keys(n, 2 * j - 2)
                        keys(n, 2 * j - 1)
                    act.wait_ge(at_ps.sem, at_ps.at(t.r, j + 1))
                    act.wait_ge(av_ps.sem, av_ps.at(t.r, j))
                    nc.scalar.activation(AT[:], ps_at[:], ACT.Copy).then_inc(at_cp.sem, 1)
                    if j + 2 < PAIRS:
                        weights(t, j + 2)
                    elif not last:
                        weights(n, j + 2 - PAIRS)
                    act.wait_ge(av_ps.sem, av_ps.at(t.r, j + 1))
                    if j == 0:
                        act.wait_ge(c_out[t.p].sem, c_out[t.p].at(t.i, 0))
                    for hq in range(HQ):
                        rows = slice(hq * HD, (hq + 1) * HD)
                        mm = nc.scalar.activation(
                            cT[t.p][rows].rearrange("p c (q b) -> p b c q", b=BG)[:, 2 * j:2 * j + 2],
                            ps_av[rows, :, :, hq * L:(hq + 1) * L], ACT.Copy)
                    mm.then_inc(av_cp.sem, 1)
                    if j + 3 < PAIRS:
                        tents(t, j + 3)
                    elif not last:
                        tents(n, j + 3 - PAIRS)
                act.wait_ge(av_cp.sem, av_cp.at(t.r, PAIRS))
                act.dma_start(a["c_scr"][bass.ds(t.r, 1)].rearrange("o p k t -> (o p) k t"), cT[t.p][:]).then_inc(c_out[t.p].sem, 16)

            for e in range(KC):
                keys(Round(0, 0), e)
            tents(Round(0, 0), 0)
            tents(Round(0, 0), 1)
            weights(Round(0, 0), 0)
            weights(Round(0, 0), 1)
            tents(Round(0, 0), 2)
            rounds(act, NG, group)
            for c in c_out:
                act.wait_ge(c.sem, c.at(NG // 2, 0))


def attend_all_phase(nc, a, k):
    MT = [(0, P), (P, P), (2 * P, M - 2 * P)]
    with ExitStack() as ctx:
        m = Mem(nc, ctx, "aa")
        craw, cb = m.sb("craw", [P, KC, M * BG]), m.sb("cb", [P, KC, M])
        Q, Qblk = m.sb("Q", [P, KC, GT]), m.sb("Qb", [P, KC, P])
        KT, V = m.sb("K", [P, KC, M]), m.sb("V", [P, len(MT), D])
        AT, cT = m.sb("AT", [P, len(MT), P]), m.sb("cT", [P, KC, GT])
        Wk, Wv, bk, bv = (k["weights"][n] for n in ("xWk", "xWv", "xbk", "xbv"))
        ip = Interpolation(m, 1, M, 1, M)
        ps, ps_at, ps_av = m.ps("big", [P, KC, 512]), m.ps("at", [P, len(MT), P]), m.ps("av", [P, 512])

        c_in, q_in, c_out = m.count("c_in", 16), m.count("q_in", 16), m.count("c_out", 16)
        zero, cb_done, qb_done = m.count("zero"), m.count("cb"), m.count("qb")
        k_ps, k_cp, v_ps, v_cp, s_ps = m.count("kp"), m.count("kc"), m.count("vp"), m.count("vc"), m.count("sp")
        diff, ab, tent = m.count("diff", KC), m.count("ab", KC), m.count("tent", KC)
        sc_done, ex_done, A_done = m.count("sc", KC), m.count("ex", KC), m.count("A", KC)
        at_ps, at_cp, av_ps, av_cp = m.count("atp", KC), m.count("atc", KC), m.count("avp", KC), m.count("avc", KC)
        link, plink = m.count("link", KC * ip.DVE_LINKS), m.count("plink", HQ)
        block = ctx.enter_context(nc.Block())

        @block.sync
        def _(sp):
            with sp.Fori(0, NG) as i:
                sp.wait_ge(av_cp.sem, av_cp.at(i * BG, 0))
                sp.dma_start(craw[:], a["ctx"][bass.ds(i, 1)].rearrange("o p c w -> (o p) c w")).then_inc(c_in.sem, 16)
                sp.dma_start(Q[:], a["q_scr"][bass.ds(i, 1)].rearrange("o p k t -> (o p) k t")).then_inc(q_in.sem, 16)
                sp.wait_ge(av_cp.sem, av_cp.at(i * BG + BG, 0))
                sp.dma_start(a["c_scr"][bass.ds(i, 1)].rearrange("o p k t -> (o p) k t"), cT[:]).then_inc(c_out.sem, 16)
            sp.wait_ge(c_out.sem, c_out.at(NG, 0))

        @block.gpsimd
        def _(pool):
            m.start(pool)
            nc.gpsimd.memset(Qblk[:], 0.0).then_inc(zero.sem, 1)
            pool.wait_ge(zero.sem, zero.at(0, 1))
            with pool.Fori(0, NG) as i:
                pool.wait_ge(q_in.sem, q_in.at(i, 16))
                m.settle(pool)
                with pool.Fori(0, PAIRS) as u:
                    for v in range(2):
                        r = i * BG + u * 2 + v
                        pool.wait_ge(s_ps.sem, s_ps.at(r, 0))
                        m.settle(pool)
                        steps = Chain(pool, plink, r, m.settle)
                        for hq in range(HQ):
                            rows = slice(hq * HD, hq * HD + HD)
                            steps.link(nc.gpsimd.tensor_copy(Qblk[rows, :, hq * L:(hq + 1) * L],
                                                             Q[rows, :, bass.ds(u * 2 * L + v * L, L)]))
                        pool.sem_inc(qb_done.sem, 1)
                        for g in range(KC):
                            pool.wait_ge(A_done.sem, A_done.at(r, g))
                            ix = k["ix"][:, bass.ds(i * PAIRS + u, 1), g, v, :].rearrange("p b k -> p (b k)")
                            ip.pool_difference(nc, 0, k["const"][:, CMC:CMC + M], ix).then_inc(diff.sem, 1)
                            pool.wait_ge(diff.sem, diff.at(r, g + 1))

        @block.vector
        def _(dve):
            with dve.Fori(0, B) as r:
                chain = Chain(dve, link, r)
                dve.wait_ge(v_ps.sem, v_ps.at(r, 1))
                for t, (_, n) in enumerate(MT):
                    last = nc.vector.tensor_tensor(V[0:n, t, :], ps[0:n, t, :], bv[0:n, :], ALU.add)
                last.then_inc(v_cp.sem, 1)
                for g in range(KC):
                    dve.wait_ge(s_ps.sem, s_ps.at(r, 1))
                    dve.wait_ge(tent.sem, tent.at(r, g + 1))
                    dve.wait_ge(A_done.sem, A_done.at(r, g))
                    ip.dve_scores(nc, chain, 0, ps[:, g:g + 1, 0:M]).then_inc(sc_done.sem, 1)
                    dve.wait_ge(ex_done.sem, ex_done.at(r, g + 1))
                    dve.wait_ge(at_ps.sem, at_ps.at(r, g))
                    ip.dve_weights(nc, chain, 0).then_inc(A_done.sem, 1)
                chain.close()

        @block.tensor
        def _(pe):
            with pe.Fori(0, B) as r:
                pe.wait_ge(cb_done.sem, cb_done.at(r, 1))
                pe.wait_ge(sc_done.sem, sc_done.at(r, 0))
                for e in range(KC):
                    for c in range(KC):
                        last = nc.tensor.matmul(ps[:, e, 0:M], Wk[:, c, e * P:(e + 1) * P], cb[:, c, :],
                                                start=(c == 0), stop=(c == KC - 1))
                last.then_inc(k_ps.sem, 1)
                pe.wait_ge(k_cp.sem, k_cp.at(r, 1))
                for t, (at, n) in enumerate(MT):
                    for c in range(KC):
                        last = nc.tensor.matmul(ps[0:n, t, :], cb[:, c, at:at + n], Wv[:, c, :],
                                                start=(c == 0), stop=(c == KC - 1))
                last.then_inc(v_ps.sem, 1)
                pe.wait_ge(v_cp.sem, v_cp.at(r, 1))
                pe.wait_ge(qb_done.sem, qb_done.at(r, 1))
                for g in range(KC):
                    last = nc.tensor.matmul(ps[:, g, 0:M], Qblk[:, g, :], KT[:, g, :], start=True, stop=True)
                last.then_inc(s_ps.sem, 1)
                for g in range(KC):
                    pe.wait_ge(A_done.sem, A_done.at(r, g + 1))
                    pe.wait_ge(at_cp.sem, at_cp.at(r, g))
                    for t, (at, n) in enumerate(MT):
                        last = nc.tensor.transpose(ps_at[0:n, t, :], ip.A[:, 0, at:at + n], k["ident"])
                    last.then_inc(at_ps.sem, 1)
                    pe.wait_ge(at_cp.sem, at_cp.at(r, g + 1))
                    pe.wait_ge(av_cp.sem, av_cp.at(r, g))
                    for t, (_, n) in enumerate(MT):
                        last = nc.tensor.matmul(ps_av[:, 0:P], V[0:n, t, g * P:(g + 1) * P], AT[0:n, t, :],
                                                start=(t == 0), stop=(t == len(MT) - 1))
                    last.then_inc(av_ps.sem, 1)

        @block.scalar
        def _(act):
            with act.Fori(0, NG) as i:
                act.wait_ge(c_in.sem, c_in.at(i, 16))
                act.wait_ge(c_out.sem, c_out.at(i, 0))
                with act.Fori(0, BG) as b:
                    r = i * BG + b
                    act.wait_ge(v_ps.sem, v_ps.at(r, 0))
                    raw = craw[:].rearrange("p c (m b) -> p c m b", b=BG)[:, :, :, bass.ds(b, 1)]
                    nc.scalar.activation(cb[:].unsqueeze(3), raw, ACT.Copy).then_inc(cb_done.sem, 1)
                    act.wait_ge(k_ps.sem, k_ps.at(r, 1))
                    act.wait_ge(s_ps.sem, s_ps.at(r, 0))
                    for e in range(KC):
                        last = nc.scalar.activation(KT[:, e, :], ps[:, e, 0:M], ACT.Identity, bias=bk[:, e:e + 1])
                    last.then_inc(k_cp.sem, 1)
                    for g in range(KC):
                        act.wait_ge(diff.sem, diff.at(r, g + 1))
                        ip.act_abs(nc, 0).then_inc(ab.sem, 1)
                        act.wait_ge(ab.sem, ab.at(r, g + 1))
                        ip.act_tent(nc, 0).then_inc(tent.sem, 1)
                        act.wait_ge(sc_done.sem, sc_done.at(r, g + 1))
                        ip.act_exp(nc).then_inc(ex_done.sem, 1)
                        act.wait_ge(at_ps.sem, at_ps.at(r, g + 1))
                        act.wait_ge(av_ps.sem, av_ps.at(r, g))
                        nc.scalar.activation(AT[:, 0:2, :], ps_at[:, 0:2, :], ACT.Copy)
                        nc.scalar.activation(AT[0:1, 2, :], ps_at[0:1, 2, :], ACT.Copy).then_inc(at_cp.sem, 1)
                        act.wait_ge(av_ps.sem, av_ps.at(r, g + 1))
                        for hq in range(HQ):
                            rows = slice(hq * HD, (hq + 1) * HD)
                            last = nc.scalar.activation(cT[rows, g, :].rearrange("p (q b) -> p q b", b=BG)[:, :, bass.ds(b, 1)],
                                                        ps_av[rows, hq * L:(hq + 1) * L].unsqueeze(2),
                                                        ACT.Copy)
                        last.then_inc(av_cp.sem, 1)


FRONT = ([("y0", "dve"), ("y1", "dve"), ("t0", "act"), ("t1", "act")]
         + [(f"q{e}", "dve") for e in range(KC)] + [("lr", "dve")] + [(f"{n}{e}", "dve") for n in "kv" for e in range(KC)])


LINKS = 2 * (2 + 4) + 2 * 4
BEGIN = [("sk0", "dve"), ("sq0", "dve"), ("vt0", "act"), ("kt0", "act"), ("si0", "dve")]
END = [("khT1", "act"), ("qhT1", "act")] + [(f"qk1{h}", "dve") for h in range(HQ)] + [("o1", "act")]
TURN = [("khT0", "act"), ("qhT0", "act")]
LEAVE = [("z0", "dve"), ("z1", "dve")]
BACK = (BEGIN + END + TURN + LEAVE + [("up", "dve")] + [(f"qk0{h}", "dve") for h in range(HQ)]
        + [("so0", "dve"), ("ti0", "act"), ("to0", "act"), ("o0", "act"), ("gi0", "dve"), ("go0", "dve"),
           ("si1", "dve"), ("so1", "dve"), ("ti1", "act"), ("to1", "act"), ("gi1", "dve"), ("go1", "dve"),
           ("sk1", "dve"), ("sq1", "dve"), ("vt1", "act"), ("wo", "act")])
BEGIN, END, TURN, LEAVE = ([n for n, _ in part] for part in (BEGIN, END, TURN, LEAVE))


def fast_phase(nc, a, k):
    S2 = 2 * KC
    FIRST, LAST = (Round(r // 2, r % 2) for r in (0, NG - 1))
    with ExitStack() as ctx:
        m = Mem(nc, ctx, "fw")
        front, back = Ring(m, "front", 4, FRONT), Ring(m, "back", 4, BACK)
        cT, xs = m.sb("cT", [P, KC, GT]), m.sb("x", [P, TT, D])
        x1 = [m.sb(f"x1{p}", [P, TT, D]) for p in range(2)]
        h, x2 = m.sb("h", [P, TT, D]), m.sb("x2", [P, TT, D])
        stats, mv, rstd = m.sb("st", [P, TT, 6]), m.sb("mv", [P, TT, 2]), m.sb("rs", [P, TT])
        hT, hx = m.sb("hT", [P, KC, GT]), m.sb("hx", [P, KC, P])
        f = [{n: m.sb(f"{n}T{p}", [P, KC, GT]) for n in "qkv"} for p in range(2)]
        lr = m.sb("lr", [P, 3, 2 * H])
        lrs = [m.sb(f"lrs{p}", [P, 3, 2 * H]) for p in range(2)]
        lrf = [m.sb(f"lrf{p}", [P, KC, 2]) for p in range(2)]
        chunks = range(L // C)
        vt, kt = [m.sb(f"vt{c}", [P, KC, P]) for c in chunks], m.sb("kt", [P, KC, P])
        e, top, tot = [m.sb(f"e{c}", [P, 2, 512]) for c in chunks], m.sb("top", [P, 2, P]), m.sb("tot", [P, 2, P])
        khT, qhT = ([m.sb(f"{n}{c}", [P, KC, P]) for c in chunks] for n in ("khT", "qhT"))
        qk = m.sb("qk", [P, HQ, KC, P])
        oT = m.sb("oT", [P, KC, GT])
        win0, wout0, wrow0 = m.sb("win0", [P, KC, P]), m.sb("wout0", [P, KC, P]), m.sb("wrow0", [P, KC, P])
        win, wout, wrow = m.sb("win", [P, KC, P]), m.sb("wout", [P, KC, P]), m.sb("wrow", [P, KC, P])
        grad = m.sb("grad", [P, 2, 512])
        at, atT = m.sb("at", [P, 2, KC, P]), m.sb("atT", [P, 2, KC, P])
        atop, asum = m.sb("atop", [P, S2]), m.sb("asum", [P, S2])
        w = k["weights"]
        Wo, Wp, Wo2, Wlr = w["xWo"], {n: w[f"aW{n}"] for n in "qkv"}, w["aWo"], w["aWlr"]
        bo, conv, wi, wt, wr = w["xbo"], w["conv"], w["aWin"], w["aWout"], w["aWout_rows"]
        wsum = m.sb("wsum", [P, 3, KC])
        const = k["const"]
        neg, own = const[:, CNEG:CNEG + P], const[:, CBM:CBM + BG]
        head, causal = const[:, CHM:CHM + P], const[:, CCA:CCA + P]

        c_in, x_in, x_out = m.count("c_in", 16), m.count("x_in", 16), m.count("x_out", 16)
        setup = m.count("setup")
        x1_done, h_done, var, std = m.count("x1"), m.count("h"), m.count("var"), m.count("std")
        hT_done, hx_done = m.count("hT"), m.count("hx")
        base_done, conv_done = m.count("base", 3 * KC), m.count("conv", 3 * KC)
        z_done, za, ze, zp, zl, lr_done = (m.count(n) for n in ("z", "za", "ze", "zp", "zl", "lrd"))
        flink, clink, rlink = m.count("flink", LN_LINKS + 1), m.count("clink", 3 * KC * 2), m.count("rlink")
        d_done, e_done, p_done = m.count("d", 2), m.count("e", 2), m.count("p", 2)
        qk_done = m.count("qkd", 2)
        s_done, a_done, n_done, w_done = m.count("s", 2), m.count("a", 2), m.count("n", 2), m.count("w", 3)
        x2_done, kept = m.count("x2"), m.count("kept")
        link, slink = m.count("link", LINKS), m.count("slink", 3)
        block = ctx.enter_context(nc.Block())

        @block.sync
        def _(sp):
            def load(t):
                sp.wait_ge(x1_done.sem, x1_done.at(t.r, 0))
                sp.dma_start(cT[:], a["c_scr"][bass.ds(t.r, 1)].rearrange("o p k t -> (o p) k t")).then_inc(c_in.sem, 16)
                sp.dma_start(xs[:], a["x_lb"][bass.ds(t.r, 1)].rearrange("o p t d -> (o p) t d")).then_inc(x_in.sem, 16)

            def store(t):
                sp.wait_ge(x2_done.sem, x2_done.at(t.r, 1))
                sp.dma_start(a["x2_scr"][bass.ds(t.r, 1)].rearrange("o p t d -> (o p) t d"), x2[:]).then_inc(x_out.sem, 16)

            def group(t, last):
                if not last:
                    load(t.next())
                store(t.prev())

            load(FIRST)
            load(FIRST.next())
            rounds(sp, NG, group, 1)
            store(LAST)
            sp.wait_ge(x_out.sem, x_out.at(NG, 0))

        @block.gpsimd
        def _(pool):
            m.start(pool)

            def first_tokens(i):
                pool.wait_ge(hT_done.sem, hT_done.at(i, 1))
                pool.wait_ge(*front.full(i, "y0"))
                m.settle(pool)
                for c in range(KC):
                    src = bc(bc(hT[:, c, 0:BG], 1, HQ), 3, DI)
                    last = nc.gpsimd.tensor_copy(hx[:, c, :].rearrange("p (h b d) -> p h b d", h=HQ, b=BG), src)
                last.then_inc(hx_done.sem, 1)

            def keep(t):
                pool.wait_ge(x1_done.sem, x1_done.at(t.r, 1))
                pool.wait_ge(x_out.sem, x_out.at(t.r, 0))
                m.settle(pool)
                nc.gpsimd.tensor_copy(x2[:], x1[t.p][:]).then_inc(kept.sem, 1)

            def group(t, last):
                keep(t.prev())
                if not last:
                    first_tokens(t.next().r)

            first_tokens(0)
            first_tokens(1)
            rounds(pool, NG, group, 1)
            keep(LAST)

        @block.vector
        def _(dve):
            st = Chain(dve, slink, 0)
            for buf in (win0, wout0, wrow0):
                last = nc.vector.memset(buf[:], 0.0)
            st.link(last)
            for hq in range(HQ):
                rows, cols = slice(hq * HD, (hq + 1) * HD), slice(hq * HD, (hq + 1) * HD)
                for dst, src in ((win0, wi), (wout0, wt)):
                    nc.vector.tensor_copy(dst[rows, :, cols].rearrange("p g (b d) -> p g b d", b=BG), bc(src[rows], 2, BG))
                last = nc.vector.tensor_copy(wrow0[rows, :, cols], wr[rows])
            st.link(last)
            st.link(nc.vector.tensor_scalar_add(wsum[:], conv[:, :, :, 3], 1.0))
            nc.vector.memset(top[:], 0.0).then_inc(setup.sem, 1)

            def enter(t):
                ch, x, i = Chain(dve, flink, t.r), x1[t.p], t.r
                dve.wait_ge(x_in.sem, x_in.at(i, 16))
                dve.wait_ge(kept.sem, kept.at(i - 2, 1))
                for j in range(TT):
                    dve.wait_ge(*front.full(i, f"y{j}"))
                    nc.vector.tensor_tensor(x[:, j, :], front.bank(f"y{j}"), xs[:, j, :], ALU.add).then_inc(front.read["dve"].sem, 1)
                dve.wait_ge(*front.used(i, "y1"))
                ch.link(nc.vector.tensor_tensor(x[:], x[:], bc(bo[:], 1, TT), ALU.add))
                dve.sem_inc(x1_done.sem, 1)
                layer_norm(nc, m, ch, x, h, stats, mv, rstd, var, std, TT).then_inc(h_done.sem, 1)
                ch.close()

            def convolve(t, fills):
                for fill in fills:
                    n, b = "qkv".index(fill[0]), int(fill[1])
                    y, at_ = f[t.p][fill[0]][:, b, :], n * KC + b
                    ch = Chain(dve, clink, t.r)
                    ch.n = 2 * at_
                    dve.wait_ge(base_done.sem, base_done.at(t.r, at_ + 1))
                    for s_ in (1, 2, 3):
                        tap = nc.vector.scalar_tensor_tensor(
                            y[:, s_ * BG:], front.bank(fill)[:, 0:GT - s_ * BG], conv[:, n, b, 3 - s_:4 - s_],
                            y[:, s_ * BG:], ALU.mult, ALU.add)
                        if s_ < 3:
                            ch.link(tap)
                    tap.then_inc(front.read["dve"].sem, 1)
                    if fill == "v3":
                        dve.wait_ge(*front.used(t.r, fill))
                        dve.sem_inc(conv_done.sem, 3 * KC)

            def rates_in(t):
                dve.wait_ge(*front.full(t.r, "lr"))
                nc.vector.tensor_scalar(lr[:], front.bank("lr")[:, 0:6 * H].rearrange("p (c n) -> p c n", c=3), 0.001, None,
                                        ALU.add).then_inc(z_done.sem, 1)
                dve.wait_ge(z_done.sem, z_done.at(t.r, 1))
                dve.sem_inc(front.read["dve"].sem, 1)

            def rates_add(t):
                dve.wait_ge(ze.sem, ze.at(t.r, 1))
                nc.vector.tensor_scalar_add(lrs[t.p][:], lrs[t.p][:], 1.0).then_inc(zp.sem, 1)

            def rates_out(t):
                out = lrs[t.p]
                dve.wait_ge(zl.sem, zl.at(t.r, 1))
                Chain(dve, rlink, t.r).link(nc.vector.scalar_tensor_tensor(out[:], lr[:], 0.0, out[:], ALU.max, ALU.add))
                for hq in range(HQ):
                    rows = slice(hq * HD, (hq + 1) * HD)
                    src = out[rows, 2, :].rearrange("p (g h j) -> p g h j", g=KC, h=HQ)[:, :, hq, :]
                    copy = nc.vector.tensor_copy(lrf[t.p][rows], src)
                copy.then_inc(lr_done.sem, 1)

            def exponents(i, ch, c):
                for j, n in enumerate((f"sk{c}", f"sq{c}")):
                    dve.wait_ge(*back.full(i, n))
                    s = back.bank(n).rearrange("p (n d) -> p n d", d=DI)
                    ch.link(nc.vector.tensor_reduce(top[:, j, :], s, AX, ALU.max))
                    nc.vector.tensor_tensor(e[c][:, j, :].rearrange("p (n d) -> p n d", d=DI), s, bc(top[:, j, :], 2, DI),
                                            ALU.subtract).then_inc(back.read["dve"].sem, 1)
                dve.wait_ge(*back.used(i, f"sq{c}"))
                dve.sem_inc(d_done.sem, 1)

            def weights(t, ch, c):
                dve.wait_ge(e_done.sem, e_done.at(t.r, c + 1))
                rows = e[c][:].rearrange("p j (n d) -> p (j n) d", d=DI)
                flat = tot[:].rearrange("p j n -> p (j n)")
                ch.link(nc.vector.tensor_reduce(flat, rows, AX, ALU.add))
                ch.link(nc.vector.reciprocal(flat, flat))
                by = tot[:].rearrange("p j (h b) -> p (j h) b", b=BG)
                ch.link(nc.vector.tensor_tensor(by, by, bc(own, 1, 2 * H), ALU.mult))
                rate = lrs[t.p][:, c, :].rearrange("p (h j) -> p h j", j=2)[:, :, 1]
                k_by = tot[:, 0, :].rearrange("p (h b) -> p h b", b=BG)
                ch.link(nc.vector.tensor_tensor(k_by, k_by, bc(rate, 2, BG), ALU.mult))
                nc.vector.tensor_tensor(rows, rows, bc(flat, 2, DI), ALU.mult).then_inc(p_done.sem, 1)

            def causal_products(i, c):
                for h_ in range(HQ):
                    n = f"qk{c}{h_}"
                    dve.wait_ge(*back.full(i, n))
                    nc.vector.tensor_tensor(qk[:, h_], back.bank(n, KC), bc(causal, 1, KC),
                                            ALU.mult).then_inc(back.read["dve"].sem, 1)
                dve.wait_ge(*back.used(i, f"qk{c}{HQ - 1}"))
                dve.sem_inc(qk_done.sem, 1)

            def add_own_heads(i, ch, fill, j, old, new):
                dve.wait_ge(*back.full(i, fill))
                g4 = grad[:, j, :].rearrange("p (g n) -> p g n", g=KC)
                nc.vector.tensor_tensor(g4, back.bank(fill, KC), bc(head, 1, KC), ALU.mult).then_inc(back.read["dve"].sem, 1)
                dve.wait_ge(*back.used(i, fill))
                return nc.vector.tensor_tensor(new[:], old[:], g4, ALU.add)

            def masked(i, fill, j):
                dve.wait_ge(*back.full(i, fill))
                nc.vector.tensor_tensor(at[:, j], back.bank(fill, KC), bc(neg, 1, KC), ALU.add).then_inc(back.read["dve"].sem, 1)

            def maxima(i, ch, it):
                dve.wait_ge(*back.used(i, f"so{it}"))
                ch.link(nc.vector.tensor_reduce(atop[:], at[:].rearrange("p j g n -> p (j g) n"), AX, ALU.max))
                nc.vector.tensor_scalar(atop[:], atop[:], -ATT_SCALE, None, ALU.mult).then_inc(s_done.sem, 1)

            def normalise(t, ch, it):
                dve.wait_ge(a_done.sem, a_done.at(t.r, it + 1))
                ch.link(nc.vector.reciprocal(asum[:], asum[:]))
                for j in range(2):
                    part = asum[:, j * KC:(j + 1) * KC]
                    mm = nc.vector.tensor_tensor(part, part, lrf[t.p][:, :, 1 - j], ALU.mult)
                ch.link(mm)
                by = at[:].rearrange("p j g n -> p (j g) n")
                nc.vector.tensor_tensor(by, by, bc(asum[:], 2, P), ALU.mult).then_inc(n_done.sem, 1)

            def step_weights(i, ch, it):
                ch.link(add_own_heads(i, ch, f"gi{it}", 0, wout, wout))
                add_own_heads(i, ch, f"go{it}", 1, win0 if it == 0 else win, win).then_inc(w_done.sem, 1)

            def leave(t, i):
                dve.wait_ge(kept.sem, kept.at(t.r, 1))
                for j in range(TT):
                    dve.wait_ge(*back.full(i, f"z{j}"))
                    nc.vector.tensor_tensor(x2[:, j, :], back.bank(f"z{j}"), x2[:, j, :], ALU.add).then_inc(back.read["dve"].sem, 1)
                dve.wait_ge(*back.used(i, "z1"))
                dve.sem_inc(x2_done.sem, 1)

            def group(t, last, has_prev=True):
                n, i = t.next(), t.r
                ch = Chain(dve, link, i)
                ahead = (lambda *fills: None) if last else (lambda *fills: convolve(n, fills))
                exponents(i, ch, 0)
                masked(i, "si0", 0)
                dve.wait_ge(lr_done.sem, lr_done.at(i, 1))
                weights(t, ch, 0)
                if has_prev:
                    causal_products(i, 1)
                else:
                    back.skip_reads(dve, "dve", i, *END, *LEAVE)
                if not last:
                    enter(n)
                if has_prev:
                    leave(t.prev(), i)
                add_own_heads(i, ch, "up", 0, wout0, wout).then_inc(w_done.sem, 1)
                causal_products(i, 0)
                masked(i, "so0", 1)
                maxima(i, ch, 0)
                normalise(t, ch, 0)
                ahead("q0", "q1", "q2", "q3")
                step_weights(i, ch, 0)
                masked(i, "si1", 0)
                masked(i, "so1", 1)
                maxima(i, ch, 1)
                if not last:
                    rates_in(n)
                ahead("k0", "k1")
                normalise(t, ch, 1)
                if not last:
                    rates_add(n)
                ahead("k2", "k3", "v0", "v1")
                step_weights(i, ch, 1)
                ahead("v2", "v3")
                exponents(i, ch, 1)
                if not last:
                    rates_out(n)
                weights(t, ch, 1)
                ch.close()

            enter(FIRST)
            convolve(FIRST, ["q0", "q1", "q2", "q3"])
            rates_in(FIRST)
            rates_add(FIRST)
            convolve(FIRST, [f"{n}{e_}" for n in "kv" for e_ in range(KC)])
            rates_out(FIRST)
            group(FIRST, False, False)
            rounds(dve, NG, group, 1)
            back.skip_reads(dve, "dve", NG, *BEGIN)
            causal_products(NG, 1)
            leave(LAST, NG)

        @block.tensor
        def _(pe):
            def blocks(i, ring, fill, parts, pairs):
                pe.wait_ge(*ring.free(i, fill))
                out = ring.bank(fill, parts)
                for g, (lhsT, rhs) in enumerate(pairs):
                    last = nc.tensor.matmul(out[:, g, :], lhsT, rhs, start=True, stop=True)
                last.then_inc(ring.filled.sem, 1)

            def transposes(i, ring, fill, parts):
                pe.wait_ge(*ring.free(i, fill))
                out = ring.bank(fill, len(parts))
                for g, x in enumerate(parts):
                    last = nc.tensor.transpose(out[:, g, :], x, k["ident"])
                last.then_inc(ring.filled.sem, 1)

            def deep(i, ring, fill, n, lhsT, rhs):
                pe.wait_ge(*ring.free(i, fill))
                for c in range(KC):
                    last = nc.tensor.matmul(ring.bank(fill)[:, 0:n], lhsT(c), rhs(c), start=(c == 0), stop=(c == KC - 1))
                last.then_inc(ring.filled.sem, 1)

            def ahead(t, *fills):
                i = t.r
                for fill in fills:
                    j = int(fill[1]) if fill[1:].isdigit() else 0
                    if fill[0] == "y":
                        if j == 0:
                            pe.wait_ge(c_in.sem, c_in.at(i, 16))
                        deep(i, front, fill, D, lambda c: cT[:, c, j * P:(j + 1) * P], lambda c: Wo[:, c, :])
                    elif fill[0] == "t":
                        if j == 0:
                            pe.wait_ge(h_done.sem, h_done.at(i, 1))
                        transposes(i, front, fill, [h[:, j, c * P:(c + 1) * P] for c in range(KC)])
                    elif fill[0] in "qkv":
                        if fill == "q0":
                            pe.wait_ge(hT_done.sem, hT_done.at(i, 1))
                        deep(i, front, fill, GT, lambda c: Wp[fill[0]][:, c, j * P:(j + 1) * P], lambda c: hT[:, c, :])
                    else:
                        pe.wait_ge(*front.free(i, "lr"))
                        pe.wait_ge(hx_done.sem, hx_done.at(i, 1))
                        for part in range(3):
                            for c in range(KC):
                                tokens = hx[:, c, :] if part == 2 else hT[:, c, part * P:(part + 1) * P]
                                mm = nc.tensor.matmul(front.bank("lr")[:, part * 2 * H:(part + 1) * 2 * H], tokens, Wlr[:, c, :],
                                                      start=(c == 0), stop=(c == KC - 1))
                        mm.then_inc(front.filled.sem, 1)

            def turned_softmax(t, i, c):
                pe.wait_ge(p_done.sem, p_done.at(t.r, c + 1))
                transposes(i, back, f"khT{c}", [e[c][:, 0, g * P:(g + 1) * P] for g in range(KC)])
                transposes(i, back, f"qhT{c}", [e[c][:, 1, g * P:(g + 1) * P] for g in range(KC)])

            def causal(i, c):
                pe.wait_ge(*back.used(i, f"qhT{c}"))
                for h_ in range(HQ):
                    r = slice(h_ * HD, (h_ + 1) * HD)
                    blocks(i, back, f"qk{c}{h_}", KC, [(khT[c][r, g, :], qhT[c][r, g, :]) for g in range(KC)])

            def output(t, i, c):
                pe.wait_ge(*back.free(i, f"o{c}"))
                pe.wait_ge(qk_done.sem, qk_done.at(t.r, c + 1))
                out, w_row = back.bank(f"o{c}", KC), wrow if c else wrow0
                for g in range(KC):
                    nc.tensor.matmul(out[:, g, :], w_row[:, g, :], qhT[c][:, g, :], start=True, stop=False)
                    for h_ in range(HQ):
                        r = slice(h_ * HD, (h_ + 1) * HD)
                        mm = nc.tensor.matmul(out[r, g, :], vt[c][:, g, r], qk[:, h_, g, :], start=False, stop=True)
                mm.then_inc(back.filled.sem, 1)

            def project(i):
                pe.wait_ge(*back.used(i, "o1"))
                for j in range(TT):
                    deep(i, back, f"z{j}", D, lambda c: oT[:, c, j * P:(j + 1) * P], lambda c: Wo2[:, c, :])

            def group(t, last, has_prev=True):
                n, i = t.next(), t.r
                q, key, v = (f[t.p][x] for x in "qkv")
                by_g, halves = range(KC), [slice(0, P), slice(P, 2 * P)]
                go = (lambda *fills: None) if last else (lambda *fills: ahead(n, *fills))

                pe.wait_ge(conv_done.sem, conv_done.at(i, 3 * KC))
                blocks(i, back, "sk0", KC, [(key[:, g, halves[0]], win0[:, g, :]) for g in by_g])
                blocks(i, back, "sq0", KC, [(q[:, g, halves[0]], win0[:, g, :]) for g in by_g])
                transposes(i, back, "vt0", [v[:, g, halves[0]] for g in by_g])
                transposes(i, back, "kt0", [key[:, g, halves[0]] for g in by_g])
                blocks(i, back, "si0", KC, [(win0[:, g, :], key[:, g, halves[0]]) for g in by_g])
                go("y0", "y1")
                if has_prev:
                    turned_softmax(t.prev(), i, 1)
                    causal(i, 1)
                    output(t.prev(), i, 1)
                else:
                    back.skip(pe, i, *END)
                turned_softmax(t, i, 0)
                if has_prev:
                    project(i)
                else:
                    back.skip(pe, i, *LEAVE)
                pe.wait_ge(*back.used(i, "vt0"))
                blocks(i, back, "up", KC, [(vt[0][:, g, :], e[0][:, 0, g * P:(g + 1) * P]) for g in by_g])
                go("t0", "t1")
                causal(i, 0)
                pe.wait_ge(w_done.sem, w_done.at(i, 1))
                blocks(i, back, "so0", KC, [(wout[:, g, :], v[:, g, halves[0]]) for g in by_g])
                go("q0", "q1", "q2", "q3")
                for it in range(2):
                    pe.wait_ge(n_done.sem, n_done.at(i, it + 1))
                    transposes(i, back, f"ti{it}", [at[:, 0, g, :] for g in by_g])
                    transposes(i, back, f"to{it}", [at[:, 1, g, :] for g in by_g])
                    if it == 0:
                        output(t, i, 0)
                    pe.wait_ge(*back.used(i, f"ti{it}"))
                    blocks(i, back, f"gi{it}", KC, [(vt[0][:, g, :], atT[:, 0, g, :]) for g in by_g])
                    pe.wait_ge(*back.used(i, f"to{it}"))
                    blocks(i, back, f"go{it}", KC, [(kt[:, g, :], atT[:, 1, g, :]) for g in by_g])
                    if it == 0:
                        go("lr", "k0", "k1")
                        pe.wait_ge(w_done.sem, w_done.at(i, 2))
                        blocks(i, back, "si1", KC, [(win[:, g, :], key[:, g, halves[0]]) for g in by_g])
                        blocks(i, back, "so1", KC, [(wout[:, g, :], v[:, g, halves[0]]) for g in by_g])
                        go("k2", "k3", "v0", "v1")
                go("v2", "v3")
                pe.wait_ge(w_done.sem, w_done.at(i, 3))
                blocks(i, back, "sk1", KC, [(key[:, g, halves[1]], win[:, g, :]) for g in by_g])
                blocks(i, back, "sq1", KC, [(q[:, g, halves[1]], win[:, g, :]) for g in by_g])
                transposes(i, back, "vt1", [v[:, g, halves[1]] for g in by_g])
                transposes(i, back, "wo", [wout[:, g, :] for g in by_g])

            ahead(FIRST, *[x for x, _ in FRONT])
            pe.wait_ge(setup.sem, setup.at(0, 1))
            group(FIRST, False, False)
            rounds(pe, NG, group, 1)
            back.skip(pe, NG, *BEGIN)
            turned_softmax(LAST, NG, 1)
            causal(NG, 1)
            output(LAST, NG, 1)
            back.skip(pe, NG, *TURN)
            project(NG)

        @block.scalar
        def _(act):
            act.wait_ge(setup.sem, setup.at(0, 1))

            def take(i, fill, dst, parts=KC):
                act.wait_ge(*back.full(i, fill))
                nc.scalar.activation(dst, back.bank(fill, parts), ACT.Copy).then_inc(back.read["act"].sem, 1)

            def deviation(t):
                act_deviation(nc, act, t.r, mv, rstd[:], var, std)

            def turned(t):
                for j in range(TT):
                    act.wait_ge(*front.full(t.r, f"t{j}"))
                    nc.scalar.activation(hT[:, :, j * P:(j + 1) * P], front.bank(f"t{j}", KC), ACT.Copy).then_inc(front.read["act"].sem, 1)
                act.wait_ge(*front.used(t.r, "t1"))
                act.sem_inc(hT_done.sem, 1)

            def base(t, *fills):
                for fill in fills:
                    act.wait_ge(*front.full(t.r, fill))
                    nc.scalar.activation(f[t.p][fill[0]][:, int(fill[1]), :], front.bank(fill)[:, 0:GT], ACT.Copy,
                                         scale=wsum[:, "qkv".index(fill[0]), int(fill[1]):int(fill[1]) + 1]).then_inc(base_done.sem, 1)

            def rates_exp(t):
                out = lrs[t.p]
                act.wait_ge(z_done.sem, z_done.at(t.r, 1))
                nc.scalar.activation(out[:], lr[:], ACT.Abs).then_inc(za.sem, 1)
                act.wait_ge(za.sem, za.at(t.r, 1))
                nc.scalar.activation(out[:], out[:], ACT.Exp, scale=-1.0).then_inc(ze.sem, 1)

            def rates_ln(t):
                act.wait_ge(zp.sem, zp.at(t.r, 1))
                nc.scalar.activation(lrs[t.p][:], lrs[t.p][:], ACT.Ln).then_inc(zl.sem, 1)

            def exponentials(i, c):
                act.wait_ge(d_done.sem, d_done.at(i, c + 1))
                nc.scalar.activation(e[c][:], e[c][:], ACT.Exp).then_inc(e_done.sem, 1)

            def row_exponentials(i, it):
                act.wait_ge(s_done.sem, s_done.at(i, it + 1))
                for n in range(S2):
                    mm = nc.scalar.activation(at[:, n // KC, n % KC, :], at[:, n // KC, n % KC, :], ACT.Exp,
                                              bias=atop[:, n:n + 1], scale=ATT_SCALE, accum_out=asum[:, n:n + 1])
                mm.then_inc(a_done.sem, 1)

            def end(i):
                take(i, "khT1", khT[1][:])
                take(i, "qhT1", qhT[1][:])
                take(i, "o1", oT[:, :, P:2 * P])

            def group(t, last, has_prev=True):
                n, i = t.next(), t.r
                ahead = (lambda *fills: None) if last else (lambda *fills: base(n, *fills))
                take(i, "vt0", vt[0][:])
                take(i, "kt0", kt[:])
                exponentials(i, 0)
                if has_prev:
                    end(i)
                else:
                    back.skip_reads(act, "act", i, *END, *LEAVE)
                take(i, "khT0", khT[0][:])
                take(i, "qhT0", qhT[0][:])
                if not last:
                    deviation(n)
                    turned(n)
                row_exponentials(i, 0)
                ahead("q0", "q1", "q2", "q3")
                take(i, "ti0", atT[:, 0])
                take(i, "to0", atT[:, 1])
                take(i, "o0", oT[:, :, 0:P])
                ahead("k0", "k1")
                row_exponentials(i, 1)
                if not last:
                    rates_exp(n)
                ahead("k2", "k3", "v0", "v1")
                take(i, "ti1", atT[:, 0])
                take(i, "to1", atT[:, 1])
                if not last:
                    rates_ln(n)
                ahead("v2", "v3")
                take(i, "vt1", vt[1][:])
                exponentials(i, 1)
                take(i, "wo", wrow[:])

            deviation(FIRST)
            turned(FIRST)
            base(FIRST, "q0", "q1", "q2", "q3")
            rates_exp(FIRST)
            base(FIRST, *[f"{n}{e_}" for n in "kv" for e_ in range(KC)])
            rates_ln(FIRST)
            group(FIRST, False, False)
            rounds(act, NG, group, 1)
            back.skip_reads(act, "act", NG, *BEGIN)
            end(NG)


def running_sum(nc, chain, bufs, n):
    src, dst = bufs
    step = 1
    while step < n:
        nc.vector.tensor_copy(dst[:, 0:step], src[:, 0:step])
        chain.link(nc.vector.tensor_tensor(dst[:, step:n], src[:, step:n], src[:, 0:n - step], ALU.add))
        src, dst, step = dst, src, 2 * step
    return src


def rounded(nc, chain, x, add, mul):
    chain.link(nc.vector.tensor_scalar(x, x, add, mul, ALU.add, ALU.mult))
    chain.link(nc.vector.tensor_scalar(x, x, MAGIC, None, ALU.add))
    chain.link(nc.vector.tensor_scalar(x, x, -MAGIC, None, ALU.add))


def experts_phase(nc, a, k):
    with ExitStack() as ctx:
        m = Mem(nc, ctx, "ex")
        const = k["const"]
        order, before = const[:, CORD:CORD + E], const[:, CTRI:CTRI + P]
        number, rows = const[:, CIOTA:CIOTA + P], const[:, CROW:CROW + TILES]
        Wg, We = m.sb("Wg", [P, KC, E]), m.sb("We", [P, E, KC, D])
        w_in, e_in = m.count("w_in"), m.count("e_in")
        xs = [m.sb(f"x{p}", [P, TT, D]) for p in range(2)]
        h = [m.sb(f"h{p}", [P, TT, D]) for p in range(2)]
        stats, mv, rstd = m.sb("st", [P, TT, 6]), m.sb("mv", [P, TT, 2]), m.sb("rs", [P, TT])
        hT = m.sb("hT", [P, KC, TT, P])
        turn, gate = Ring(m, "turn", 2, [("t0", "act"), ("t1", "act")]), Ring(m, "gate", 1, [("g", "act")])
        x_in = [m.count(f"x_in{p}", 16) for p in range(2)]
        h_done, var, std, nlink = m.count("h"), m.count("var"), m.count("std"), m.count("nlink", LN_LINKS)
        scores = m.sb("scores", [E, TILES, P])
        best, chosen = m.sb("best", [P, TILES]), m.sb("chosen", [P, TILES, E])
        sums = [m.sb(f"sums{j}", [P, TILES, E]) for j in range(2)]
        ends = [m.sb(f"ends{j}", [P, E]) for j in range(2)]
        tiles, slot = m.sb("tiles", [P, E]), m.sb("slot", [P, TILES])
        slot_tile, is_part = m.sb("slot_tile", [P, TILES]), m.sb("is_part", [P, TILES, P])
        in_tile = m.sb("in_tile", [P, TILES, SLOTS])
        passed = m.sb("passed", [1, SLOTS, E])
        row = m.sb("row", [P, SLOTS], I32)
        expert_f, expert = m.sb("expert_f", [1, SLOTS]), m.sb("expert", [1, SLOTS], I32)
        ps_s = m.ps("slots", [P, 512])
        slot_ps, slot_in = m.count("slot_ps"), m.count("slot_in")
        row_done, expert_done, plink = m.count("row"), m.count("expert"), m.count("plink")
        xg = [m.sb(f"xg{p}", [P, 1, D]) for p in range(2)]
        hg = [m.sb(f"hg{p}", [P, 1, D]) for p in range(2)]
        xh, res = [m.sb(f"xh{p}", [P, D]) for p in range(2)], [m.sb(f"res{p}", [P, D]) for p in range(2)]
        gT = [m.sb(f"gT{p}", [P, KC, P]) for p in range(2)]
        row_in, row_out = [m.sb(f"row_in{p}", [P, 1], I32) for p in range(2)], [m.sb(f"row_out{p}", [P, 1], I32) for p in range(2)]
        index_done = [m.count("row_in"), m.count("row_out")]
        gturn = [Ring(m, f"gturn{p}", 1, [("t", "act")]) for p in range(2)]
        prod = [Ring(m, f"prod{p}", 1, [("y", "dve")]) for p in range(2)]
        g_in, g_out = [m.count(f"g_in{p}", 16, 0) for p in range(2)], [m.count(f"g_out{p}", 16, 0) for p in range(2)]
        cleared, gh_done, gx_done, res_done = m.count("cleared"), m.count("gh"), m.count("gx"), m.count("res")
        gvar, gstd, glink = m.count("gvar"), m.count("gstd"), m.count("glink", 2)
        block = ctx.enter_context(nc.Block())

        @block.sync
        def _(sp):
            def load(t):
                sp.wait_ge(h_done.sem, h_done.at(t.r - 1, 0))
                sp.dma_start(xs[t.p][:], a["x2_scr"][bass.ds(t.r, 1)].rearrange("o p t d -> (o p) t d")).then_inc(x_in[t.p].sem, 16)

            sp.dma_start(Wg[:], a["gate"]).then_inc(w_in.sem, 16)
            load(Round(0, 0))
            rounds(sp, NG, lambda t, last: None if last else load(t.next()))
            sp.dma_start(We[:], a["expert"].rearrange("e p c d -> p e c d")).then_inc(e_in.sem, 16)
            sp.wait_ge(e_in.sem, e_in.at(0, 16))

        @block.gpsimd
        def _(pool):
            m.start(pool)
            nc.gpsimd.memset(xg[0][:], 0.0)
            nc.gpsimd.memset(xg[1][:], 0.0).then_inc(cleared.sem, 1)
            x_rows, o_rows = (a[n].rearrange("g p t d -> (g p t) d") for n in ("x2_scr", "out"))

            def index(t, buf, n):
                nc.gpsimd.tensor_copy(buf[:], row[:, bass.ds(t.r, 1)]).then_inc(index_done[n].sem, 1)
                pool.wait_ge(index_done[n].sem, index_done[n].at(t.r, 1))
                m.settle(pool)
                return bass.IndirectOffsetOnAxis(ap=buf[:], axis=0)

            def gather(t):
                pool.wait_ge(gx_done.sem, gx_done.at(t.r - 1, 0))
                m.settle(pool)
                nc.gpsimd.indirect_dma_start(xg[t.p][:, 0, :], None, x_rows, index(t, row_in[t.p], 0), bounds_check=B * L - 1,
                                             oob_is_err=False).then_inc(g_in[t.p].sem, 16)

            def scatter(t):
                pool.wait_ge(res_done.sem, res_done.at(t.r, 1))
                m.settle(pool)
                nc.gpsimd.indirect_dma_start(o_rows, index(t, row_out[t.p], 1), res[t.p][:], None, bounds_check=B * L - 1,
                                             oob_is_err=False).then_inc(g_out[t.p].sem, 16)

            def tile(t, last):
                gather(t.next().next().next())
                scatter(t)

            pool.wait_ge(cleared.sem, cleared.at(0, 1))
            pool.wait_ge(row_done.sem, row_done.at(0, 1))
            for r in range(3):
                gather(Round(r // 2, r % 2))
            rounds(pool, SLOTS - 3, tile)
            for r in range(SLOTS - 3, SLOTS):
                scatter(Round(r // 2, r % 2))
            for p in range(2):
                pool.wait_ge(g_out[p].sem, g_out[p].at((SLOTS + 1 - p) // 2, 0))

        @block.vector
        def _(dve):
            def norm(t):
                dve.wait_ge(x_in[t.p].sem, x_in[t.p].at(t.i, 16))
                dve.wait_ge(*turn.full(t.r - 2, "t1"))
                layer_norm(nc, m, Chain(dve, nlink, t.r), xs[t.p], h[t.p], stats, mv, rstd, var, std, TT).then_inc(h_done.sem, 1)

            rounds(dve, NG, lambda t, last: norm(t))

            step = Chain(dve, plink, 0)
            dve.wait_ge(slot_ps.sem, slot_ps.at(0, 1))
            by_token = ps_s[:, 0:TILES * E].rearrange("p (t e) -> p t e", e=E)
            step.link(nc.vector.tensor_reduce(best[:], by_token, AX, ALU.max))
            step.link(nc.vector.tensor_tensor(chosen[:], by_token, bc(best[:], 2, E), ALU.is_ge))
            step.link(nc.vector.tensor_tensor(chosen[:], chosen[:], bc(order, 1, TILES), ALU.mult))
            step.link(nc.vector.tensor_reduce(best[:], chosen[:], AX, ALU.max))
            nc.vector.tensor_tensor(chosen[:], chosen[:], bc(best[:], 2, E), ALU.is_equal).then_inc(slot_in.sem, 1)

            dve.wait_ge(slot_ps.sem, slot_ps.at(0, 2))
            rank, tile_sum = (ps_s[:, j * P:(j + 1) * P].rearrange("p (t e) -> p t e", e=E) for j in range(2))
            step.link(nc.vector.tensor_copy(sums[0][:], tile_sum))
            total = running_sum(nc, step, sums, TILES)
            other = sums[1] if total is sums[0] else sums[0]
            step.link(nc.vector.tensor_copy(ends[0][:], total[:, TILES - 1, :]))
            rounded(nc, step, ends[0][:], (P - 1) / 2, 1.0 / P)
            step.link(nc.vector.tensor_copy(tiles[:], ends[0][:]))
            end = running_sum(nc, step, ends, E)
            step.link(nc.vector.tensor_tensor(tiles[:], end[:], tiles[:], ALU.subtract))
            step.link(nc.vector.tensor_scalar(tiles[:], tiles[:], float(P), None, ALU.mult))
            step.link(nc.vector.tensor_tensor(other[:], total[:], tile_sum, ALU.subtract))
            step.link(nc.vector.tensor_tensor(other[:], other[:], rank, ALU.add))
            step.link(nc.vector.tensor_tensor(other[:], other[:], bc(tiles[:], 1, TILES), ALU.add))
            step.link(nc.vector.tensor_tensor(other[:], other[:], chosen[:], ALU.mult))
            step.link(nc.vector.tensor_reduce(slot[:], other[:], AX, ALU.add))
            step.link(nc.vector.tensor_copy(slot_tile[:], slot[:]))
            rounded(nc, step, slot_tile[:], -(P - 1) / 2, 1.0 / P)
            step.link(nc.vector.tensor_scalar(best[:], slot_tile[:], -float(P), None, ALU.mult))
            step.link(nc.vector.tensor_tensor(slot[:], slot[:], best[:], ALU.add))
            nc.vector.tensor_tensor(is_part[:], bc(number, 1, TILES), bc(slot[:], 2, P), ALU.is_equal)
            step.link(nc.vector.tensor_tensor(in_tile[:], bc(number[:, 0:SLOTS], 1, TILES), bc(slot_tile[:], 2, SLOTS), ALU.is_equal))
            nc.vector.tensor_tensor(in_tile[:], in_tile[:], bc(rows, 2, SLOTS), ALU.mult).then_inc(slot_in.sem, 1)
            step.link(nc.vector.tensor_tensor(passed[:], bc(number[0:1, 0:SLOTS], 2, E), bc(end[0:1, :], 1, SLOTS), ALU.is_ge))
            step.link(nc.vector.tensor_reduce(expert_f[:], passed[:], AX, ALU.add))
            nc.vector.tensor_scalar(expert[:], expert_f[:], float(E - 1), None, ALU.min).then_inc(expert_done.sem, 1)
            dve.wait_ge(slot_ps.sem, slot_ps.at(0, 3))
            nc.vector.tensor_scalar(row[:], ps_s[:, 2 * P:2 * P + SLOTS], float(B * L), None, ALU.add).then_inc(row_done.sem, 1)

            def slot_norm(t):
                dve.wait_ge(g_in[t.p].sem, g_in[t.p].at(t.i, 16))
                dve.wait_ge(*gturn[t.p].full(t.i - 1, "t"))
                layer_norm(nc, m, Chain(dve, glink, t.r), xg[t.p], hg[t.p], stats, mv, rstd, gvar, gstd, 1).then_inc(gh_done.sem, 1)

            def slot_sum(t):
                dve.wait_ge(gh_done.sem, gh_done.at(t.r, 1))
                nc.vector.tensor_tensor(xh[t.p][:], xg[t.p][:, 0, :], hg[t.p][:, 0, :], ALU.add).then_inc(gx_done.sem, 1)

            def result(t):
                dve.wait_ge(*prod[t.p].full(t.i, "y"))
                dve.wait_ge(gx_done.sem, gx_done.at(t.r, 1))
                if not (isinstance(t.i, int) and t.i == 0):
                    dve.wait_ge(g_out[t.p].sem, g_out[t.p].at(t.i, 0))
                nc.vector.tensor_tensor(res[t.p][:], prod[t.p].bank("y"), xh[t.p][:], ALU.add).then_inc(prod[t.p].read["dve"].sem, 1)
                dve.wait_ge(*prod[t.p].used(t.i, "y"))
                dve.sem_inc(res_done.sem, 1)

            def tile(t, last):
                n = t.next().next()
                slot_norm(n)
                result(t)
                slot_sum(n)

            for p in range(2):
                slot_norm(Round(0, p))
                slot_sum(Round(0, p))
            for p in range(2):
                tile(Round(0, p), False)
            rounds(dve, SLOTS - 2, tile, 2)
            for r in range(SLOTS - 2, SLOTS):
                result(Round(r // 2, r % 2))

        @block.tensor
        def _(pe):
            def turned(t):
                pe.wait_ge(h_done.sem, h_done.at(t.r, 1))
                for j in range(TT):
                    pe.wait_ge(*turn.free(t.r, f"t{j}"))
                    for c in range(KC):
                        last = nc.tensor.transpose(turn.bank(f"t{j}", KC)[:, c, :], h[t.p][:, j, c * P:(c + 1) * P], k["ident"])
                    last.then_inc(turn.filled.sem, 1)

            def group(t, last):
                pe.wait_ge(*turn.used(t.r, "t1"))
                pe.wait_ge(*gate.free(t.r, "g"))
                for c in range(KC):
                    mm = nc.tensor.matmul(gate.bank("g")[0:E, 0:GT], Wg[:, c, :], hT[:, c].rearrange("p t n -> p (t n)"),
                                          start=(c == 0), stop=(c == KC - 1))
                mm.then_inc(gate.filled.sem, 1)
                if not last:
                    turned(t.next())

            turned(Round(0, 0))
            pe.wait_ge(w_in.sem, w_in.at(0, 16))
            rounds(pe, NG, group)

            pe.wait_ge(*gate.used(NG - 1, "g"))
            for t in range(TILES):
                mm = nc.tensor.transpose(ps_s[:, t * E:(t + 1) * E], scores[:, t, :], k["ident"][0:E, 0:E])
            mm.then_inc(slot_ps.sem, 1)

            pe.wait_ge(slot_in.sem, slot_in.at(0, 1))
            flat = chosen[:].rearrange("p t e -> p (t e)")
            nc.tensor.matmul(ps_s[:, 0:P], before, flat, start=True, stop=True)
            nc.tensor.matmul(ps_s[:, P:2 * P], k["ones"].broadcast_to([P, P]), flat, start=True, stop=True).then_inc(slot_ps.sem, 1)
            pe.wait_ge(slot_in.sem, slot_in.at(0, 2))
            for t in range(TILES):
                mm = nc.tensor.matmul(ps_s[:, 2 * P:2 * P + SLOTS], is_part[:, t, :], in_tile[:, t, :],
                                      start=(t == 0), stop=(t == TILES - 1))
            mm.then_inc(slot_ps.sem, 1)

            def slots_turned(t):
                pe.wait_ge(gh_done.sem, gh_done.at(t.r, 1))
                pe.wait_ge(*gturn[t.p].free(t.i, "t"))
                for c in range(KC):
                    last = nc.tensor.transpose(gturn[t.p].bank("t", KC)[:, c, :], hg[t.p][:, 0, c * P:(c + 1) * P], k["ident"])
                last.then_inc(gturn[t.p].filled.sem, 1)

            def tile(t, last):
                if not last:
                    slots_turned(t.next())
                which = pe.value_load(expert[0:1, bass.ds(t.r, 1)], min_val=0, max_val=E - 1)
                pe.wait_ge(*gturn[t.p].used(t.i, "t"))
                pe.wait_ge(*prod[t.p].free(t.i, "y"))
                for c in range(KC):
                    expert_rows = We[:, bass.ds(which, 1), c, :].rearrange("p o d -> p (o d)")
                    mm = nc.tensor.matmul(prod[t.p].bank("y"), gT[t.p][:, c, :], expert_rows,
                                          start=(c == 0), stop=(c == KC - 1))
                mm.then_inc(prod[t.p].filled.sem, 1)

            slots_turned(Round(0, 0))
            pe.wait_ge(expert_done.sem, expert_done.at(0, 1))
            pe.wait_ge(e_in.sem, e_in.at(0, 16))
            rounds(pe, SLOTS, tile)

        @block.scalar
        def _(act):
            def deviation(t):
                act_deviation(nc, act, t.r, mv, rstd[:], var, std)

            def turned(t):
                for j in range(TT):
                    act.wait_ge(*turn.full(t.r, f"t{j}"))
                    nc.scalar.activation(hT[:, :, j, :], turn.bank(f"t{j}", KC), ACT.Copy).then_inc(turn.read["act"].sem, 1)

            def group(t, last):
                if not last:
                    deviation(t.next())
                act.wait_ge(*gate.full(t.r, "g"))
                nc.scalar.activation(scores[:, bass.ds(t.r * TT, TT), :], gate.bank("g")[0:E, 0:GT].rearrange("p (t n) -> p t n", t=TT),
                                     ACT.Copy).then_inc(gate.read["act"].sem, 1)
                if not last:
                    turned(t.next())

            deviation(Round(0, 0))
            turned(Round(0, 0))
            rounds(act, NG, group)

            def slots_turned(t, last):
                act.wait_ge(gvar.sem, gvar.at(t.r, 1))
                nc.scalar.activation(rstd[:, 0:1], mv[:, 0:1, 1], ACT.Sqrt, bias=EPS).then_inc(gstd.sem, 1)
                act.wait_ge(*prod[t.p].full(t.i - 1, "y"))
                act.wait_ge(*gturn[t.p].full(t.i, "t"))
                nc.scalar.activation(gT[t.p][:], gturn[t.p].bank("t", KC), ACT.Copy).then_inc(gturn[t.p].read["act"].sem, 1)

            rounds(act, SLOTS, slots_turned)


def layer(nc, a):
    with ExitStack() as ctx:
        m = Mem(nc, ctx, "all")
        k = {"const": m.sb("const", [P, CN]), "ix": m.sb("ix", [P, B // 2, KC, 2, NK])[:]}
        k["flag"] = m.sb("flag", [1, 1], I32)[:]
        k["weights"] = {n: m.sb(n, [P, *a[n].shape[len(a[n].shape) > 1:]]) for n in WEIGHTS}
        k["ident"] = k["const"][:, CI:CI + P]
        k["ones"] = k["const"][:, CONE:CONE + 1]
        project_phase(nc, a, k)
        outside = nc.values_load(k["flag"], min_val=0, max_val=P)
        with nc.If(outside < 1):
            attend_window_phase(nc, a, k)
        with nc.Else():
            attend_all_phase(nc, a, k)
        fast_phase(nc, a, k)
        experts_phase(nc, a, k)


def feature_blocks(w):
    return np.ascontiguousarray(w.reshape(KC, P, -1).transpose(1, 0, 2))


def layouts(v):
    out = {
        "x_tok": v["x"].reshape(NG, TT, P, D),
        "x_lb": v["x"].reshape(NG, BG, TT, C, D).transpose(0, 3, 1, 2, 4).reshape(NG, P, TT, D),
        "ctx": np.roll(v["ctx_1024"], TAIL, axis=1).reshape(NG, BG, M, KC, P).transpose(0, 4, 3, 2, 1).reshape(NG, P, KC, M * BG),
        "mask": v["mask_BxS2_if0"],
        "const": shape_constants(),
        "xWoff": feature_blocks(v["L0_xattn_Woff"].T), "xboff": v["L0_xattn_boff"],
        "xbo": v["L0_xattn_bo"], "xbv": v["L0_xattn_bv"],
    }
    for n in ("Wq", "Wk", "Wv", "Wo"):
        out["x" + n] = feature_blocks(v["L0_xattn_" + n].T)
        out["a" + n] = feature_blocks(v["L0_attn_" + n])
    for n in ("bq", "bk"):
        out["x" + n] = v["L0_xattn_" + n].reshape(KC, P).T
    out["aWlr"] = feature_blocks(v["L0_attn_Wlr"])
    out["conv"] = np.stack([v["L0_attn_conv_" + n].reshape(KC, P, 4) for n in "qkv"]).transpose(2, 0, 1, 3)
    for n in ("in", "out"):
        w = v[f"L0_attn_W_{n}_init"][0].reshape(DI, KC, HQ, HD)
        out["aW" + n] = w.transpose(2, 3, 1, 0).reshape(P, KC, DI)
    out["aWout_rows"] = np.repeat(v["L0_attn_W_out_init"][0].reshape(DI, KC, HQ, 1, HD).transpose(2, 3, 0, 1, 4), BG,
                                  axis=1).reshape(P, KC, HD)
    out["gate"] = feature_blocks(v["L0_ffn_gate_w"].T)
    out["expert"] = v["L0_ffn_expert_w"].transpose(0, 2, 1).reshape(E, KC, P, D).transpose(0, 2, 1, 3)
    return {n: np.ascontiguousarray(w) for n, w in out.items()}


WEIGHTS = ("xWk", "xWv", "xbk", "xbv", "xWo", "xbo", "aWq", "aWk", "aWv", "aWo", "aWlr", "conv", "aWin", "aWout", "aWout_rows")
SCRATCH = {"q_scr": (NG, P, KC, GT), "c_scr": (NG, P, KC, GT), "x2_scr": (NG, P, TT, D)}


def kernel(**inputs):
    import concourse.bacc as bacc
    from concourse.bass_utils import run_bass_kernel_spmd

    nc = bacc.Bacc("TRN2", target_bir_lowering=False, num_devices=1)
    arrays = layouts({n: np.asarray(w) for n, w in inputs.items()})
    a = {n: nc.dram_tensor(n, w.shape, mybir.dt.from_np(w.dtype), kind="ExternalInput").ap() for n, w in arrays.items()}
    for n, shape in SCRATCH.items():
        a[n] = nc.dram_tensor(n, shape, F32).ap()
    a["out"] = nc.dram_tensor("out", (NG, P, TT, D), F32, kind="ExternalOutput").ap()
    layer(nc, a)
    r = run_bass_kernel_spmd(nc, [arrays], core_ids=[0])
    return r.results[0]["out"].reshape(NG, C, BG, TT, D).transpose(0, 2, 3, 1, 4).reshape(B, L, D)
```
